# Optimizing a Trainium2 kernel written in Bass

```python
import numpy as np
import jax
import jax.numpy as jnp

def _softmax(x, axis=-1):
    return jax.nn.softmax(x, axis=axis)

def _gelu(x):
    return jax.nn.gelu(x, approximate=True)

def _silu(x):
    return jax.nn.silu(x)

def _sigmoid(x):
    return jax.nn.sigmoid(x)

def _layernorm(x, axis=-1, eps=1e-05):
    m = jnp.mean(x, axis=axis, keepdims=True)
    v = jnp.var(x, axis=axis, keepdims=True)
    return (x - m) / jnp.sqrt(v + eps)

def _scatter_add(tgt, idx, src, axis=0):
    return tgt.at[idx].add(src)

def _segment_sum(src, seg, n):
    return jax.ops.segment_sum(src, seg, n)
kernel_name = 'mk_adj_ffn_d2_adj_r2_867567'

def setup_inputs(seed: int=0):
    np.random.seed(seed)
    _w = jnp.asarray

    def _rec_inputs():
        import jax
        import jax.numpy as jnp
        _gk = jax.random.key(seed)
        x = -0.0002928 + 1 * jax.random.normal(jax.random.fold_in(_gk, 1), (3327, 256), jnp.float32)
        _w = (1.0 + jnp.arange(3327, dtype=jnp.float32)) ** (-0.5)
        _w = _w / _w.mean()
        _pij = jnp.clip(0.00961827 * _w[:, None] * _w[None, :], 0.0, 1.0)
        _a = jax.random.uniform(jax.random.fold_in(_gk, 2), (3327, 3327)) < _pij
        _a = jnp.logical_or(_a, jnp.eye(3327, dtype=bool))
        _af = _a.astype(jnp.float32)
        _af = _af * jax.random.uniform(jax.random.fold_in(_gk, 3), (3327, 3327), jnp.float32, 0.05, 1)
        adj = _af
        return (x, adj)
    x, adj = _rec_inputs()

    def _L0_gnn_setup():
        import jax, jax.numpy as jnp
        import numpy as np
        EPS = 1e-08
        key = jax.random.key(seed)
        k1, k2, k3, k4 = jax.random.split(key, 4)
        N, IN, OUT = (4096, 256, 256)
        x = jax.random.normal(k1, (N, IN), dtype=jnp.float32)
        adj = jax.random.uniform(k2, (N, N), dtype=jnp.float32)
        W = jax.random.normal(k3, (OUT, IN), dtype=jnp.float32) * (1.0 / np.sqrt(IN))
        b = jax.random.normal(k4, (OUT,), dtype=jnp.float32) * 0.01
        return {'x': x, 'adj': adj, 'W': W, 'b': b}
    _L0_gnn_all = _L0_gnn_setup()
    _L0_gnn_in = {k: v for k, v in _L0_gnn_all.items() if k in ('W', 'b')}
    del _L0_gnn_all

    def _L0_ffn_setup():
        import jax, jax.numpy as jnp
        import numpy as np
        TOP_K = 2
        key = jax.random.key(seed)
        ks = jax.random.split(key, 4)
        B, S, D, H, E = (2, 2048, 256, 1024, 8)
        scale_in = 1.0 / np.sqrt(D)
        scale_h = 1.0 / np.sqrt(H)
        return {'x': jax.random.normal(ks[0], (B, S, D), dtype=jnp.float32), 'gate_w': jax.random.normal(ks[1], (D, E), dtype=jnp.float32) * scale_in, 'gate_b': jnp.zeros((E,), dtype=jnp.float32), 'w1': jax.random.normal(ks[2], (E, D, H), dtype=jnp.float32) * scale_in, 'b1': jnp.zeros((E, H), dtype=jnp.float32), 'w2': jax.random.normal(ks[3], (E, H, D), dtype=jnp.float32) * scale_h, 'b2': jnp.zeros((E, D), dtype=jnp.float32)}
    _L0_ffn_all = _L0_ffn_setup()
    _L0_ffn_in = {k: v for k, v in _L0_ffn_all.items() if k in ('gate_w', 'gate_b', 'w1', 'b1', 'w2', 'b2')}
    del _L0_ffn_all

    def _L1_gnn_setup():
        import jax, jax.numpy as jnp
        import numpy as np
        N = 4096
        DIN = 256
        DOUT = 256
        key = jax.random.key(seed)
        k1, k2, k3 = jax.random.split(key, 3)
        x = jax.random.normal(k1, (N, DIN), dtype=jnp.float32)
        adj = jax.random.uniform(k2, (N, N), dtype=jnp.float32)
        W = jax.random.normal(k3, (DIN, DOUT), dtype=jnp.float32) * (1.0 / np.sqrt(DIN))
        b = jnp.zeros((DOUT,), dtype=jnp.float32)
        return {'x': x, 'adj': adj, 'W': W, 'b': b}
    _L1_gnn_all = _L1_gnn_setup()
    _L1_gnn_in = {k: v for k, v in _L1_gnn_all.items() if k in ('W', 'b')}
    del _L1_gnn_all

    def _L1_ffn_setup():
        import jax, jax.numpy as jnp
        import numpy as np
        D_MODEL = 256
        D_FF = 1024
        N_HEADS = 8
        N_EXPERTS = 8
        TOP_K = 2
        CAPACITY_FACTOR = 1.6
        BATCH = 2048
        SEQ = 16
        LN_EPS = 1e-05

        def _layernorm(x, g, b):
            mu = x.mean(-1, keepdims=True)
            var = ((x - mu) ** 2).mean(-1, keepdims=True)
            return (x - mu) * jax.lax.rsqrt(var + LN_EPS) * g + b

        def _moe(xf, router_w, router_b, w1, b1, w2, b2):
            T = xf.shape[0]
            probs = jax.nn.softmax(xf @ router_w + router_b, axis=-1)
            _, topk_idx = jax.lax.top_k(probs, TOP_K)
            capacity = int(np.ceil(T * CAPACITY_FACTOR / N_EXPERTS))
            out = jnp.zeros_like(xf)
            tok = jnp.arange(T)
            for i in range(N_EXPERTS):
                mask = (topk_idx == i).any(-1)
                pos = jnp.where(mask, tok, T)
                sel = jnp.sort(pos)[:capacity]
                xi = xf[jnp.minimum(sel, T - 1)]
                hi = jax.nn.gelu(xi @ w1[i] + b1[i], approximate=False)
                yi = hi @ w2[i] + b2[i]
                out = out.at[sel].set(yi, mode='drop')
            return out
        key = jax.random.key(seed)
        ks = jax.random.split(key, 24)
        s = 0.02
        d, f, e = (D_MODEL, D_FF, N_EXPERTS)
        inp = {'x': jax.random.normal(ks[0], (BATCH, SEQ, d), dtype=jnp.float32), 'ln1_g': jnp.ones((d,), jnp.float32), 'ln1_b': jnp.zeros((d,), jnp.float32), 'ln2_g': jnp.ones((d,), jnp.float32), 'ln2_b': jnp.zeros((d,), jnp.float32), 'wq': jax.random.normal(ks[1], (d, d)) * s, 'bq': jnp.zeros((d,)), 'wk': jax.random.normal(ks[2], (d, d)) * s, 'bk': jnp.zeros((d,)), 'wv': jax.random.normal(ks[3], (d, d)) * s, 'bv': jnp.zeros((d,)), 'wo': jax.random.normal(ks[4], (d, d)) * s, 'bo': jnp.zeros((d,)), 'router_w': jax.random.normal(ks[5], (d, e)) * s, 'router_b': jnp.zeros((e,)), 'w1': jax.random.normal(ks[6], (e, d, f)) * s, 'b1': jnp.zeros((e, f)), 'w2': jax.random.normal(ks[7], (e, f, d)) * s, 'b2': jnp.zeros((e, d))}
        return inp
    _L1_ffn_all = _L1_ffn_setup()
    _L1_ffn_in = {k: v for k, v in _L1_ffn_all.items() if k in ('ln1_g', 'ln1_b', 'ln2_g', 'ln2_b', 'wq', 'bq', 'wk', 'bk', 'wv', 'bv', 'wo', 'bo', 'router_w', 'router_b', 'w1', 'b1', 'w2', 'b2')}
    del _L1_ffn_all
    return {'x': x, 'adj': adj, 'L0_gnn_W': _L0_gnn_in['W'], 'L0_gnn_b': _L0_gnn_in['b'], 'L0_ffn_gate_w': _L0_ffn_in['gate_w'], 'L0_ffn_gate_b': _L0_ffn_in['gate_b'], 'L0_ffn_w1': _L0_ffn_in['w1'], 'L0_ffn_b1': _L0_ffn_in['b1'], 'L0_ffn_w2': _L0_ffn_in['w2'], 'L0_ffn_b2': _L0_ffn_in['b2'], 'L1_gnn_W': _L1_gnn_in['W'], 'L1_gnn_b': _L1_gnn_in['b'], 'L1_ffn_ln1_g': _L1_ffn_in['ln1_g'], 'L1_ffn_ln1_b': _L1_ffn_in['ln1_b'], 'L1_ffn_ln2_g': _L1_ffn_in['ln2_g'], 'L1_ffn_ln2_b': _L1_ffn_in['ln2_b'], 'L1_ffn_wq': _L1_ffn_in['wq'], 'L1_ffn_bq': _L1_ffn_in['bq'], 'L1_ffn_wk': _L1_ffn_in['wk'], 'L1_ffn_bk': _L1_ffn_in['bk'], 'L1_ffn_wv': _L1_ffn_in['wv'], 'L1_ffn_bv': _L1_ffn_in['bv'], 'L1_ffn_wo': _L1_ffn_in['wo'], 'L1_ffn_bo': _L1_ffn_in['bo'], 'L1_ffn_router_w': _L1_ffn_in['router_w'], 'L1_ffn_router_b': _L1_ffn_in['router_b'], 'L1_ffn_w1': _L1_ffn_in['w1'], 'L1_ffn_b1': _L1_ffn_in['b1'], 'L1_ffn_w2': _L1_ffn_in['w2'], 'L1_ffn_b2': _L1_ffn_in['b2']}

def reference(x, adj, L0_gnn_W, L0_gnn_b, L0_ffn_gate_w, L0_ffn_gate_b, L0_ffn_w1, L0_ffn_b1, L0_ffn_w2, L0_ffn_b2, L1_gnn_W, L1_gnn_b, L1_ffn_ln1_g, L1_ffn_ln1_b, L1_ffn_ln2_g, L1_ffn_ln2_b, L1_ffn_wq, L1_ffn_bq, L1_ffn_wk, L1_ffn_bk, L1_ffn_wv, L1_ffn_bv, L1_ffn_wo, L1_ffn_bo, L1_ffn_router_w, L1_ffn_router_b, L1_ffn_w1, L1_ffn_b1, L1_ffn_w2, L1_ffn_b2):
    import jax
    import jax.numpy as jnp

    def _L0_gnn_ref(x, adj, W, b):
        import jax, jax.numpy as jnp
        import numpy as np
        EPS = 1e-08
        deg = adj.sum(axis=1)
        dis = (deg + EPS) ** (-0.5)
        a_norm = dis[:, None] * adj * dis[None, :]
        h = a_norm @ x
        return h @ W.T + b

    def _L0_ffn_ref(x, gate_w, gate_b, w1, b1, w2, b2):
        import jax, jax.numpy as jnp
        import numpy as np
        TOP_K = 2
        B, S, D = x.shape
        E = gate_w.shape[1]
        flat_x = x.reshape(-1, D)
        gate_logits = flat_x @ gate_w + gate_b
        raw_weights = jax.nn.softmax(gate_logits, axis=-1)
        top_w, top_idx = jax.lax.top_k(raw_weights, TOP_K)
        one_hot = jax.nn.one_hot(top_idx, E, dtype=flat_x.dtype)
        gate_output = (one_hot * top_w[..., None]).sum(axis=-2)
        h = jax.nn.gelu(jnp.einsum('td,edh->teh', flat_x, w1) + b1, approximate=False)
        expert_out = jnp.einsum('teh,ehd->ted', h, w2) + b2
        combined = jnp.einsum('ted,te->td', expert_out, gate_output)
        return combined.reshape(B, S, -1)

    def _L1_gnn_ref(x, adj, W, b):
        import jax, jax.numpy as jnp
        import numpy as np
        N = 4096
        DIN = 256
        DOUT = 256
        rowsum = adj.sum(axis=1)
        d_inv_sqrt = jnp.where(rowsum > 0, rowsum ** (-0.5), 0.0)
        normalized_adj = d_inv_sqrt[:, None] * adj * d_inv_sqrt[None, :]
        support = normalized_adj @ x
        out = support @ W + b
        return jax.nn.relu(out)

    def _L1_ffn_ref(x, ln1_g, ln1_b, ln2_g, ln2_b, wq, bq, wk, bk, wv, bv, wo, bo, router_w, router_b, w1, b1, w2, b2):
        import jax, jax.numpy as jnp
        import numpy as np
        D_MODEL = 256
        D_FF = 1024
        N_HEADS = 8
        N_EXPERTS = 8
        TOP_K = 2
        CAPACITY_FACTOR = 1.6
        BATCH = 2048
        SEQ = 16
        LN_EPS = 1e-05

        def _layernorm(x, g, b):
            mu = x.mean(-1, keepdims=True)
            var = ((x - mu) ** 2).mean(-1, keepdims=True)
            return (x - mu) * jax.lax.rsqrt(var + LN_EPS) * g + b

        def _moe(xf, router_w, router_b, w1, b1, w2, b2):
            T = xf.shape[0]
            probs = jax.nn.softmax(xf @ router_w + router_b, axis=-1)
            _, topk_idx = jax.lax.top_k(probs, TOP_K)
            capacity = int(np.ceil(T * CAPACITY_FACTOR / N_EXPERTS))
            out = jnp.zeros_like(xf)
            tok = jnp.arange(T)
            for i in range(N_EXPERTS):
                mask = (topk_idx == i).any(-1)
                pos = jnp.where(mask, tok, T)
                sel = jnp.sort(pos)[:capacity]
                xi = xf[jnp.minimum(sel, T - 1)]
                hi = jax.nn.gelu(xi @ w1[i] + b1[i], approximate=False)
                yi = hi @ w2[i] + b2[i]
                out = out.at[sel].set(yi, mode='drop')
            return out
        B, S, D = x.shape
        dk = D // N_HEADS
        h = _layernorm(x, ln1_g, ln1_b)
        q = (h @ wq + bq).reshape(B, S, N_HEADS, dk)
        k = (h @ wk + bk).reshape(B, S, N_HEADS, dk)
        v = (h @ wv + bv).reshape(B, S, N_HEADS, dk)
        scores = jnp.einsum('bqhd,bkhd->bhqk', q, k) / np.sqrt(dk).astype(np.float32)
        attn = jax.nn.softmax(scores, axis=-1)
        ctx = jnp.einsum('bhqk,bkhd->bqhd', attn, v).reshape(B, S, D)
        x = x + ctx @ wo + bo
        h2 = _layernorm(x, ln2_g, ln2_b)
        moe_out = _moe(h2.reshape(-1, D), router_w, router_b, w1, b1, w2, b2)
        return x + moe_out.reshape(B, S, D)
    x = x + _L0_gnn_ref(_layernorm(x, axis=-1), adj, L0_gnn_W, L0_gnn_b)
    x = x + _L0_ffn_ref(_layernorm(x, axis=-1)[None], L0_ffn_gate_w, L0_ffn_gate_b, L0_ffn_w1, L0_ffn_b1, L0_ffn_w2, L0_ffn_b2)[0]
    x = x + _L1_gnn_ref(_layernorm(x, axis=-1), adj, L1_gnn_W, L1_gnn_b)
    x = x + _L1_ffn_ref(_layernorm(x, axis=-1)[None], L1_ffn_ln1_g, L1_ffn_ln1_b, L1_ffn_ln2_g, L1_ffn_ln2_b, L1_ffn_wq, L1_ffn_bq, L1_ffn_wk, L1_ffn_bk, L1_ffn_wv, L1_ffn_bv, L1_ffn_wo, L1_ffn_bo, L1_ffn_router_w, L1_ffn_router_b, L1_ffn_w1, L1_ffn_b1, L1_ffn_w2, L1_ffn_b2)[0]
    return x

_drawn_inputs = setup_inputs


def setup_inputs(seed=0):
    import zlib

    import numpy as np

    out = dict(_drawn_inputs(seed))
    spreads = {'L0_ffn_gate_b': (0.0, 0.1),
     'L0_ffn_b1': (0.0, 0.1),
     'L0_ffn_b2': (0.0, 0.1),
     'L1_gnn_b': (0.0, 0.1),
     'L1_ffn_ln1_g': (1.0, 0.6),
     'L1_ffn_ln1_b': (0.0, 0.548),
     'L1_ffn_ln2_g': (1.0, 0.2),
     'L1_ffn_ln2_b': (0.0, 0.1),
     'L1_ffn_bq': (0.0, 0.8),
     'L1_ffn_bk': (0.0, 0.8),
     'L1_ffn_bv': (0.0, 0.38),
     'L1_ffn_bo': (0.0, 0.1),
     'L1_ffn_router_b': (0.0, 0.1),
     'L1_ffn_b1': (0.0, 0.477),
     'L1_ffn_b2': (0.0, 0.1)}
    factors = {'L0_gnn_b': 3.01, 'L1_ffn_wq': 8.0, 'L1_ffn_wk': 8.0, 'L1_ffn_wv': 4.401}
    for name, (base, spread) in spreads.items():
        noise = np.random.default_rng([zlib.crc32(name.encode()), seed]).standard_normal(out[name].shape)
        drawn = base * np.exp(spread * noise) if base else spread * noise
        out[name] = jnp.asarray(drawn.astype(out[name].dtype))
    for name, factor in factors.items():
        out[name] = (out[name] * factor).astype(out[name].dtype)
    return out
```

```python
import numpy as np
from contextlib import ExitStack
import concourse.bass as bass
from concourse import mybir

F32 = mybir.dt.float32
F32R = mybir.dt.float32r
BF16 = mybir.dt.bfloat16
I32 = mybir.dt.int32
ALU = mybir.AluOpType
ACT = mybir.ActivationFunctionType
AX = mybir.AxisListType
ds = bass.ds

TOKENS, D, HID, EXPERTS, HEADS = 3327, 256, 1024, 8, 8
P = 128
DK = D // HEADS
NT = -(-TOKENS // P)
NP = NT * P
KT = D // P
HT = HID // P
LAST = TOKENS - (NT - 1) * P
CHUNK = 256
NCH = NP // CHUNK
HALF = NT // 2
TOP_K = 2
CAPACITY = int(np.ceil(TOKENS * 1.6 / EXPERTS))
HG = HEADS // 4
ZERO_COLS = 4096
LN_EPS, GNN_EPS = 1e-5, 1e-8
N_ROWS, N_COLS = 6, 8


def slot_chunks(assigned):
    most = (assigned + EXPERTS * (CHUNK - 1)) // CHUNK
    return most + most % 2


MOE0_CHUNKS = slot_chunks(TOP_K * TOKENS)
MOE1_CHUNKS = slot_chunks(TOKENS)


NAMES = []


def named(name):
    NAMES.append(name)
    return f"{name}_{len(NAMES)}"


class Count:

    def __init__(self, sem):
        self.sem, self.value = sem, 0

    def inc(self, ins):
        ins.then_inc(self.sem, 1)
        self.value += 1

    def settle(self, eng):
        eng.wait_ge(self.sem, self.value)


def constants(nc, m, t, s):
    made, loaded = s("made"), s("params_loaded")
    x_loaded, zero_made, zero_done = s("x_loaded"), s("zero_made"), s("zero_done")
    rows_loaded = [s("rows_loaded0"), s("rows_loaded1")]
    rows_summed = s("rows_summed")
    zero_dmas = []
    with nc.sbuf_tensor(named("adj_rows"), [P, 2, NP], F32) as adj_rows, \
            nc.sbuf_tensor(named("zeros"), [P, ZERO_COLS], F32) as zeros, \
            nc.sbuf_tensor(named("iota_i"), [P, 64], I32) as iota_i, \
            nc.Block() as block:

        @block.gpsimd
        def _(pool):
            c = Count(made)
            c.inc(pool.memset(m.ident[:], 0.0))
            c.inc(pool.memset(m.ident_b[:], 0.0))
            c.inc(pool.memset(m.ones[:], 1.0))
            c.settle(pool)
            c.inc(pool.affine_select(out=m.ident[:], in_=m.ident[:], compare_op=ALU.not_equal, fill=1.0, base=0,
                                     pattern=[[-1, P]], channel_multiplier=1))
            c.inc(pool.affine_select(out=m.ident_b[:], in_=m.ident_b[:], compare_op=ALU.not_equal, fill=1.0,
                                     base=0, pattern=[[-1, P]], channel_multiplier=1))
            c.inc(pool.affine_select(out=m.before[:], in_=m.ones[:], compare_op=ALU.is_gt, fill=0.0, base=0,
                                     pattern=[[1, P]], channel_multiplier=-1))
            c.inc(pool.affine_select(out=m.real[:], in_=m.ones[:, 0:NT], compare_op=ALU.is_gt, fill=0.0,
                                     base=TOKENS, pattern=[[-P, NT]], channel_multiplier=-1))
            c.inc(pool.iota(iota_i[:], [[1, 64]], base=0, channel_multiplier=0))
            c.inc(pool.iota(m.token[:], [[P, NT]], base=0, channel_multiplier=1))
            c.settle(pool)
            c.inc(pool.tensor_copy(m.iota[:], iota_i[:]))
            c.inc(pool.tensor_copy(m.token_f[:], m.token[:]))
            c.settle(pool)
            c.inc(pool.tensor_scalar(m.multiples[:], m.iota[:, 0:NCH], float(CHUNK), None, ALU.mult))
            c.settle(pool)

        @block.scalar
        def _(act):
            for dst, src in ((m.wg0, t["W0"]), (m.wg1, t["W1"]), (m.gate, t["gate"]), (m.router, t["router"]),
                             (m.rows, t["rows"]), (m.cols, t["cols"]), (m.bias8, t["bias8"])):
                act.dma_start(dst[:], src).then_inc(loaded, 16)
            act.wait_ge(zero_made, 1)
            for slots, rows in ((m.slots0, MOE0_CHUNKS * 2), (m.slots1, MOE1_CHUNKS * 2)):
                view = slots[0:rows * P, :].rearrange("(p n) d -> p (n d)", n=rows)
                for n in range(0, rows * D, ZERO_COLS):
                    w = min(ZERO_COLS, rows * D - n)
                    act.dma_start(view[:, n:n + w], zeros[:, 0:w]).then_inc(zero_done, 16)
                    zero_dmas.append(n)
            act.wait_ge(loaded, 16 * 7)
            act.wait_ge(zero_done, 16 * len(zero_dmas))

        @block.sync
        def _(sp):
            sp.dma_start(m.x[:], t["x"]).then_inc(x_loaded, 16)
            with sp.Fori(0, NT // 2) as i:
                for k in range(2):
                    sp.wait_ge(rows_summed, i * 2 + k + 1)
                    sp.dma_start(adj_rows[:, k, :], t["adj"][ds(i * 2 * P + k * P, P), :]).then_inc(rows_loaded[k], 16)
            sp.wait_ge(x_loaded, 16)

        @block.vector
        def _(dve):
            dve.sem_inc(rows_summed, 2)
            dve.memset(zeros[:], 0.0).then_inc(zero_made, 1)
            with dve.Fori(0, NT // 2) as i:
                for k in range(2):
                    dve.wait_ge(rows_loaded[k], i * 16 + 16)
                    dve.tensor_reduce(m.deg[:, ds(i * 2 + k, 1)], adj_rows[:, k, :], AX.X, ALU.add)\
                       .then_inc(rows_summed, 1)
            dve.wait_ge(rows_summed, NT + 2)


def inverse_root(dve, c, rooted, n, r, w, tmp):
    dve.wait_ge(rooted, n)
    for ins in (lambda: dve.reciprocal(r, r),
                lambda: dve.tensor_tensor(tmp, r, r, ALU.mult),
                lambda: dve.tensor_tensor(tmp, tmp, w, ALU.mult),
                lambda: dve.tensor_scalar(tmp, tmp, -0.5, 1.5, ALU.mult, ALU.add),
                lambda: dve.tensor_tensor(r, r, tmp, ALU.mult)):
        c.inc(ins())
        c.settle(dve)


def inverse_roots(nc, m, s):
    guard, rooted = s("guarded"), s("rooted")
    with nc.sbuf_tensor(named("deg_tmp"), [P, 4, NT], F32) as tmp, nc.Block() as block:

        @block.vector
        def _(dve):
            c = Count(guard)
            c.inc(dve.tensor_scalar(tmp[:, 0, :], m.deg[:], GNN_EPS, None, ALU.add))
            c.inc(dve.tensor_scalar(tmp[:, 1, :], m.deg[:], 1e-34, None, ALU.max))
            c.inc(dve.tensor_scalar(tmp[:, 2, :], m.deg[:], 0.0, None, ALU.is_gt))
            inverse_root(dve, c, rooted, 1, m.dis0[:], tmp[:, 0, :], tmp[:, 3, :])
            inverse_root(dve, c, rooted, 2, m.dis1[:], tmp[:, 1, :], tmp[:, 3, :])
            c.inc(dve.tensor_tensor(m.dis1[:], m.dis1[:], tmp[:, 2, :], ALU.mult))
            c.settle(dve)

        @block.scalar
        def _(act):
            act.wait_ge(guard, 2)
            act.activation(m.dis0[:], tmp[:, 0, :], ACT.Sqrt).then_inc(rooted, 1)
            act.activation(m.dis1[:], tmp[:, 1, :], ACT.Sqrt).then_inc(rooted, 1)


def normalise(nc, m, s, src, dst):
    stats, rooted, applied = s("stats"), s("var_rooted"), s("applied")
    with nc.sbuf_tensor(named("bn_st"), [P, NT, 6], F32) as st, nc.sbuf_tensor(named("bn_mv"), [P, NT, 2], F32) as mv, \
            nc.sbuf_tensor(named("bn_rs"), [P, NT], F32) as rs, nc.sbuf_tensor(named("bn_nb"), [P, NT], F32) as nb, \
            nc.sbuf_tensor(named("bn_vr"), [P, NT], F32) as vr, \
            nc.Block() as block:

        @block.vector
        def _(dve):
            c = Count(stats)
            for k in range(NT):
                c.inc(dve.bn_stats(st[:, k, :], src[:, k, :]))
            c.settle(dve)
            for k in range(NT):
                c.inc(dve.bn_aggr(mv[:, k, :], st[:, k, :]))
            c.settle(dve)
            c.inc(dve.tensor_scalar(vr[:], mv[:, :, 1], LN_EPS, None, ALU.add))
            inverse_root(dve, c, rooted, 1, rs[:], vr[:], nb[:])
            dve.scalar_tensor_tensor(nb[:], mv[:, :, 0], -1.0, rs[:], ALU.mult, ALU.mult).then_inc(applied, 1)
            with dve.Fori(0, NT // 2) as i:
                dve.tensor_scalar(dst[:, ds(i, 1), :], src[:, ds(i, 1), :],
                                  mv[:, ds(i, 1), 0:1].rearrange("p a b -> p (a b)"),
                                  rs[:, ds(i, 1)], ALU.subtract, ALU.mult)
            dve.drain()

        @block.scalar
        def _(act):
            act.wait_ge(stats, 2 * NT + 1)
            act.activation(rs[:], vr[:], ACT.Sqrt).then_inc(rooted, 1)
            act.wait_ge(applied, 1)
            with act.Fori(NT // 2, NT) as i:
                act.activation(dst[:, ds(i, 1), :], src[:, ds(i, 1), :], ACT.Identity,
                               bias=nb[:, ds(i, 1)], scale=rs[:, ds(i, 1)])
            act.drain()


def transposed_products(nc, m, s, src, products, take_act, take_dve, n_psum, affine=None, tail_sp=None):
    turned, copied, multiplied = s("turned"), s("copied"), s("multiplied")
    act_took, dve_took = s("act_took"), s("dve_took")
    with nc.sbuf_tensor(named("xt"), [P, 2, KT, P], F32) as xt, nc.psum_tensor(named("ps_turn"), [P, 2, 512], F32) as ps_turn, \
            nc.psum_tensor(named("ps_prod"), [P, 2, n_psum, 512], F32) as ps, nc.Block() as block:

        @block.tensor
        def _(pe):
            def turn(k):
                if k >= 2:
                    pe.wait_ge(copied, k - 1)
                for j in range(KT):
                    last = pe.transpose(ps_turn[:, k % 2, j * P:(j + 1) * P], src[:, k, j * P:(j + 1) * P], m.ident[:])
                last.then_inc(turned, 1)

            def multiply(k):
                pe.wait_ge(copied, k + 1)
                if k >= 2:
                    pe.wait_ge(act_took, k - 1)
                    pe.wait_ge(dve_took, k - 1)
                products(pe, xt[:, k % 2], ps[:, k % 2]).then_inc(multiplied, 1)

            turn(0)
            for k in range(NT):
                if k + 1 < NT:
                    turn(k + 1)
                multiply(k)

        @block.scalar
        def _(act):
            def copy(k):
                act.wait_ge(turned, k + 1)
                if k >= 2:
                    act.wait_ge(multiplied, k - 1)
                for j in range(KT):
                    if affine:
                        last = act.activation(xt[:, k % 2, j, :], ps_turn[:, k % 2, j * P:(j + 1) * P], ACT.Identity,
                                              bias=affine[1][:, j:j + 1], scale=affine[0][:, j:j + 1])
                if not affine:
                    last = act.activation(xt[:, k % 2].rearrange("p j n -> p (j n)"), ps_turn[:, k % 2, 0:D], ACT.Copy)
                last.then_inc(copied, 1)

            copy(0)
            for k in range(NT):
                if k + 1 < NT:
                    copy(k + 1)
                act.wait_ge(multiplied, k + 1)
                take_act(act, k, ps[:, k % 2], act_took)
            act.wait_ge(act_took, NT)

        @block.vector
        def _(dve):
            for k in range(NT):
                dve.wait_ge(multiplied, k + 1)
                take_dve(dve, k, ps[:, k % 2], act_took, dve_took)
            dve.wait_ge(dve_took, NT)

        if tail_sp:
            @block.sync
            def _(sp):
                tail_sp(sp, act_took, dve_took)


def graph_layer(nc, m, t, s, w, dis, bias, relu):
    with nc.sbuf_tensor(named("y_hi"), [P, NT, D], F32R) as y_hi, nc.sbuf_tensor(named("y_lo"), [P, NT, D], F32R) as y_lo:

        def products(pe, xt, ps):
            for j in range(KT):
                last = pe.matmul(ps[:, 0, 0:D], xt[:, j, :], w[:, j, :], start=j == 0, stop=j == KT - 1)
            return last

        def take_act(act, k, ps, took):
            act.activation(y_hi[:, k, :], ps[:, 0, 0:D], ACT.Copy, scale=dis[:, k:k + 1]).then_inc(took, 1)

        def take_dve(dve, k, ps, act_took, took):
            dve.wait_ge(act_took, k + 1)
            dve.scalar_tensor_tensor(y_lo[:, k, :], ps[:, 0, 0:D], dis[:, k:k + 1], y_hi[:, k, :].bitcast(F32),
                                     ALU.mult, ALU.subtract).then_inc(took, 1)

        transposed_products(nc, m, s, m.xhat, products, take_act, take_dve, 1)

        loaded = [s("adj_loaded0"), s("adj_loaded1")]
        hi_made, lo_made, used = s("hi_made"), s("lo_made"), s("halves_used")
        summed, taken, chain = s("chunk_summed"), s("chunk_taken"), s("taking")
        with nc.sbuf_tensor(named("adj_raw"), [P, 2, HALF * CHUNK], F32) as raw, \
                nc.sbuf_tensor(named("adj_hi"), [P, 2, HALF, CHUNK], F32R) as hi, \
                nc.sbuf_tensor(named("adj_lo"), [P, 2, HALF, CHUNK], F32R) as lo, \
                nc.sbuf_tensor(named("gnn_tmp"), [P, 2, D], F32) as tmp, \
                nc.psum_tensor(named("ps_gnn"), [P, 2, 512], F32) as ps, nc.Block() as block:

            @block.sync
            def _(sp):
                with sp.Fori(0, NCH) as c:
                    for k in range(2):
                        sp.wait_ge(lo_made, c * 2 + k + 1)
                        sp.dma_start(raw[:, k, :], t["adjT"][ds(c, 1), k].rearrange("a p n -> p (a n)")).then_inc(loaded[k], 16)

            @block.scalar
            def _(act):
                def split_hi(c, k):
                    act.wait_ge(loaded[k], c * 16 + 16)
                    if k == 0:
                        act.wait_ge(used, c + 1)
                    else:
                        act.wait_ge(summed, c * 2 + 2)
                    act.activation(hi[:, k].rearrange("p j n -> p (j n)"), raw[:, k, :], ACT.Copy).then_inc(hi_made, 1)

                with act.Fori(0, NCH) as c:
                    for k in range(2):
                        split_hi(c, k)
                act.wait_ge(hi_made, 2 * NCH)

            @block.tensor
            def _(pe):
                pe.sem_inc(used, 1)
                pe.sem_inc(summed, 2)
                with pe.Fori(0, NCH) as c:
                    for k in range(2):
                        pe.wait_ge(hi_made, c * 2 + k + 1)
                        pe.wait_ge(lo_made, c * 2 + k + 3)
                        for i in range(2):
                            if k == 0:
                                pe.wait_ge(taken, c * 2 + i + 1)
                            for j in range(HALF):
                                rows = slice(i * P, (i + 1) * P)
                                n = k * HALF + j
                                out = ps[:, i, 0:D]
                                pe.matmul(out, hi[:, k, j, rows], y_hi[:, n, :], start=n == 0, stop=False)
                                pe.matmul(out, hi[:, k, j, rows], y_lo[:, n, :], start=False, stop=False)
                                last = pe.matmul(out, lo[:, k, j, rows], y_hi[:, n, :], start=False, stop=n == NT - 1)
                            if k == 1:
                                last.then_inc(summed, 1)
                        if k == 0:
                            last.then_inc(used, 1)

            @block.vector
            def _(dve):
                dve.sem_inc(lo_made, 2)
                dve.sem_inc(taken, 2)

                def split_lo(c, k):
                    dve.wait_ge(hi_made, c * 2 + k + 1)
                    dve.tensor_tensor(lo[:, k].rearrange("p j n -> p (j n)"), raw[:, k, :],
                                      hi[:, k].rearrange("p j n -> p (j n)").bitcast(F32), ALU.subtract).then_inc(lo_made, 1)

                def take(c):
                    for i in range(2):
                        xs = m.x[:, ds(c * 2 + i, 1), :].rearrange("p a d -> p (a d)")
                        dve.wait_ge(summed, c * 2 + i + 3)
                        dve.scalar_tensor_tensor(tmp[:, i, :], ps[:, i, 0:D], dis[:, ds(c * 2 + i, 1)], bias,
                                                 ALU.mult, ALU.add).then_inc(taken, 1)
                        dve.wait_ge(taken, c * 2 + i + 3)
                        if relu:
                            dve.scalar_tensor_tensor(xs, tmp[:, i, :], 0.0, xs, ALU.max, ALU.add).then_inc(chain, 1)
                        else:
                            dve.tensor_tensor(xs, tmp[:, i, :], xs, ALU.add).then_inc(chain, 1)
                        dve.wait_ge(chain, c * 2 + i + 1)

                split_lo(0, 0)
                split_lo(0, 1)
                with dve.Fori(0, NCH - 1) as c:
                    split_lo(c + 1, 0)
                    take(c)
                    split_lo(c + 1, 1)
                take(NCH - 1)


def mixture_routes(nc, m, s, bias, top, capacity, chunks, slot_sets, weights):
    c_act, c_dve, c_pe = s("route_exp"), s("route_dve"), s("route_sums")
    with ExitStack() as ctx:
        def sb(name, shape, dt=F32):
            return ctx.enter_context(nc.sbuf_tensor(named("rt_" + name), shape, dt))

        hots = [sb(f"choice{k}", [P, NT, EXPERTS]) for k in range(top)]
        prob, key, mask = sb("prob", [P, NT, EXPERTS]), sb("key", [P, NT, EXPERTS]), sb("mask", [P, NT, EXPERTS])
        rank, best, total = sb("rank", [P, NT, EXPERTS]), sb("best", [P, NT]), sb("total", [P, NT])
        carry = sb("carry", [P, NT + 1, EXPERTS])
        steps, full = sb("steps", [P, EXPERTS, NCH]), sb("full", [P, EXPERTS])
        ends, base = sb("ends", [P, EXPERTS + 1]), sb("base", [P, EXPERTS])
        fine = sb("fine", [P, NT])
        mask_at = []
        owner, owner_f = sb("owner", [P, chunks, EXPERTS]), sb("owner_f", [P, chunks])
        ps = ctx.enter_context(nc.psum_tensor(named("ps_rank"), [P, 2, 512], F32))
        block = ctx.enter_context(nc.Block())
        W = NT * EXPERTS
        rounds = 1 if capacity is None else 2

        def over_experts(a):
            return a.rearrange("p (t a) -> p t a", a=1).broadcast_to([P, NT, EXPERTS])

        def by_expert(a):
            return a.rearrange("p (a e) -> p a e", a=1).broadcast_to([P, NT, EXPERTS])

        @block.vector
        def _(dve):
            c = Count(c_dve)

            def do(ins):
                c.inc(ins)
                c.settle(dve)

            up = m.iota[:, 1:EXPERTS + 1]

            do(dve.tensor_tensor(mask[:], m.logits[:], by_expert(bias), ALU.add))
            do(dve.tensor_reduce(best[:], mask[:], AX.X, ALU.max))
            do(dve.tensor_tensor(key[:], mask[:], over_experts(best[:]), ALU.subtract))
            dve.wait_ge(c_act, 1)
            do(dve.tensor_reduce(total[:], prob[:], AX.X, ALU.add))
            do(dve.reciprocal(total[:], total[:]))
            do(dve.tensor_tensor(prob[:], prob[:], over_experts(total[:]), ALU.mult))

            def first_of(values, hot):
                do(dve.tensor_reduce(best[:], values[:], AX.X, ALU.max))
                do(dve.tensor_tensor(key[:], values[:], over_experts(best[:]), ALU.is_equal))
                do(dve.tensor_tensor(key[:], key[:], by_expert(m.falling[:]), ALU.mult))
                do(dve.tensor_reduce(total[:], key[:], AX.X, ALU.max))
                do(dve.tensor_tensor(hot[:], key[:], over_experts(total[:]), ALU.is_equal))

            do(dve.tensor_scalar(m.falling[:], m.iota[:, 0:EXPERTS], -1.0, float(EXPERTS), ALU.mult, ALU.add))
            for k in range(top):
                first_of(prob, hots[k])
                if capacity is None:
                    do(dve.tensor_copy(weights[k][:], best[:]))
                if k + 1 < top:
                    do(dve.scalar_tensor_tensor(prob[:], hots[k][:], -4.0, prob[:], ALU.mult, ALU.add))

            def ranks():
                mask_at.append(c.value)
                dve.wait_ge(c_pe, len(mask_at))
                do(dve.memset(carry[:, 0, :], 0.0))
                for k in range(NT):
                    do(dve.tensor_tensor(carry[:, k + 1, :], carry[:, k, :],
                                         ps[:, 1, k * EXPERTS:(k + 1) * EXPERTS], ALU.add))
                do(dve.tensor_tensor(rank[:], carry[:, 0:NT, :],
                                     ps[:, 0, 0:W].rearrange("p (t e) -> p t e", e=EXPERTS), ALU.add))

            do(dve.tensor_tensor(mask[:], hots[0][:], hots[1][:], ALU.add))
            do(dve.tensor_tensor(mask[:], mask[:], over_experts(m.real[:]), ALU.mult))
            ranks()
            if capacity is not None:
                do(dve.scalar_tensor_tensor(key[:], rank[:], float(capacity), mask[:], ALU.is_lt, ALU.mult))
                do(dve.tensor_tensor(key[:], key[:], by_expert(up), ALU.mult))
                do(dve.tensor_reduce(best[:], key[:], AX.X, ALU.max))
                do(dve.tensor_scalar(weights[0][:], best[:], 0.0, None, ALU.is_gt))
                do(dve.tensor_tensor(mask[:], key[:], over_experts(best[:]), ALU.is_equal))
                do(dve.tensor_tensor(mask[:], mask[:], over_experts(weights[0][:]), ALU.mult))
                ranks()
                rows_of, ok = [mask], weights[0]
            else:
                rows_of, ok = hots, m.real
            do(dve.tensor_tensor(steps[:], carry[:, NT, :].rearrange("p (e a) -> p e a", a=1).broadcast_to([P, EXPERTS, NCH]),
                                 m.multiples[:].rearrange("p (a n) -> p a n", a=1).broadcast_to([P, EXPERTS, NCH]), ALU.is_gt))
            do(dve.tensor_reduce(full[:], steps[:], AX.X, ALU.add))
            do(dve.memset(ends[:, 0:1], 0.0))
            for e in range(EXPERTS):
                do(dve.tensor_tensor(ends[:, e + 1:e + 2], ends[:, e:e + 1], full[:, e:e + 1], ALU.add))
            do(dve.tensor_tensor(owner[:], ends[:, 1:].rearrange("p (a e) -> p a e", a=1).broadcast_to([P, chunks, EXPERTS]),
                                 m.iota[:, 0:chunks].rearrange("p (n a) -> p n a", a=1).broadcast_to([P, chunks, EXPERTS]), ALU.is_le))
            do(dve.tensor_reduce(owner_f[:], owner[:], AX.X, ALU.add))
            do(dve.tensor_scalar(m.owner[:, 0:chunks], owner_f[:], float(EXPERTS - 1), None, ALU.min))
            do(dve.tensor_scalar(base[:], ends[:, 0:EXPERTS], float(CHUNK), None, ALU.mult))
            do(dve.tensor_tensor(rank[:], rank[:], by_expert(base[:]), ALU.add))
            do(dve.tensor_scalar(fine[:], ok[:], -1.0, 1.0, ALU.mult, ALU.add))
            for n, (hot, (put, get)) in enumerate(zip(rows_of, slot_sets)):
                do(dve.tensor_tensor(key[:], hot[:], rank[:], ALU.mult))
                do(dve.tensor_reduce(best[:], key[:], AX.X, ALU.add))
                do(dve.scalar_tensor_tensor(total[:], m.token_f[:], float(chunks * CHUNK + n * NP), best[:],
                                            ALU.add, ALU.subtract))
                do(dve.tensor_tensor(total[:], total[:], fine[:], ALU.mult))
                do(dve.tensor_tensor(put[:], total[:], best[:], ALU.add))
                do(dve.tensor_scalar(get[:], best[:], float(chunks * CHUNK - 1), None, ALU.min))

        @block.scalar
        def _(act):
            act.wait_ge(c_dve, 3)
            act.activation(prob[:], key[:], ACT.Exp).then_inc(c_act, 1)

        @block.tensor
        def _(pe):
            for r in range(rounds):
                pe.wait_ge(c_dve, mask_at[r])
                flat = mask[:].rearrange("p t e -> p (t e)")
                pe.matmul(ps[:, 0, 0:W], m.before[:], flat, start=True, stop=True)
                pe.matmul(ps[:, 1, 0:W], m.ones[:], flat, start=True, stop=True).then_inc(c_pe, 1)



def mixture_scatter(nc, m, s, rows, slots, puts):
    sent = s("rows_sent")
    with nc.Block() as block:

        @block.gpsimd
        def _(pool):
            for put in puts:
                for k in range(NT):
                    pool.indirect_dma_start(out=slots, out_offset=bass.IndirectOffsetOnAxis(put[:, k:k + 1], 0),
                                            in_=rows[:, k, :], in_offset=None).then_inc(sent, 16)
            pool.wait_ge(sent, 16 * NT * len(puts))


def expert_layers(nc, m, t, s, layer, chunks, slots, results):
    loaded = [s("expert_loaded0"), s("expert_loaded1")]
    turned, copied, hidden_ps, hidden = s("ex_turned"), s("ex_copied"), s("ex_hidden_ps"), s("ex_hidden")
    out_ps, out_made = s("ex_out_ps"), s("ex_out_made")
    stored, res_free = [s("ex_stored0"), s("ex_stored1")], s("ex_res_free")
    w1_d, w2_d, b1_d, b2_d = (t[f"{n}_{layer}"] for n in ("w1", "w2", "b1", "b2"))
    TT = CHUNK // P
    with ExitStack() as ctx:
        def sb(name, shape, dt=F32):
            return ctx.enter_context(nc.sbuf_tensor(named("ex_" + name), shape, dt))

        w1, w2 = sb("w1", [P, 2, KT * HID]), sb("w2", [P, 2, HT * D])
        b1, b2 = sb("b1", [P, 2, HT]), sb("b2", [P, 2, D])
        rows, rows_t = sb("rows", [P, 2, TT, D]), sb("rows_t", [P, KT, CHUNK])
        hid, res = sb("hid", [P, HT, CHUNK]), sb("res", [P, 2, TT, D])
        ps_t = ctx.enter_context(nc.psum_tensor(named("ps_ex_t"), [P, KT, 512], F32))
        ps_h = ctx.enter_context(nc.psum_tensor(named("ps_ex_h"), [P, 4, 512], F32))
        ps_o = ctx.enter_context(nc.psum_tensor(named("ps_ex_o"), [P, TT, 512], F32))
        block = ctx.enter_context(nc.Block())

        @block.sync
        def _(sp):
            with sp.Fori(0, chunks // 2) as i:
                for k in range(2):
                    n = i * 2 + k
                    sp.wait_ge(out_made, n + 1)
                    e = sp.value_load(m.owner[0:1, ds(n, 1)], min_val=0, max_val=EXPERTS - 1)
                    sp.dma_start(rows[:, k], slots[ds(i * 2 * CHUNK + k * CHUNK, CHUNK), :].rearrange("(a p) d -> p a d", p=P)).then_inc(loaded[k], 16)
                    sp.dma_start(w1[:, k, :], w1_d[ds(e, 1)].rearrange("a p n -> (a p) n")).then_inc(loaded[k], 16)
                    sp.dma_start(b1[:, k, :], b1_d[ds(e, 1)].rearrange("a p n -> (a p) n")).then_inc(loaded[k], 16)
                    sp.dma_start(b2[:, k, :], b2_d[ds(e, 1)].rearrange("a p n -> (a p) n")).then_inc(loaded[k], 16)
                    sp.dma_start(w2[:, k, :], w2_d[ds(e, 1)].rearrange("a p n -> (a p) n")).then_inc(loaded[k], 16)

        @block.tensor
        def _(pe):
            with pe.Fori(0, chunks // 2) as i:
                for k in range(2):
                    n = i * 2 + k
                    pe.wait_ge(loaded[k], i * 80 + 80)
                    pe.wait_ge(copied, n + 1)
                    for a in range(TT):
                        for j in range(KT):
                            last = pe.transpose(ps_t[:, j, a * P:(a + 1) * P], rows[:, k, a, j * P:(j + 1) * P], m.ident[:])
                    last.then_inc(turned, 1)
                    pe.wait_ge(copied, n + 2)
                    for h in range(HT):
                        pe.wait_ge(hidden, n * HT + h + 1)
                        for j in range(KT):
                            last = pe.matmul(ps_h[:, h % 4, 0:CHUNK], w1[:, k, j * HID + h * P:j * HID + (h + 1) * P],
                                             rows_t[:, j, :], start=j == 0, stop=j == KT - 1)
                        last.then_inc(hidden_ps, 1)
                    pe.wait_ge(out_made, n + 2)
                    pe.wait_ge(hidden, n * HT + HT + 4)
                    for a in range(TT):
                        for h in range(HT):
                            last = pe.matmul(ps_o[:, a, 0:D], hid[:, h, a * P:(a + 1) * P],
                                             w2[:, k, h * D:(h + 1) * D], start=h == 0, stop=h == HT - 1)
                    last.then_inc(out_ps, 1)

        @block.scalar
        def _(act):
            act.sem_inc(copied, 1)
            act.sem_inc(hidden, 4)
            with act.Fori(0, chunks // 2) as i:
                for k in range(2):
                    n = i * 2 + k
                    act.wait_ge(turned, n + 1)
                    act.activation(rows_t[:], ps_t[:, :, 0:CHUNK], ACT.Copy).then_inc(copied, 1)
                    act.wait_ge(out_ps, n + 1)
                    for h in range(HT):
                        act.wait_ge(hidden_ps, n * HT + h + 1)
                        act.activation(hid[:, h, :], ps_h[:, h % 4, 0:CHUNK], ACT.Gelu, bias=b1[:, k, h:h + 1]).then_inc(hidden, 1)

        @block.vector
        def _(dve):
            dve.sem_inc(out_ps, 1)
            dve.sem_inc(out_made, 2)
            with dve.Fori(0, chunks // 2) as i:
                for k in range(2):
                    n = i * 2 + k
                    dve.wait_ge(out_ps, n + 2)
                    dve.wait_ge(res_free, n + 1)
                    dve.tensor_tensor(res[:, k], ps_o[:, :, 0:D], b2[:, k, :].rearrange("p (a d) -> p a d", a=1).broadcast_to([P, TT, D]),
                                      ALU.add).then_inc(out_made, 1)
            dve.wait_ge(out_made, chunks + 2)

        @block.gpsimd
        def _(pool):
            pool.sem_inc(res_free, 2)
            with pool.Fori(0, chunks // 2) as i:
                for k in range(2):
                    n = i * 2 + k
                    pool.wait_ge(out_made, n + 3)
                    pool.dma_start(results[ds(i * 2 * CHUNK + k * CHUNK, CHUNK), :].rearrange("(a p) d -> p a d", p=P),
                                   res[:, k]).then_inc(stored[k], 16)
                    pool.wait_ge(stored[k], i * 16 + 16)
                    pool.sem_inc(res_free, 1)


def mixture_gather(nc, m, s, results, gets, weights, x):
    RING = 4
    come = [s(f"row_come{k}") for k in range(RING)]
    added = s("row_added")
    with nc.sbuf_tensor(named("got"), [P, RING, D], F32) as got, nc.Block() as block:
        jobs = [(k, c) for k in range(NT) for c in range(len(gets))]

        @block.gpsimd
        def _(pool):
            for n, (k, c) in enumerate(jobs):
                if n >= RING:
                    pool.wait_ge(added, n - RING + 1)
                pool.indirect_dma_start(out=got[:, n % RING, :], out_offset=None, in_=results,
                                        in_offset=bass.IndirectOffsetOnAxis(gets[c][:, k:k + 1], 0)).then_inc(come[n % RING], 16)

        @block.vector
        def _(dve):
            for n, (k, c) in enumerate(jobs):
                dve.wait_ge(come[n % RING], 16 * (n // RING) + 16)
                if n:
                    dve.wait_ge(added, n)
                dve.scalar_tensor_tensor(x[:, k, :], got[:, n % RING, :], weights[c][:, k:k + 1], x[:, k, :],
                                         ALU.mult, ALU.add).then_inc(added, 1)
            dve.wait_ge(added, len(jobs))


def gate_logits(nc, m, s, src, w):
    def products(pe, xt, ps):
        for j in range(KT):
            last = pe.matmul(ps[:, 0, 0:EXPERTS], xt[:, j, :], w[:, j, :], start=j == 0, stop=j == KT - 1)
        return last

    def take_act(act, k, ps, took):
        act.activation(m.logits[:, k, :], ps[:, 0, 0:EXPERTS], ACT.Copy).then_inc(took, 1)

    def take_dve(dve, k, ps, act_took, took):
        dve.sem_inc(took, 1)

    transposed_products(nc, m, s, src, products, take_act, take_dve, 1)


def mixture(nc, m, t, s, layer, src, gate, bias, capacity, chunks, slots, results, x):
    n_rows = TOP_K if capacity is None else 1
    with ExitStack() as ctx:
        def sb(name, shape, dt=F32):
            return ctx.enter_context(nc.sbuf_tensor(f"mx{layer}_" + name, shape, dt))

        slot_sets = [(sb(f"put{c}", [P, NT], I32), sb(f"get{c}", [P, NT], I32)) for c in range(n_rows)]
        weights = [sb(f"weight{c}", [P, NT]) for c in range(n_rows)]
        gate_logits(nc, m, s, src, gate)
        mixture_routes(nc, m, s, bias, TOP_K, capacity, chunks, slot_sets, weights)
        mixture_scatter(nc, m, s, src, slots, [put for put, _ in slot_sets])
        expert_layers(nc, m, t, s, layer, chunks, slots, results)
        mixture_gather(nc, m, s, results, [get for _, get in slot_sets], weights, x)


def add_rows(nc, m, s, row):
    done = s("row_added_all")
    with nc.Block() as block:

        @block.vector
        def _(dve):
            dve.tensor_tensor(m.x[:], m.x[:], m.rows[:, row:row + 1, :].broadcast_to([P, NT, D]), ALU.add).then_inc(done, 1)
            dve.wait_ge(done, 1)


def keep_x(nc, m, s):
    stored = s("x_stored")
    with nc.Block() as block:

        @block.sync
        def _(sp):
            sp.dma_start(m.x_kept, m.x[:].rearrange("p t d -> p (t d)")).then_inc(stored, 16)
            sp.wait_ge(stored, 16)


def project(nc, m, t, s):
    loaded, kept = s("qkv_loaded"), [s("qk_kept0"), s("qk_kept1")]
    G = 2 * HG
    with nc.sbuf_tensor(named("wqk"), [P, 2, KT, D], F32) as wqk, nc.sbuf_tensor(named("wv"), [P, KT, D], F32) as wv, \
            nc.sbuf_tensor(named("qk_hi"), [P, 2, G, P], F32R) as hi, nc.sbuf_tensor(named("qk_lo"), [P, 2, G, P], F32R) as lo:
        with nc.Block() as block:

            @block.sync
            def _(sp):
                sp.dma_start(wqk[:, 0], t["wq"]).then_inc(loaded, 16)
                sp.dma_start(wqk[:, 1], t["wk"]).then_inc(loaded, 16)
                sp.dma_start(wv[:], t["wv"]).then_inc(loaded, 16)
                sp.wait_ge(loaded, 48)

        def products(pe, xt, ps):
            for g in range(G):
                for j in range(KT):
                    pe.matmul(ps[:, 0, g * P:(g + 1) * P], wqk[:, g // HG, j, g % HG * P:(g % HG + 1) * P], xt[:, j, :],
                              start=j == 0, stop=j == KT - 1)
            for j in range(KT):
                last = pe.matmul(ps[:, 1, 0:D], xt[:, j, :], wv[:, j, :], start=j == 0, stop=j == KT - 1)
            return last

        def take_act(act, k, ps, took):
            if k >= 2:
                act.wait_ge(kept[k % 2], k // 2 * 32)
            for g in range(G):
                last = act.activation(hi[:, k % 2, g, :], ps[:, 0, g * P:(g + 1) * P], ACT.Identity,
                                      bias=m.cols[:, 4 + g:5 + g])
            last.then_inc(took, 1)

        def take_dve(dve, k, ps, act_took, took):
            dve.tensor_tensor(m.xhat[:, k, :], ps[:, 1, 0:D], m.rows[:, 4, :], ALU.add)
            dve.wait_ge(act_took, k + 1)
            for g in range(G):
                last = dve.scalar_tensor_tensor(lo[:, k % 2, g, :], ps[:, 0, g * P:(g + 1) * P], m.cols[:, 4 + g:5 + g],
                                                hi[:, k % 2, g, :].bitcast(F32), ALU.add, ALU.subtract)
            last.then_inc(took, 1)

        def store(sp, act_took, dve_took):
            for k in range(NT):
                sp.wait_ge(act_took, k + 1)
                sp.wait_ge(dve_took, k + 1)
                for n, part in enumerate((hi, lo)):
                    sp.dma_start(m.qk[n, :, :, k * P:(k + 1) * P].rearrange("g p n -> p g n"),
                                 part[:, k % 2].bitcast(F32)).then_inc(kept[k % 2], 16)
            for k in range(2):
                sp.wait_ge(kept[k], 16 * NT)

        transposed_products(nc, m, s, m.xhat, products, take_act, take_dve, 2,
                            affine=(m.cols[:, 0:2], m.cols[:, 2:4]), tail_sp=store)


KEYS = 512
STACK = 3 * DK
FOUR = 4


def attend(nc, m, t, s):
    KC = -(-NP // KEYS)
    QT = CHUNK // P
    N_MAX = QT * FOUR * KC
    N_USES = N_MAX + 2 + QT
    PER_HG = (N_MAX + 2) + (NCH - 1) * N_USES + QT
    scale = float(DK) ** -0.5
    k_loaded, q_loaded, wo_loaded = s("k_loaded"), [s("q_loaded0"), s("q_loaded1")], s("wo_loaded")
    ones_row = s("ones_row")
    scored, exped, used = s("scored"), s("exped"), s("probs_used")
    x_made, x_free, max_made, rows_made, context = s("x_made"), s("x_free"), s("max_made"), s("rows_made"), s("context")
    with ExitStack() as ctx:
        def sb(name, shape, dt=F32):
            return ctx.enter_context(nc.sbuf_tensor("at_" + name, shape, dt))

        def pb(name, shape):
            return ctx.enter_context(nc.psum_tensor("ps_" + name, shape, F32))

        kst, qst = sb("kst", [STACK + 1, FOUR, NP], F32R), sb("qst", [STACK + 1, 2, FOUR, CHUNK], F32R)
        probs, wo = sb("probs", [P, 2, FOUR, CHUNK]), sb("wo", [P, HG, D])
        part_max, maxima = sb("part_max", [P, QT * FOUR, KC]), sb("maxima", [P, QT * FOUR], BF16)
        rden, cx = sb("rden", [P, CHUNK]), sb("cx", [P, CHUNK])
        ps_s, ps_o, ps_z = pb("s", [P, 2, FOUR, CHUNK]), pb("o", [P, 512]), pb("z", [P, 512])
        ps_x = pb("x", [P, 2, 512])
        block = ctx.enter_context(nc.Block())

        def blocks(eng, one):
            for hg in range(HG):
                one(hg, -1, 1, True)
                with eng.Fori(0, NCH // 2) as i:
                    one(hg, i * 2, 0, True)
                    one(hg, i * 2 + 1, 1, True)
                one(hg, NCH - 1, 0, False)

        def uses_before(hg, b):
            return b * N_USES + (hg * PER_HG + N_MAX + 2)

        @block.sync
        def _(sp):
            sp.dma_start(wo[:], t["wo"]).then_inc(wo_loaded, 16)

            def load_queries(hg, b, par):
                sp.wait_ge(scored, hg * NCH * NT + 2 * NT if isinstance(b, int) else b * NT + (hg * NCH + 1) * NT)
                for r, part in enumerate((0, 1, 0)):
                    sp.dma_start(qst[r * DK:(r + 1) * DK, par, :, :].bitcast(F32),
                                 m.qk[part, hg, :, ds(b * CHUNK, CHUNK)].rearrange("(h p) n -> p h n", p=DK)).then_inc(q_loaded[par], 16)

            for hg in range(HG):
                load_queries(hg, 0, 0)
                for h in range(FOUR):
                    for r, part in enumerate((0, 0, 1)):
                        sp.dma_start(kst[r * DK:(r + 1) * DK, h, :].bitcast(F32),
                                     m.qk[part, HG + hg, h * DK:(h + 1) * DK, :]).then_inc(k_loaded, 16)
                with sp.Fori(0, NCH // 2) as i:
                    load_queries(hg, i * 2 + 1, 1)
                    load_queries(hg, i * 2 + 2, 0)

        @block.gpsimd
        def _(pool):
            pool.memset(kst[STACK:STACK + 1].bitcast(F32), 1.0).then_inc(ones_row, 1)

        @block.tensor
        def _(pe):
            pe.sem_inc(scored, 2 * NT)
            pe.sem_inc(used, 2)

            def maxima_step(hg, b, par, c, u0):
                qt, h, kc = c // (FOUR * KC), c // KC % FOUR, c % KC
                n = min(KEYS, NP - kc * KEYS)
                pe.wait_ge(x_free, u0 + (c + 1))
                pe.matmul(ps_x[:, c % 2, 0:n], qst[0:STACK, par, h, qt * P:(qt + 1) * P],
                          kst[0:STACK, h, kc * KEYS:kc * KEYS + n], start=True, stop=True).then_inc(x_made, 1)

            def maxima_rows(hg, b, u0):
                pe.wait_ge(max_made, b + (hg * NCH + 2))
                for half in range(2):
                    pe.wait_ge(x_free, u0 + (N_MAX + half + 1))
                    for hh in range(2):
                        for qt in range(QT):
                            col = qt * FOUR + half * 2 + hh
                            last = pe.matmul(ps_x[STACK:STACK + 1, half, hh * CHUNK + qt * P:hh * CHUNK + (qt + 1) * P],
                                             maxima[:, col:col + 1], m.ident_b[:], start=True, stop=True)
                    last.then_inc(x_made, 1)

            def scores(hg, b, par, k):
                g = b + hg * NCH
                pe.wait_ge(exped, g * NT + (k + 1))
                if k == 0:
                    pe.wait_ge(rows_made, g + 1)
                for h in range(FOUR):
                    last = pe.matmul(ps_s[:, k % 2, h, :], kst[:, h, k * P:(k + 1) * P], qst[:, par, h, :],
                                     start=True, stop=True)
                last.then_inc(scored, 1)

            def values(hg, b, k):
                g = b + hg * NCH
                pe.wait_ge(exped, g * NT + (k + 3))
                if k == 0:
                    pe.wait_ge(context, g * 2 + 1)
                rows = LAST if k == NT - 1 else P
                for h in range(FOUR):
                    lanes = slice(h * DK, (h + 1) * DK)
                    pe.matmul(ps_o[lanes, 0:CHUNK], m.xhat[0:rows, k, (hg * FOUR + h) * DK:(hg * FOUR + h + 1) * DK],
                              probs[0:rows, k % 2, h, :], start=k == 0, stop=k == NT - 1)
                for h in range(FOUR):
                    last = pe.matmul(ps_z[h * DK:(h + 1) * DK, 0:CHUNK], m.ones[0:rows, 0:DK],
                                     probs[0:rows, k % 2, h, :], start=k == 0, stop=k == NT - 1)
                last.then_inc(used, 1)

            def one(hg, b, par, has_next):
                first = isinstance(b, int) and b < 0
                u0 = hg * PER_HG if first else uses_before(hg, b)
                if first:
                    pe.wait_ge(k_loaded, (hg + 1) * 16 * 3 * FOUR)
                    if hg == 0:
                        pe.wait_ge(ones_row, 1)
                        pe.wait_ge(wo_loaded, 16)
                if has_next:
                    if first:
                        pe.wait_ge(q_loaded[0], 48 * (hg * (NCH // 2 + 1) + 1))
                    elif par == 0:
                        pe.wait_ge(q_loaded[1], b * 24 + 48 * (hg * (NCH // 2) + 1))
                    else:
                        pe.wait_ge(q_loaded[0], b * 24 + (24 + 48 * (hg * (NCH // 2 + 1) + 1)))
                done = 0
                for k in range(NT):
                    if not first:
                        scores(hg, b, par, k)
                    if has_next:
                        upto = -(-N_MAX * (k + 1) // (NT - 3)) if not first else N_MAX
                        while done < min(upto, N_MAX):
                            maxima_step(hg, b, 1 - par, done, u0)
                            done += 1
                        if k == (NT - 2 if not first else 0):
                            maxima_rows(hg, b, u0)
                    if first:
                        return
                    if k:
                        values(hg, b, k - 1)
                values(hg, b, NT - 1)
                pe.wait_ge(context, (b + hg * NCH) * 2 + 3)
                for a in range(QT):
                    u = (N_MAX + 2 if has_next else 0) + a
                    pe.wait_ge(x_free, u0 + (u + 1))
                    pe.matmul(ps_x[:, a, 0:D], cx[:, a * P:(a + 1) * P], wo[:, hg, :], start=True, stop=True).then_inc(x_made, 1)

            blocks(pe, one)

        @block.scalar
        def _(act):
            act.sem_inc(exped, 2)

            def one(hg, b, par, has_next):
                if isinstance(b, int) and b < 0:
                    return
                g = b + hg * NCH
                for k in range(NT):
                    act.wait_ge(scored, g * NT + (k + 1 + 2 * NT))
                    act.wait_ge(used, g * NT + (k + 1))
                    act.activation(probs[:, k % 2], ps_s[:, k % 2], ACT.Exp, scale=scale).then_inc(exped, 1)

            blocks(act, one)

        @block.vector
        def _(dve):
            dve.sem_inc(x_free, 2)
            dve.sem_inc(context, 1)

            def one(hg, b, par, has_next):
                first = isinstance(b, int) and b < 0
                u0 = hg * PER_HG if first else uses_before(hg, b)
                if has_next:
                    for c in range(N_MAX):
                        kc = c % KC
                        n = min(KEYS, TOKENS - kc * KEYS)
                        dve.wait_ge(x_made, u0 + (c + 1))
                        dve.tensor_reduce(part_max[:, c // KC, kc:kc + 1], ps_x[:, c % 2, 0:n], AX.X, ALU.max)\
                           .then_inc(x_free, 1)
                    dve.wait_ge(x_free, u0 + (N_MAX + 2))
                    dve.tensor_reduce(maxima[:], part_max[:], AX.X, ALU.max).then_inc(max_made, 1)
                    for half in range(2):
                        dve.wait_ge(x_made, u0 + (N_MAX + half + 1))
                        dve.tensor_scalar(qst[STACK:STACK + 1, 1 - par, half * 2:half * 2 + 2, :].rearrange("p h n -> p (h n)"),
                                          ps_x[STACK:STACK + 1, half, :], -1.0, None, ALU.mult).then_inc(x_free, 1)
                    dve.wait_ge(x_free, u0 + (N_MAX + 4))
                    dve.sem_inc(rows_made, 1)
                if first:
                    return
                g = b + hg * NCH
                dve.wait_ge(used, g * NT + (NT + 2))
                dve.reciprocal(rden[:], ps_z[:, 0:CHUNK]).then_inc(context, 1)
                dve.wait_ge(context, g * 2 + 2)
                dve.tensor_tensor(cx[:], ps_o[:, 0:CHUNK], rden[:], ALU.mult).then_inc(context, 1)
                for a in range(QT):
                    u = (N_MAX + 2 if has_next else 0) + a
                    xs = m.x[:, ds(b * QT + a, 1), :].rearrange("p a d -> p (a d)")
                    dve.wait_ge(x_made, u0 + (u + 1))
                    dve.tensor_tensor(xs, ps_x[:, a, 0:D], xs, ALU.add).then_inc(x_free, 1)

            blocks(dve, one)
            dve.wait_ge(x_free, HG * PER_HG + 2)


def attention(nc, m, t, s):
    keep_x(nc, m, s)
    normalise(nc, m, s, m.x, m.x)
    normalise(nc, m, s, m.x, m.xhat)
    project(nc, m, t, s)
    add_rows(nc, m, s, 5)
    attend(nc, m, t, s)


def second_mixture(nc, m, t, s):
    normalise(nc, m, s, m.x, m.xhat)
    scaled, loaded = s("ln2_scaled"), s("x_back")
    with nc.sbuf_tensor(named("x_back"), [P, NT, D], F32) as back, nc.Block() as block:

        @block.sync
        def _(sp):
            sp.dma_start(back[:].rearrange("p t d -> p (t d)"), m.x_kept).then_inc(loaded, 16)

        @block.vector
        def _(dve):
            dve.tensor_tensor(m.xhat[:], m.xhat[:], m.rows[:, 2:3, :].broadcast_to([P, NT, D]), ALU.mult).then_inc(scaled, 1)
            dve.wait_ge(scaled, 1)
            dve.tensor_tensor(m.xhat[:], m.xhat[:], m.rows[:, 3:4, :].broadcast_to([P, NT, D]), ALU.add).then_inc(scaled, 1)
            dve.wait_ge(loaded, 16)
            dve.tensor_tensor(m.x[:], m.x[:], back[:], ALU.add).then_inc(scaled, 1)
            dve.wait_ge(scaled, 3)

    mixture(nc, m, t, s, 1, m.xhat, m.router, m.bias8[:, 1, :], CAPACITY, MOE1_CHUNKS, m.slots1, m.results1, m.x)


class Memory:

    def __init__(self, nc, ctx):
        def sb(name, shape, dt=F32):
            return ctx.enter_context(nc.sbuf_tensor("k_" + name, shape, dt))

        def dram(name, shape):
            return nc.dram_tensor(name, shape, F32).ap()

        self.x, self.xhat = sb("x", [P, NT, D]), sb("xhat", [P, NT, D])
        self.ident, self.ident_b = sb("ident", [P, P]), sb("ident_b", [P, P], BF16)
        self.ones, self.before = sb("ones", [P, P]), sb("before", [P, P])
        self.real, self.token, self.token_f = sb("real", [P, NT]), sb("token", [P, NT], I32), sb("token_f", [P, NT])
        self.iota, self.falling = sb("iota", [P, 64]), sb("falling", [P, EXPERTS])
        self.multiples = sb("multiples", [P, NCH])
        self.deg, self.dis0, self.dis1 = sb("deg", [P, NT]), sb("dis0", [P, NT]), sb("dis1", [P, NT])
        self.wg0, self.wg1 = sb("wg0", [P, KT, D]), sb("wg1", [P, KT, D])
        self.gate, self.router = sb("gate", [P, KT, EXPERTS]), sb("router", [P, KT, EXPERTS])
        self.rows, self.cols = sb("rows", [P, N_ROWS, D]), sb("cols", [P, N_COLS])
        self.bias8, self.logits = sb("bias8", [P, 2, EXPERTS]), sb("logits", [P, NT, EXPERTS])
        self.owner = sb("owner", [P, 64], I32)
        self.slots0 = dram("slots0", [MOE0_CHUNKS * CHUNK + TOP_K * NP, D])
        self.slots1 = dram("slots1", [MOE1_CHUNKS * CHUNK + NP, D])
        self.results0, self.results1 = dram("results0", [MOE0_CHUNKS * CHUNK, D]), dram("results1", [MOE1_CHUNKS * CHUNK, D])
        self.x_kept, self.qk = dram("x_kept", [P, NT * D]), dram("qk_parts", [2, 2 * HG, P, NP])


def program(nc, t, out, phases="gnn0 moe0 gnn1 att moe1"):
    NAMES.clear()
    with ExitStack() as ctx:
        used = [0]

        def stage():
            stack = ExitStack()

            def sem(name):
                used[0] += 1
                return stack.enter_context(nc.semaphore(f"{name}_{used[0]}"))

            return stack, sem

        m = Memory(nc, ctx)
        stack, s = stage()
        with stack:
            constants(nc, m, t, s)
        stack, s = stage()
        with stack:
            inverse_roots(nc, m, s)
        if "gnn0" in phases:
            stack, s = stage()
            with stack:
                normalise(nc, m, s, m.x, m.xhat)
                graph_layer(nc, m, t, s, m.wg0, m.dis0, m.rows[:, 0, :], False)
        if "moe0" in phases:
            stack, s = stage()
            with stack:
                normalise(nc, m, s, m.x, m.xhat)
                mixture(nc, m, t, s, 0, m.xhat, m.gate, m.bias8[:, 0, :], None, MOE0_CHUNKS, m.slots0, m.results0, m.x)
        if "gnn1" in phases:
            stack, s = stage()
            with stack:
                normalise(nc, m, s, m.x, m.xhat)
                graph_layer(nc, m, t, s, m.wg1, m.dis1, m.rows[:, 1, :], True)
        if "att" in phases:
            stack, s = stage()
            with stack:
                attention(nc, m, t, s)
        if "moe1" in phases:
            stack, s = stage()
            with stack:
                second_mixture(nc, m, t, s)
        stack, s = stage()
        with stack:
            put = s("out_stored")
            with nc.Block() as block:

                @block.sync
                def _(sp):
                    sp.dma_start(out, m.x[:]).then_inc(put, 16)
                    sp.wait_ge(put, 16)




def host_layout(inputs):
    g = {k: np.asarray(v) for k, v in inputs.items()}
    x = np.zeros((NP, D), np.float32)
    x[:TOKENS] = g["x"]
    adj = np.zeros((NP, NP), np.float32)
    adj[:TOKENS, :TOKENS] = g["adj"]
    a = {"x": x.reshape(NT, P, D).transpose(1, 0, 2), "adj": adj,
         "adjT": adj.reshape(NCH, CHUNK, 2, HALF, P).transpose(0, 2, 4, 3, 1).reshape(NCH, 2, P, HALF * CHUNK)}

    def by_feature(w):
        return w.reshape(KT, P, -1).transpose(1, 0, 2)

    a["W0"], a["W1"] = by_feature(g["L0_gnn_W"].T), by_feature(g["L1_gnn_W"])
    a["gate"], a["router"] = by_feature(g["L0_ffn_gate_w"]), by_feature(g["L1_ffn_router_w"])
    for n in "qkvo":
        a["w" + n] = by_feature(g[f"L1_ffn_w{n}"])
    rows = ("L0_gnn_b", "L1_gnn_b", "L1_ffn_ln2_g", "L1_ffn_ln2_b", "L1_ffn_bv", "L1_ffn_bo")
    a["rows"] = np.broadcast_to(np.stack([g[n] for n in rows]), (P, N_ROWS, D))
    a["cols"] = np.concatenate([g[n].reshape(KT, P).T for n in ("L1_ffn_ln1_g", "L1_ffn_ln1_b", "L1_ffn_bq", "L1_ffn_bk")], 1)
    a["bias8"] = np.broadcast_to(np.stack([g["L0_ffn_gate_b"], g["L1_ffn_router_b"]]), (P, 2, EXPERTS))
    for n in (0, 1):
        f = f"L{n}_ffn_"
        a[f"w1_{n}"] = g[f + "w1"].reshape(EXPERTS, KT, P, HID).transpose(0, 2, 1, 3).reshape(EXPERTS, P, KT * HID)
        a[f"w2_{n}"] = g[f + "w2"].reshape(EXPERTS, HT, P, D).transpose(0, 2, 1, 3).reshape(EXPERTS, P, HT * D)
        a[f"b1_{n}"] = g[f + "b1"].reshape(EXPERTS, HT, P).transpose(0, 2, 1)
        a[f"b2_{n}"] = np.broadcast_to(g[f + "b2"][:, None], (EXPERTS, P, D))
    return {k: np.ascontiguousarray(v) for k, v in a.items()}


def kernel(**inputs):
    import concourse.bacc as bacc
    from concourse.bass_utils import run_bass_kernel_spmd

    nc = bacc.Bacc("TRN2", target_bir_lowering=False, num_devices=1)
    arrays = host_layout(inputs)
    t = {n: nc.dram_tensor(n, a.shape, F32, kind="ExternalInput").ap() for n, a in arrays.items()}
    out = nc.dram_tensor("out", (P, NT, D), F32, kind="ExternalOutput").ap()
    program(nc, t, out)
    r = run_bass_kernel_spmd(nc, [arrays], core_ids=[0])
    return r.results[0]["out"].transpose(1, 0, 2).reshape(NP, D)[:TOKENS]
```

```python
import numpy as np
from contextlib import ExitStack
import concourse.bass as bass
from concourse import mybir

F32 = mybir.dt.float32
F32R = mybir.dt.float32r
BF16 = mybir.dt.bfloat16
I32 = mybir.dt.int32
ALU = mybir.AluOpType
ACT = mybir.ActivationFunctionType
AX = mybir.AxisListType
ds = bass.ds

TOKENS, D, HID, EXPERTS, HEADS = 3327, 256, 1024, 8, 8
P = 128
DK = D // HEADS
NT = -(-TOKENS // P)
NP = NT * P
KT = D // P
HT = HID // P
LAST = TOKENS - (NT - 1) * P
CHUNK = 256
NCH = NP // CHUNK
HALF = NT // 2
TOP_K = 2
CAPACITY = int(np.ceil(TOKENS * 1.6 / EXPERTS))
HG = HEADS // 4
ZERO_COLS = 4096
LN_EPS, GNN_EPS = 1e-5, 1e-8
N_ROWS, N_COLS = 6, 8


def slot_chunks(assigned):
    most = (assigned + EXPERTS * (CHUNK - 1)) // CHUNK
    return most + most % 2


MOE0_CHUNKS = slot_chunks(TOP_K * TOKENS)
MOE1_CHUNKS = slot_chunks(TOKENS)


NAMES = []


def named(name):
    NAMES.append(name)
    return f"{name}_{len(NAMES)}"


class Count:

    def __init__(self, sem):
        self.sem, self.value = sem, 0

    def inc(self, ins):
        ins.then_inc(self.sem, 1)
        self.value += 1

    def settle(self, eng):
        eng.wait_ge(self.sem, self.value)


def constants(nc, m, t, s):
    made, loaded = s("made"), s("params_loaded")
    x_loaded, zero_made, zero_done = s("x_loaded"), s("zero_made"), s("zero_done")
    rows_loaded = [s("rows_loaded0"), s("rows_loaded1")]
    rows_summed = s("rows_summed")
    zero_dmas = []
    with nc.sbuf_tensor(named("adj_rows"), [P, 2, NP], F32) as adj_rows, \
            nc.sbuf_tensor(named("zeros"), [P, ZERO_COLS], F32) as zeros, \
            nc.sbuf_tensor(named("iota_i"), [P, 64], I32) as iota_i, \
            nc.Block() as block:

        @block.gpsimd
        def _(pool):
            c = Count(made)
            c.inc(pool.memset(m.ident[:], 0.0))
            c.inc(pool.memset(m.ident_b[:], 0.0))
            c.inc(pool.memset(m.ones[:], 1.0))
            c.settle(pool)
            c.inc(pool.affine_select(out=m.ident[:], in_=m.ident[:], compare_op=ALU.not_equal, fill=1.0, base=0,
                                     pattern=[[-1, P]], channel_multiplier=1))
            c.inc(pool.affine_select(out=m.ident_b[:], in_=m.ident_b[:], compare_op=ALU.not_equal, fill=1.0,
                                     base=0, pattern=[[-1, P]], channel_multiplier=1))
            c.inc(pool.affine_select(out=m.before[:], in_=m.ones[:], compare_op=ALU.is_gt, fill=0.0, base=0,
                                     pattern=[[1, P]], channel_multiplier=-1))
            c.inc(pool.affine_select(out=m.real[:], in_=m.ones[:, 0:NT], compare_op=ALU.is_gt, fill=0.0,
                                     base=TOKENS, pattern=[[-P, NT]], channel_multiplier=-1))
            c.inc(pool.iota(iota_i[:], [[1, 64]], base=0, channel_multiplier=0))
            c.inc(pool.iota(m.token[:], [[P, NT]], base=0, channel_multiplier=1))
            c.settle(pool)
            c.inc(pool.tensor_copy(m.iota[:], iota_i[:]))
            c.inc(pool.tensor_copy(m.token_f[:], m.token[:]))
            c.settle(pool)
            c.inc(pool.tensor_scalar(m.multiples[:], m.iota[:, 0:NCH], float(CHUNK), None, ALU.mult))
            c.settle(pool)

        @block.scalar
        def _(act):
            for dst, src in ((m.wg0, t["W0"]), (m.wg1, t["W1"]), (m.gate, t["gate"]), (m.router, t["router"]),
                             (m.rows, t["rows"]), (m.cols, t["cols"]), (m.bias8, t["bias8"])):
                act.dma_start(dst[:], src).then_inc(loaded, 16)
            act.wait_ge(zero_made, 1)
            for slots, rows in ((m.slots0, MOE0_CHUNKS * 2), (m.slots1, MOE1_CHUNKS * 2)):
                view = slots[0:rows * P, :].rearrange("(p n) d -> p (n d)", n=rows)
                for n in range(0, rows * D, ZERO_COLS):
                    w = min(ZERO_COLS, rows * D - n)
                    act.dma_start(view[:, n:n + w], zeros[:, 0:w]).then_inc(zero_done, 16)
                    zero_dmas.append(n)
            act.wait_ge(loaded, 16 * 7)
            act.wait_ge(zero_done, 16 * len(zero_dmas))

        @block.sync
        def _(sp):
            sp.dma_start(m.x[:], t["x"]).then_inc(x_loaded, 16)
            with sp.Fori(0, NT // 2) as i:
                for k in range(2):
                    sp.wait_ge(rows_summed, i * 2 + k + 1)
                    sp.dma_start(adj_rows[:, k, :], t["adj"][ds(i * 2 * P + k * P, P), :]).then_inc(rows_loaded[k], 16)
            sp.wait_ge(x_loaded, 16)

        @block.vector
        def _(dve):
            dve.sem_inc(rows_summed, 2)
            dve.memset(zeros[:], 0.0).then_inc(zero_made, 1)
            with dve.Fori(0, NT // 2) as i:
                for k in range(2):
                    dve.wait_ge(rows_loaded[k], i * 16 + 16)
                    dve.tensor_reduce(m.deg[:, ds(i * 2 + k, 1)], adj_rows[:, k, :], AX.X, ALU.add)\
                       .then_inc(rows_summed, 1)
            dve.wait_ge(rows_summed, NT + 2)


def inverse_root(dve, c, rooted, n, r, w, tmp):
    dve.wait_ge(rooted, n)
    for ins in (lambda: dve.reciprocal(r, r),
                lambda: dve.tensor_tensor(tmp, r, r, ALU.mult),
                lambda: dve.tensor_tensor(tmp, tmp, w, ALU.mult),
                lambda: dve.tensor_scalar(tmp, tmp, -0.5, 1.5, ALU.mult, ALU.add),
                lambda: dve.tensor_tensor(r, r, tmp, ALU.mult)):
        c.inc(ins())
        c.settle(dve)


def inverse_roots(nc, m, s):
    guard, rooted = s("guarded"), s("rooted")
    with nc.sbuf_tensor(named("deg_tmp"), [P, 4, NT], F32) as tmp, nc.Block() as block:

        @block.vector
        def _(dve):
            c = Count(guard)
            c.inc(dve.tensor_scalar(tmp[:, 0, :], m.deg[:], GNN_EPS, None, ALU.add))
            c.inc(dve.tensor_scalar(tmp[:, 1, :], m.deg[:], 1e-34, None, ALU.max))
            c.inc(dve.tensor_scalar(tmp[:, 2, :], m.deg[:], 0.0, None, ALU.is_gt))
            inverse_root(dve, c, rooted, 1, m.dis0[:], tmp[:, 0, :], tmp[:, 3, :])
            inverse_root(dve, c, rooted, 2, m.dis1[:], tmp[:, 1, :], tmp[:, 3, :])
            c.inc(dve.tensor_tensor(m.dis1[:], m.dis1[:], tmp[:, 2, :], ALU.mult))
            c.settle(dve)

        @block.scalar
        def _(act):
            act.wait_ge(guard, 2)
            act.activation(m.dis0[:], tmp[:, 0, :], ACT.Sqrt).then_inc(rooted, 1)
            act.activation(m.dis1[:], tmp[:, 1, :], ACT.Sqrt).then_inc(rooted, 1)


def normalise(nc, m, s, src, dst):
    stats, rooted, applied = s("stats"), s("var_rooted"), s("applied")
    with nc.sbuf_tensor(named("bn_st"), [P, NT, 6], F32) as st, nc.sbuf_tensor(named("bn_mv"), [P, NT, 2], F32) as mv, \
            nc.sbuf_tensor(named("bn_rs"), [P, NT], F32) as rs, nc.sbuf_tensor(named("bn_nb"), [P, NT], F32) as nb, \
            nc.sbuf_tensor(named("bn_vr"), [P, NT], F32) as vr, \
            nc.Block() as block:

        @block.vector
        def _(dve):
            c = Count(stats)
            for k in range(NT):
                c.inc(dve.bn_stats(st[:, k, :], src[:, k, :]))
            c.settle(dve)
            for k in range(NT):
                c.inc(dve.bn_aggr(mv[:, k, :], st[:, k, :]))
            c.settle(dve)
            c.inc(dve.tensor_scalar(vr[:], mv[:, :, 1], LN_EPS, None, ALU.add))
            inverse_root(dve, c, rooted, 1, rs[:], vr[:], nb[:])
            dve.scalar_tensor_tensor(nb[:], mv[:, :, 0], -1.0, rs[:], ALU.mult, ALU.mult).then_inc(applied, 1)
            with dve.Fori(0, NT // 2) as i:
                dve.tensor_scalar(dst[:, ds(i, 1), :], src[:, ds(i, 1), :],
                                  mv[:, ds(i, 1), 0:1].rearrange("p a b -> p (a b)"),
                                  rs[:, ds(i, 1)], ALU.subtract, ALU.mult)
            dve.drain()

        @block.scalar
        def _(act):
            act.wait_ge(stats, 2 * NT + 1)
            act.activation(rs[:], vr[:], ACT.Sqrt).then_inc(rooted, 1)
            act.wait_ge(applied, 1)
            with act.Fori(NT // 2, NT) as i:
                act.activation(dst[:, ds(i, 1), :], src[:, ds(i, 1), :], ACT.Identity,
                               bias=nb[:, ds(i, 1)], scale=rs[:, ds(i, 1)])
            act.drain()


def transposed_products(nc, m, s, src, products, take_act, take_dve, n_psum, affine=None, tail_sp=None):
    turned, copied, multiplied = s("turned"), s("copied"), s("multiplied")
    act_took, dve_took = s("act_took"), s("dve_took")
    with nc.sbuf_tensor(named("xt"), [P, 2, KT, P], F32) as xt, nc.psum_tensor(named("ps_turn"), [P, 2, 512], F32) as ps_turn, \
            nc.psum_tensor(named("ps_prod"), [P, 2, n_psum, 512], F32) as ps, nc.Block() as block:

        @block.tensor
        def _(pe):
            def turn(k):
                if k >= 2:
                    pe.wait_ge(copied, k - 1)
                for j in range(KT):
                    last = pe.transpose(ps_turn[:, k % 2, j * P:(j + 1) * P], src[:, k, j * P:(j + 1) * P], m.ident[:])
                last.then_inc(turned, 1)

            def multiply(k):
                pe.wait_ge(copied, k + 1)
                if k >= 2:
                    pe.wait_ge(act_took, k - 1)
                    pe.wait_ge(dve_took, k - 1)
                products(pe, xt[:, k % 2], ps[:, k % 2]).then_inc(multiplied, 1)

            turn(0)
            for k in range(NT):
                if k + 1 < NT:
                    turn(k + 1)
                multiply(k)

        @block.scalar
        def _(act):
            def copy(k):
                act.wait_ge(turned, k + 1)
                if k >= 2:
                    act.wait_ge(multiplied, k - 1)
                for j in range(KT):
                    if affine:
                        last = act.activation(xt[:, k % 2, j, :], ps_turn[:, k % 2, j * P:(j + 1) * P], ACT.Identity,
                                              bias=affine[1][:, j:j + 1], scale=affine[0][:, j:j + 1])
                if not affine:
                    last = act.activation(xt[:, k % 2].rearrange("p j n -> p (j n)"), ps_turn[:, k % 2, 0:D], ACT.Copy)
                last.then_inc(copied, 1)

            copy(0)
            for k in range(NT):
                if k + 1 < NT:
                    copy(k + 1)
                act.wait_ge(multiplied, k + 1)
                take_act(act, k, ps[:, k % 2], act_took)
            act.wait_ge(act_took, NT)

        @block.vector
        def _(dve):
            for k in range(NT):
                dve.wait_ge(multiplied, k + 1)
                take_dve(dve, k, ps[:, k % 2], act_took, dve_took)
            dve.wait_ge(dve_took, NT)

        if tail_sp:
            @block.sync
            def _(sp):
                tail_sp(sp, act_took, dve_took)


def graph_layer(nc, m, t, s, w, dis, bias, relu):
    with nc.sbuf_tensor(named("y_hi"), [P, NT, D], F32R) as y_hi, nc.sbuf_tensor(named("y_lo"), [P, NT, D], F32R) as y_lo:

        def products(pe, xt, ps):
            for j in range(KT):
                last = pe.matmul(ps[:, 0, 0:D], xt[:, j, :], w[:, j, :], start=j == 0, stop=j == KT - 1)
            return last

        def take_act(act, k, ps, took):
            act.activation(y_hi[:, k, :], ps[:, 0, 0:D], ACT.Copy, scale=dis[:, k:k + 1]).then_inc(took, 1)

        def take_dve(dve, k, ps, act_took, took):
            dve.wait_ge(act_took, k + 1)
            dve.scalar_tensor_tensor(y_lo[:, k, :], ps[:, 0, 0:D], dis[:, k:k + 1], y_hi[:, k, :].bitcast(F32),
                                     ALU.mult, ALU.subtract).then_inc(took, 1)

        transposed_products(nc, m, s, m.xhat, products, take_act, take_dve, 1)

        loaded = [s("adj_loaded0"), s("adj_loaded1")]
        hi_made, lo_made, used = s("hi_made"), s("lo_made"), s("halves_used")
        summed, taken, chain = s("chunk_summed"), s("chunk_taken"), s("taking")
        with nc.sbuf_tensor(named("adj_raw"), [P, 2, HALF * CHUNK], F32) as raw, \
                nc.sbuf_tensor(named("adj_hi"), [P, 2, HALF, CHUNK], F32R) as hi, \
                nc.sbuf_tensor(named("adj_lo"), [P, 2, HALF, CHUNK], F32R) as lo, \
                nc.sbuf_tensor(named("gnn_tmp"), [P, 2, D], F32) as tmp, \
                nc.psum_tensor(named("ps_gnn"), [P, 2, 512], F32) as ps, nc.Block() as block:

            @block.sync
            def _(sp):
                with sp.Fori(0, NCH) as c:
                    for k in range(2):
                        sp.wait_ge(lo_made, c * 2 + k + 1)
                        sp.dma_start(raw[:, k, :], t["adjT"][ds(c, 1), k].rearrange("a p n -> p (a n)")).then_inc(loaded[k], 16)

            @block.scalar
            def _(act):
                def split_hi(c, k):
                    act.wait_ge(loaded[k], c * 16 + 16)
                    if k == 0:
                        act.wait_ge(used, c + 1)
                    else:
                        act.wait_ge(summed, c * 2 + 2)
                    act.activation(hi[:, k].rearrange("p j n -> p (j n)"), raw[:, k, :], ACT.Copy).then_inc(hi_made, 1)

                with act.Fori(0, NCH) as c:
                    for k in range(2):
                        split_hi(c, k)
                act.wait_ge(hi_made, 2 * NCH)

            @block.tensor
            def _(pe):
                pe.sem_inc(used, 1)
                pe.sem_inc(summed, 2)
                with pe.Fori(0, NCH) as c:
                    for k in range(2):
                        pe.wait_ge(hi_made, c * 2 + k + 1)
                        pe.wait_ge(lo_made, c * 2 + k + 3)
                        for i in range(2):
                            if k == 0:
                                pe.wait_ge(taken, c * 2 + i + 1)
                            for j in range(HALF):
                                rows = slice(i * P, (i + 1) * P)
                                n = k * HALF + j
                                out = ps[:, i, 0:D]
                                pe.matmul(out, hi[:, k, j, rows], y_hi[:, n, :], start=n == 0, stop=False)
                                pe.matmul(out, hi[:, k, j, rows], y_lo[:, n, :], start=False, stop=False)
                                last = pe.matmul(out, lo[:, k, j, rows], y_hi[:, n, :], start=False, stop=n == NT - 1)
                            if k == 1:
                                last.then_inc(summed, 1)
                        if k == 0:
                            last.then_inc(used, 1)

            @block.vector
            def _(dve):
                dve.sem_inc(lo_made, 2)
                dve.sem_inc(taken, 2)

                def split_lo(c, k):
                    dve.wait_ge(hi_made, c * 2 + k + 1)
                    dve.tensor_tensor(lo[:, k].rearrange("p j n -> p (j n)"), raw[:, k, :],
                                      hi[:, k].rearrange("p j n -> p (j n)").bitcast(F32), ALU.subtract).then_inc(lo_made, 1)

                def take(c):
                    for i in range(2):
                        xs = m.x[:, ds(c * 2 + i, 1), :].rearrange("p a d -> p (a d)")
                        dve.wait_ge(summed, c * 2 + i + 3)
                        dve.scalar_tensor_tensor(tmp[:, i, :], ps[:, i, 0:D], dis[:, ds(c * 2 + i, 1)], bias,
                                                 ALU.mult, ALU.add).then_inc(taken, 1)
                        dve.wait_ge(taken, c * 2 + i + 3)
                        if relu:
                            dve.scalar_tensor_tensor(xs, tmp[:, i, :], 0.0, xs, ALU.max, ALU.add).then_inc(chain, 1)
                        else:
                            dve.tensor_tensor(xs, tmp[:, i, :], xs, ALU.add).then_inc(chain, 1)
                        dve.wait_ge(chain, c * 2 + i + 1)

                split_lo(0, 0)
                split_lo(0, 1)
                with dve.Fori(0, NCH - 1) as c:
                    split_lo(c + 1, 0)
                    take(c)
                    split_lo(c + 1, 1)
                take(NCH - 1)


def mixture_routes(nc, m, s, bias, top, capacity, chunks, slot_sets, weights):
    c_act, c_dve, c_pe = s("route_exp"), s("route_dve"), s("route_sums")
    with ExitStack() as ctx:
        def sb(name, shape, dt=F32):
            return ctx.enter_context(nc.sbuf_tensor(named("rt_" + name), shape, dt))

        hots = [sb(f"choice{k}", [P, NT, EXPERTS]) for k in range(top)]
        prob, key, mask = sb("prob", [P, NT, EXPERTS]), sb("key", [P, NT, EXPERTS]), sb("mask", [P, NT, EXPERTS])
        rank, best, total = sb("rank", [P, NT, EXPERTS]), sb("best", [P, NT]), sb("total", [P, NT])
        carry = sb("carry", [P, NT + 1, EXPERTS])
        steps, full = sb("steps", [P, EXPERTS, NCH]), sb("full", [P, EXPERTS])
        ends, base = sb("ends", [P, EXPERTS + 1]), sb("base", [P, EXPERTS])
        fine = sb("fine", [P, NT])
        mask_at = []
        owner, owner_f = sb("owner", [P, chunks, EXPERTS]), sb("owner_f", [P, chunks])
        ps = ctx.enter_context(nc.psum_tensor(named("ps_rank"), [P, 2, 512], F32))
        block = ctx.enter_context(nc.Block())
        W = NT * EXPERTS
        rounds = 1 if capacity is None else 2

        def over_experts(a):
            return a.rearrange("p (t a) -> p t a", a=1).broadcast_to([P, NT, EXPERTS])

        def by_expert(a):
            return a.rearrange("p (a e) -> p a e", a=1).broadcast_to([P, NT, EXPERTS])

        @block.vector
        def _(dve):
            c = Count(c_dve)

            def do(ins):
                c.inc(ins)
                c.settle(dve)

            up = m.iota[:, 1:EXPERTS + 1]

            do(dve.tensor_tensor(mask[:], m.logits[:], by_expert(bias), ALU.add))
            do(dve.tensor_reduce(best[:], mask[:], AX.X, ALU.max))
            do(dve.tensor_tensor(key[:], mask[:], over_experts(best[:]), ALU.subtract))
            dve.wait_ge(c_act, 1)
            do(dve.tensor_reduce(total[:], prob[:], AX.X, ALU.add))
            do(dve.reciprocal(total[:], total[:]))
            do(dve.tensor_tensor(prob[:], prob[:], over_experts(total[:]), ALU.mult))

            def first_of(values, hot):
                do(dve.tensor_reduce(best[:], values[:], AX.X, ALU.max))
                do(dve.tensor_tensor(key[:], values[:], over_experts(best[:]), ALU.is_equal))
                do(dve.tensor_tensor(key[:], key[:], by_expert(m.falling[:]), ALU.mult))
                do(dve.tensor_reduce(total[:], key[:], AX.X, ALU.max))
                do(dve.tensor_tensor(hot[:], key[:], over_experts(total[:]), ALU.is_equal))

            do(dve.tensor_scalar(m.falling[:], m.iota[:, 0:EXPERTS], -1.0, float(EXPERTS), ALU.mult, ALU.add))
            for k in range(top):
                first_of(prob, hots[k])
                if capacity is None:
                    do(dve.tensor_copy(weights[k][:], best[:]))
                if k + 1 < top:
                    do(dve.scalar_tensor_tensor(prob[:], hots[k][:], -4.0, prob[:], ALU.mult, ALU.add))

            def ranks():
                mask_at.append(c.value)
                dve.wait_ge(c_pe, len(mask_at))
                do(dve.memset(carry[:, 0, :], 0.0))
                for k in range(NT):
                    do(dve.tensor_tensor(carry[:, k + 1, :], carry[:, k, :],
                                         ps[:, 1, k * EXPERTS:(k + 1) * EXPERTS], ALU.add))
                do(dve.tensor_tensor(rank[:], carry[:, 0:NT, :],
                                     ps[:, 0, 0:W].rearrange("p (t e) -> p t e", e=EXPERTS), ALU.add))

            do(dve.tensor_tensor(mask[:], hots[0][:], hots[1][:], ALU.add))
            do(dve.tensor_tensor(mask[:], mask[:], over_experts(m.real[:]), ALU.mult))
            ranks()
            if capacity is not None:
                do(dve.scalar_tensor_tensor(key[:], rank[:], float(capacity), mask[:], ALU.is_lt, ALU.mult))
                do(dve.tensor_tensor(key[:], key[:], by_expert(up), ALU.mult))
                do(dve.tensor_reduce(best[:], key[:], AX.X, ALU.max))
                do(dve.tensor_scalar(weights[0][:], best[:], 0.0, None, ALU.is_gt))
                do(dve.tensor_tensor(mask[:], key[:], over_experts(best[:]), ALU.is_equal))
                do(dve.tensor_tensor(mask[:], mask[:], over_experts(weights[0][:]), ALU.mult))
                ranks()
                rows_of, ok = [mask], weights[0]
            else:
                rows_of, ok = hots, m.real
            do(dve.tensor_tensor(steps[:], carry[:, NT, :].rearrange("p (e a) -> p e a", a=1).broadcast_to([P, EXPERTS, NCH]),
                                 m.multiples[:].rearrange("p (a n) -> p a n", a=1).broadcast_to([P, EXPERTS, NCH]), ALU.is_gt))
            do(dve.tensor_reduce(full[:], steps[:], AX.X, ALU.add))
            do(dve.memset(ends[:, 0:1], 0.0))
            for e in range(EXPERTS):
                do(dve.tensor_tensor(ends[:, e + 1:e + 2], ends[:, e:e + 1], full[:, e:e + 1], ALU.add))
            do(dve.tensor_tensor(owner[:], ends[:, 1:].rearrange("p (a e) -> p a e", a=1).broadcast_to([P, chunks, EXPERTS]),
                                 m.iota[:, 0:chunks].rearrange("p (n a) -> p n a", a=1).broadcast_to([P, chunks, EXPERTS]), ALU.is_le))
            do(dve.tensor_reduce(owner_f[:], owner[:], AX.X, ALU.add))
            do(dve.tensor_scalar(m.owner[:, 0:chunks], owner_f[:], float(EXPERTS - 1), None, ALU.min))
            do(dve.tensor_scalar(base[:], ends[:, 0:EXPERTS], float(CHUNK), None, ALU.mult))
            do(dve.tensor_tensor(rank[:], rank[:], by_expert(base[:]), ALU.add))
            do(dve.tensor_scalar(fine[:], ok[:], -1.0, 1.0, ALU.mult, ALU.add))
            for n, (hot, (put, get)) in enumerate(zip(rows_of, slot_sets)):
                do(dve.tensor_tensor(key[:], hot[:], rank[:], ALU.mult))
                do(dve.tensor_reduce(best[:], key[:], AX.X, ALU.add))
                do(dve.scalar_tensor_tensor(total[:], m.token_f[:], float(chunks * CHUNK + n * NP), best[:],
                                            ALU.add, ALU.subtract))
                do(dve.tensor_tensor(total[:], total[:], fine[:], ALU.mult))
                do(dve.tensor_tensor(put[:], total[:], best[:], ALU.add))
                do(dve.tensor_scalar(get[:], best[:], float(chunks * CHUNK - 1), None, ALU.min))

        @block.scalar
        def _(act):
            act.wait_ge(c_dve, 3)
            act.activation(prob[:], key[:], ACT.Exp).then_inc(c_act, 1)

        @block.tensor
        def _(pe):
            for r in range(rounds):
                pe.wait_ge(c_dve, mask_at[r])
                flat = mask[:].rearrange("p t e -> p (t e)")
                pe.matmul(ps[:, 0, 0:W], m.before[:], flat, start=True, stop=True)
                pe.matmul(ps[:, 1, 0:W], m.ones[:], flat, start=True, stop=True).then_inc(c_pe, 1)



def mixture_scatter(nc, m, s, rows, slots, puts):
    sent = s("rows_sent")
    with nc.Block() as block:

        @block.gpsimd
        def _(pool):
            for put in puts:
                for k in range(NT):
                    pool.indirect_dma_start(out=slots, out_offset=bass.IndirectOffsetOnAxis(put[:, k:k + 1], 0),
                                            in_=rows[:, k, :], in_offset=None).then_inc(sent, 16)
            pool.wait_ge(sent, 16 * NT * len(puts))


def expert_layers(nc, m, t, s, layer, chunks, slots, results):
    loaded = [s("expert_loaded0"), s("expert_loaded1")]
    bias_loaded = [s("bias_loaded0"), s("bias_loaded1")]
    turned, rows_hi, rows_lo = s("ex_turned"), s("ex_rows_hi"), s("ex_rows_lo")
    weights_hi, weights_lo = s("ex_weights_hi"), s("ex_weights_lo")
    hidden_ps, gelu_made, hidden_hi, hidden_lo = s("ex_hidden_ps"), s("ex_gelu"), s("ex_hidden_hi"), s("ex_hidden_lo")
    out_ps, out_made = s("ex_out_ps"), s("ex_out_made")
    stored, res_free = [s("ex_stored0"), s("ex_stored1")], s("ex_res_free")
    w1_d, w2_d, b1_d, b2_d = (t[f"{n}_{layer}"] for n in ("w1", "w2", "b1", "b2"))
    TT = CHUNK // P
    W = KT * HID
    PAIRS = HT // 2
    with ExitStack() as ctx:
        def sb(name, shape, dt=F32):
            return ctx.enter_context(nc.sbuf_tensor(named("ex_" + name), shape, dt))

        w, w_hi, w_lo = sb("w", [P, 2, 2, W]), sb("w_hi", [P, 2, 2, W], F32R), sb("w_lo", [P, 2, 2, W], F32R)
        b1, b2 = sb("b1", [P, 2, HT]), sb("b2", [P, 2, D])
        rows = sb("rows", [P, 2, TT, D])
        rt_hi, rt_lo = sb("rt_hi", [P, KT, CHUNK], F32R), sb("rt_lo", [P, KT, CHUNK], F32R)
        hid, hid_hi, hid_lo = sb("hid", [P, HT, CHUNK]), sb("hid_hi", [P, HT, CHUNK], F32R), sb("hid_lo", [P, HT, CHUNK], F32R)
        res = sb("res", [P, 2, TT, D])
        ps_t = ctx.enter_context(nc.psum_tensor(named("ps_ex_t"), [P, KT, 512], F32))
        ps_h = ctx.enter_context(nc.psum_tensor(named("ps_ex_h"), [P, 4, 512], F32))
        ps_o = ctx.enter_context(nc.psum_tensor(named("ps_ex_o"), [P, TT, 512], F32))
        block = ctx.enter_context(nc.Block())

        def each_chunk(eng, one):
            with eng.Fori(0, chunks // 2 - 1) as i:
                one(i * 2, 0, True)
                one(i * 2 + 1, 1, True)
            one(chunks - 2, 0, True)
            one(chunks - 1, 1, False)

        @block.sync
        def _(sp):
            with sp.Fori(0, chunks // 2) as i:
                for k in range(2):
                    n = i * 2 + k
                    sp.wait_ge(weights_lo, n * 2 + 2)
                    e = sp.value_load(m.owner[0:1, ds(n, 1)], min_val=0, max_val=EXPERTS - 1)
                    sp.dma_start(rows[:, k], slots[ds(i * 2 * CHUNK + k * CHUNK, CHUNK), :].rearrange("(a p) d -> p a d", p=P)).then_inc(loaded[k], 16)
                    for dst, src in ((w[:, k, 0, :], w1_d), (w[:, k, 1, :], w2_d)):
                        sp.dma_start(dst, src[ds(e, 1)].rearrange("a p n -> (a p) n")).then_inc(loaded[k], 16)
                    sp.wait_ge(out_made, n + 1)
                    for dst, src in ((b1[:, k, :], b1_d), (b2[:, k, :], b2_d)):
                        sp.dma_start(dst, src[ds(e, 1)].rearrange("a p n -> (a p) n")).then_inc(bias_loaded[k], 16)

        def arrived(eng, n, k):
            eng.wait_ge(loaded[k], n * 24 + (48 - 24 * k))

        @block.tensor
        def _(pe):
            def turn(n, k):
                arrived(pe, n, k)
                for a in range(TT):
                    for j in range(KT):
                        last = pe.transpose(ps_t[:, j, a * P:(a + 1) * P], rows[:, k, a, j * P:(j + 1) * P], m.ident[:])
                last.then_inc(turned, 1)

            def three(out, hi, lo, by_hi, by_lo, start, stop):
                pe.matmul(out, hi, by_hi, start=start, stop=False)
                pe.matmul(out, hi, by_lo, start=False, stop=False)
                return pe.matmul(out, lo, by_hi, start=False, stop=stop)

            turn(0, 0)

            def one(n, k, has_next):
                pe.wait_ge(rows_lo, n + 1)
                pe.wait_ge(weights_lo, n * 2 + 5)
                for h in range(HT):
                    pe.wait_ge(gelu_made, n * HT + (h + 1))
                    for j in range(KT):
                        at = slice(j * HID + h * P, j * HID + (h + 1) * P)
                        last = three(ps_h[:, h % 4, 0:CHUNK], w_hi[:, k, 0, at], w_lo[:, k, 0, at],
                                     rt_hi[:, j, :], rt_lo[:, j, :], j == 0, j == KT - 1)
                    last.then_inc(hidden_ps, 1)
                if has_next:
                    turn(n + 1, 1 - k)
                pe.wait_ge(out_made, n + 2)
                pe.wait_ge(hidden_lo, n * PAIRS + 2 * PAIRS)
                pe.wait_ge(weights_lo, n * 2 + 6)
                for a in range(TT):
                    for h in range(HT):
                        at, rows_at = slice(h * D, (h + 1) * D), slice(a * P, (a + 1) * P)
                        last = three(ps_o[:, a, 0:D], hid_hi[:, h, rows_at], hid_lo[:, h, rows_at],
                                     w_hi[:, k, 1, at], w_lo[:, k, 1, at], h == 0, h == HT - 1)
                last.then_inc(out_ps, 1)

            each_chunk(pe, one)

        @block.scalar
        def _(act):
            act.sem_inc(gelu_made, 4)

            def prepare(n, k):
                act.wait_ge(turned, n + 1)
                act.activation(rt_hi[:], ps_t[:, :, 0:CHUNK], ACT.Copy).then_inc(rows_hi, 1)
                arrived(act, n, k)
                for layer in range(2):
                    act.activation(w_hi[:, k, layer, :], w[:, k, layer, :], ACT.Copy).then_inc(weights_hi, 1)

            prepare(0, 0)

            def one(n, k, has_next):
                act.wait_ge(bias_loaded[k], n * 16 + (32 - 16 * k))
                for h in range(HT):
                    act.wait_ge(hidden_ps, n * HT + (h + 1))
                    if h % 2 == 0:
                        act.wait_ge(hidden_lo, n * PAIRS + (h // 2 + 1))
                    act.activation(hid[:, h, :], ps_h[:, h % 4, 0:CHUNK], ACT.Gelu, bias=b1[:, k, h:h + 1]).then_inc(gelu_made, 1)
                if has_next:
                    prepare(n + 1, 1 - k)

            each_chunk(act, one)

        @block.vector
        def _(dve):
            dve.sem_inc(out_ps, 1)
            dve.sem_inc(out_made, 2)
            dve.sem_inc(hidden_lo, PAIRS)
            dve.sem_inc(weights_lo, 4)

            def prepare(n, k):
                dve.wait_ge(rows_hi, n + 1)
                dve.tensor_tensor(rt_lo[:], ps_t[:, :, 0:CHUNK], rt_hi[:].bitcast(F32), ALU.subtract).then_inc(rows_lo, 1)
                for layer in range(2):
                    dve.wait_ge(weights_hi, n * 2 + (layer + 1))
                    dve.tensor_tensor(w_lo[:, k, layer, :], w[:, k, layer, :], w_hi[:, k, layer, :].bitcast(F32),
                                      ALU.subtract).then_inc(weights_lo, 1)

            prepare(0, 0)

            def one(n, k, has_next):
                dve.wait_ge(out_ps, n + 1)
                for q in range(PAIRS):
                    two = slice(2 * q, 2 * q + 2)
                    dve.wait_ge(gelu_made, n * HT + (2 * q + 6))
                    dve.tensor_copy(hid_hi[:, two, :], hid[:, two, :]).then_inc(hidden_hi, 1)
                    dve.wait_ge(hidden_hi, n * PAIRS + (q + 1))
                    dve.tensor_tensor(hid_lo[:, two, :], hid[:, two, :], hid_hi[:, two, :].bitcast(F32), ALU.subtract).then_inc(hidden_lo, 1)
                if has_next:
                    prepare(n + 1, 1 - k)
                dve.wait_ge(bias_loaded[k], n * 16 + (32 - 16 * k))
                dve.wait_ge(out_ps, n + 2)
                dve.wait_ge(res_free, n + 1)
                dve.tensor_tensor(res[:, k], ps_o[:, :, 0:D], b2[:, k, :].rearrange("p (a d) -> p a d", a=1).broadcast_to([P, TT, D]),
                                  ALU.add).then_inc(out_made, 1)

            each_chunk(dve, one)
            dve.wait_ge(out_made, chunks + 2)

        @block.gpsimd
        def _(pool):
            pool.sem_inc(res_free, 2)
            with pool.Fori(0, chunks // 2) as i:
                for k in range(2):
                    n = i * 2 + k
                    pool.wait_ge(out_made, n + 3)
                    pool.dma_start(results[ds(i * 2 * CHUNK + k * CHUNK, CHUNK), :].rearrange("(a p) d -> p a d", p=P),
                                   res[:, k]).then_inc(stored[k], 16)
                    pool.wait_ge(stored[k], i * 16 + 16)
                    pool.sem_inc(res_free, 1)


def mixture_gather(nc, m, s, results, gets, weights, x):
    RING = 4
    come = [s(f"row_come{k}") for k in range(RING)]
    added = s("row_added")
    with nc.sbuf_tensor(named("got"), [P, RING, D], F32) as got, nc.Block() as block:
        jobs = [(k, c) for k in range(NT) for c in range(len(gets))]

        @block.gpsimd
        def _(pool):
            for n, (k, c) in enumerate(jobs):
                if n >= RING:
                    pool.wait_ge(added, n - RING + 1)
                pool.indirect_dma_start(out=got[:, n % RING, :], out_offset=None, in_=results,
                                        in_offset=bass.IndirectOffsetOnAxis(gets[c][:, k:k + 1], 0)).then_inc(come[n % RING], 16)

        @block.vector
        def _(dve):
            for n, (k, c) in enumerate(jobs):
                dve.wait_ge(come[n % RING], 16 * (n // RING) + 16)
                if n:
                    dve.wait_ge(added, n)
                dve.scalar_tensor_tensor(x[:, k, :], got[:, n % RING, :], weights[c][:, k:k + 1], x[:, k, :],
                                         ALU.mult, ALU.add).then_inc(added, 1)
            dve.wait_ge(added, len(jobs))


def gate_logits(nc, m, s, src, w):
    def products(pe, xt, ps):
        for j in range(KT):
            last = pe.matmul(ps[:, 0, 0:EXPERTS], xt[:, j, :], w[:, j, :], start=j == 0, stop=j == KT - 1)
        return last

    def take_act(act, k, ps, took):
        act.activation(m.logits[:, k, :], ps[:, 0, 0:EXPERTS], ACT.Copy).then_inc(took, 1)

    def take_dve(dve, k, ps, act_took, took):
        dve.sem_inc(took, 1)

    transposed_products(nc, m, s, src, products, take_act, take_dve, 1)


def mixture(nc, m, t, s, layer, src, gate, bias, capacity, chunks, slots, results, x):
    n_rows = TOP_K if capacity is None else 1
    with ExitStack() as ctx:
        def sb(name, shape, dt=F32):
            return ctx.enter_context(nc.sbuf_tensor(f"mx{layer}_" + name, shape, dt))

        slot_sets = [(sb(f"put{c}", [P, NT], I32), sb(f"get{c}", [P, NT], I32)) for c in range(n_rows)]
        weights = [sb(f"weight{c}", [P, NT]) for c in range(n_rows)]
        gate_logits(nc, m, s, src, gate)
        mixture_routes(nc, m, s, bias, TOP_K, capacity, chunks, slot_sets, weights)
        mixture_scatter(nc, m, s, src, slots, [put for put, _ in slot_sets])
        expert_layers(nc, m, t, s, layer, chunks, slots, results)
        mixture_gather(nc, m, s, results, [get for _, get in slot_sets], weights, x)


def add_rows(nc, m, s, row):
    done = s("row_added_all")
    with nc.Block() as block:

        @block.vector
        def _(dve):
            dve.tensor_tensor(m.x[:], m.x[:], m.rows[:, row:row + 1, :].broadcast_to([P, NT, D]), ALU.add).then_inc(done, 1)
            dve.wait_ge(done, 1)


def keep_x(nc, m, s):
    stored = s("x_stored")
    with nc.Block() as block:

        @block.sync
        def _(sp):
            sp.dma_start(m.x_kept, m.x[:].rearrange("p t d -> p (t d)")).then_inc(stored, 16)
            sp.wait_ge(stored, 16)


def project(nc, m, t, s):
    loaded, kept = s("qkv_loaded"), [s("qk_kept0"), s("qk_kept1")]
    G = 2 * HG
    with nc.sbuf_tensor(named("wqk"), [P, 2, KT, D], F32) as wqk, nc.sbuf_tensor(named("wv"), [P, KT, D], F32) as wv, \
            nc.sbuf_tensor(named("qk_hi"), [P, 2, G, P], F32R) as hi, nc.sbuf_tensor(named("qk_lo"), [P, 2, G, P], F32R) as lo:
        with nc.Block() as block:

            @block.sync
            def _(sp):
                sp.dma_start(wqk[:, 0], t["wq"]).then_inc(loaded, 16)
                sp.dma_start(wqk[:, 1], t["wk"]).then_inc(loaded, 16)
                sp.dma_start(wv[:], t["wv"]).then_inc(loaded, 16)
                sp.wait_ge(loaded, 48)

        def products(pe, xt, ps):
            for g in range(G):
                for j in range(KT):
                    pe.matmul(ps[:, 0, g * P:(g + 1) * P], wqk[:, g // HG, j, g % HG * P:(g % HG + 1) * P], xt[:, j, :],
                              start=j == 0, stop=j == KT - 1)
            for j in range(KT):
                last = pe.matmul(ps[:, 1, 0:D], xt[:, j, :], wv[:, j, :], start=j == 0, stop=j == KT - 1)
            return last

        def take_act(act, k, ps, took):
            if k >= 2:
                act.wait_ge(kept[k % 2], k // 2 * 32)
            for g in range(G):
                last = act.activation(hi[:, k % 2, g, :], ps[:, 0, g * P:(g + 1) * P], ACT.Identity,
                                      bias=m.cols[:, 4 + g:5 + g])
            last.then_inc(took, 1)

        def take_dve(dve, k, ps, act_took, took):
            dve.tensor_tensor(m.xhat[:, k, :], ps[:, 1, 0:D], m.rows[:, 4, :], ALU.add)
            dve.wait_ge(act_took, k + 1)
            for g in range(G):
                last = dve.scalar_tensor_tensor(lo[:, k % 2, g, :], ps[:, 0, g * P:(g + 1) * P], m.cols[:, 4 + g:5 + g],
                                                hi[:, k % 2, g, :].bitcast(F32), ALU.add, ALU.subtract)
            last.then_inc(took, 1)

        def store(sp, act_took, dve_took):
            for k in range(NT):
                sp.wait_ge(act_took, k + 1)
                sp.wait_ge(dve_took, k + 1)
                for n, part in enumerate((hi, lo)):
                    sp.dma_start(m.qk[n, :, :, k * P:(k + 1) * P].rearrange("g p n -> p g n"),
                                 part[:, k % 2].bitcast(F32)).then_inc(kept[k % 2], 16)
            for k in range(2):
                sp.wait_ge(kept[k], 16 * NT)

        transposed_products(nc, m, s, m.xhat, products, take_act, take_dve, 2,
                            affine=(m.cols[:, 0:2], m.cols[:, 2:4]), tail_sp=store)


KEYS = 512
STACK = 3 * DK
FOUR = 4
RING = 4
POOL_TILES = [k for k in range(NT - 4) if k % 3 != 2]
DVE_TILES = [k for k in range(NT - 20) if k % 3 == 2]


def up_to(tiles, k):
    return sum(x <= k for x in tiles) if k >= 0 else -sum(x > NT + k for x in tiles)


def attend(nc, m, t, s):
    KC = -(-NP // KEYS)
    QT = CHUNK // P
    N_MAX = QT * FOUR * KC
    SPREAD = 3
    WO_AT = 8
    ahead = [("max", c) for c in range(N_MAX)] + [("row", half) for half in range(2)]
    finish = [("out", a) for a in range(QT)]

    def uses(b, has_next):
        last = finish if not (isinstance(b, int) and b <= 0) else []
        return ahead[:WO_AT] + last + ahead[WO_AT:] if has_next else last

    N_USES = len(ahead) + len(finish)
    PER_HG = len(ahead) * NCH + len(finish) * NCH
    scale = float(DK) ** -0.5
    k_loaded = [s(f"k_loaded{h}") for h in range(FOUR)]
    q_loaded, wo_loaded = [s("q_loaded0"), s("q_loaded1")], s("wo_loaded")
    ones_row = s("ones_row")
    scored, exped, used = s("scored"), s("exped"), s("probs_used")
    x_made, x_free, max_made, rows_made, context = s("x_made"), s("x_free"), s("max_made"), s("rows_made"), s("context")
    pool_added, dve_added, summed = s("pool_added"), s("dve_added"), s("summed")
    with ExitStack() as ctx:
        def sb(name, shape, dt=F32):
            return ctx.enter_context(nc.sbuf_tensor(named("at_" + name), shape, dt))

        def pb(name, shape):
            return ctx.enter_context(nc.psum_tensor("ps_" + name, shape, F32))

        kst, qst = sb("kst", [STACK + 1, FOUR, NP], F32R), sb("qst", [STACK + 1, 2, FOUR, CHUNK], F32R)
        probs, wo = sb("probs", [P, RING, FOUR, CHUNK]), sb("wo", [P, HG, D])
        pool_sum, dve_sum = sb("pool_sum", [P, 2, FOUR, CHUNK]), sb("dve_sum", [P, 2, FOUR, CHUNK])
        part_max, maxima = sb("part_max", [P, QT * FOUR, KC]), sb("maxima", [P, QT * FOUR], BF16)
        rden, cx = sb("rden", [P, CHUNK]), sb("cx", [P, CHUNK])
        ps_s, ps_oz = pb("s", [P, 2, FOUR, CHUNK]), pb("oz", [P, 2, 2, CHUNK])
        ps_x = pb("x", [P, 2, 512])
        block = ctx.enter_context(nc.Block())

        def blocks(eng, one):
            for hg in range(HG):
                one(hg, -1, 1, True)
                one(hg, 0, 0, True)
                with eng.Fori(0, (NCH - 3) // 2) as i:
                    one(hg, i * 2 + 1, 1, True)
                    one(hg, i * 2 + 2, 0, True)
                one(hg, NCH - 2, 1, True)
                one(hg, NCH - 1, 0, False)

        def uses_before(hg, b):
            if isinstance(b, int) and b <= 0:
                return hg * PER_HG + (len(ahead) if b == 0 else 0)
            return b * N_USES + (hg * PER_HG + 2 * len(ahead) - N_USES)

        def slot(par, k):
            return (par * NT + k) % RING

        @block.sync
        def _(sp):
            sp.dma_start(wo[:], t["wo"]).then_inc(wo_loaded, 16)

            def load_queries(hg, b, par):
                sp.wait_ge(scored, hg * NCH * NT + 2 * NT if isinstance(b, int) else b * NT + (hg * NCH + 1) * NT)
                for r, part in enumerate((0, 1, 0)):
                    sp.dma_start(qst[r * DK:(r + 1) * DK, par, :, :].bitcast(F32),
                                 m.qk[part, hg, :, ds(b * CHUNK, CHUNK)].rearrange("(h p) n -> p h n", p=DK)).then_inc(q_loaded[par], 16)

            for hg in range(HG):
                load_queries(hg, 0, 0)
                for h in range(FOUR):
                    for r, part in enumerate((0, 0, 1)):
                        sp.dma_start(kst[r * DK:(r + 1) * DK, h, :].bitcast(F32),
                                     m.qk[part, HG + hg, h * DK:(h + 1) * DK, :]).then_inc(k_loaded[h], 16)
                with sp.Fori(0, NCH // 2) as i:
                    load_queries(hg, i * 2 + 1, 1)
                    load_queries(hg, i * 2 + 2, 0)

        def sum_tiles(eng, hg, b, par, k, tiles, total, added):
            g = b + hg * NCH
            n = tiles.index(k)
            if n == 0:
                return
            eng.wait_ge(exped, g * NT + (k + 3))
            if n == 1:
                eng.wait_ge(summed, g + 1)
                eng.tensor_tensor(total[:, par], probs[:, slot(par, tiles[0])], probs[:, slot(par, k)], ALU.add)\
                   .then_inc(added, 2)
            else:
                eng.wait_ge(added, g * len(tiles) + (n + RING))
                eng.tensor_tensor(total[:, par], total[:, par], probs[:, slot(par, k)], ALU.add).then_inc(added, 1)

        @block.gpsimd
        def _(pool):
            pool.memset(kst[STACK:STACK + 1].bitcast(F32), 1.0).then_inc(ones_row, 1)
            pool.sem_inc(pool_added, RING)

            def one(hg, b, par, has_next):
                if isinstance(b, int) and b < 0:
                    return
                for k in POOL_TILES:
                    sum_tiles(pool, hg, b, par, k, POOL_TILES, pool_sum, pool_added)

            blocks(pool, one)

        @block.tensor
        def _(pe):
            pe.sem_inc(scored, 2 * NT)
            pe.sem_inc(used, RING)
            pe.sem_inc(summed, 2)

            def use_x(hg, b, par, kind, c, u):
                if kind == "max":
                    h, qt, kc = c // (QT * KC), c // KC % QT, c % KC
                    n = min(KEYS, NP - kc * KEYS)
                    if isinstance(b, int) and b < 0 and qt == 0 and kc == 0:
                        pe.wait_ge(k_loaded[h], (hg + 1) * 48)
                    pe.wait_ge(x_free, u + 1)
                    pe.matmul(ps_x[:, c % 2, 0:n], qst[0:STACK, 1 - par, h, qt * P:(qt + 1) * P],
                              kst[0:STACK, h, kc * KEYS:kc * KEYS + n], start=True, stop=True).then_inc(x_made, 1)
                elif kind == "row":
                    if c == 0:
                        pe.wait_ge(max_made, b + (hg * NCH + 2))
                    pe.wait_ge(x_free, u + 1)
                    for hh in range(2):
                        for qt in range(QT):
                            col = (c * 2 + hh) * QT + qt
                            last = pe.matmul(ps_x[STACK:STACK + 1, c, hh * CHUNK + qt * P:hh * CHUNK + (qt + 1) * P],
                                             maxima[:, col:col + 1], m.ident_b[:], start=True, stop=True)
                    last.then_inc(x_made, 1)
                else:
                    if c == 0:
                        pe.wait_ge(context, (b + hg * NCH) * 2)
                    pe.wait_ge(x_free, u + 1)
                    pe.matmul(ps_x[:, c, 0:D], cx[:, c * P:(c + 1) * P], wo[:, hg, :], start=True, stop=True).then_inc(x_made, 1)

            def scores(hg, b, par, k, between):
                g = b + hg * NCH
                pe.wait_ge(exped, g * NT + (k + 1))
                if k == 0:
                    pe.wait_ge(rows_made, g + 1)
                for h in range(FOUR):
                    last = pe.matmul(ps_s[:, k % 2, h, :], kst[:, h, k * P:(k + 1) * P], qst[:, par, h, :],
                                     start=True, stop=True)
                    if h == 1:
                        between()
                last.then_inc(scored, 1)

            def sums(par, source, rows, stop):
                for h in range(FOUR):
                    last = pe.matmul(ps_oz[h * DK:(h + 1) * DK, par, 1, :], m.ones[0:rows, 0:DK],
                                     source[0:rows, h, :], start=False, stop=stop, skip_group_check=True)
                return last

            direct = [k for k in range(NT) if k not in POOL_TILES and k not in DVE_TILES]

            def values(hg, b, par, k):
                g = b + hg * NCH
                pe.wait_ge(exped, g * NT + (k + 3))
                rows = LAST if k == NT - 1 else P
                for h in range(FOUR):
                    lanes = slice(h * DK, (h + 1) * DK)
                    last = pe.matmul(ps_oz[lanes, par, 0, :], m.xhat[0:rows, k, (hg * FOUR + h) * DK:(hg * FOUR + h + 1) * DK],
                                     probs[0:rows, slot(par, k), h, :], start=k == 0, stop=k == NT - 1,
                                     skip_group_check=True)
                if k in direct:
                    last = sums(par, probs[:, slot(par, k)], rows, False)
                last.then_inc(used, 1)

            def one(hg, b, par, has_next):
                first = isinstance(b, int) and b < 0
                todo = [(kind, c, uses_before(hg, b) + n) for n, (kind, c) in enumerate(uses(b, has_next))]
                if first and hg == 0:
                    pe.wait_ge(ones_row, 1)
                    pe.wait_ge(wo_loaded, 16)
                if has_next:
                    if first:
                        pe.wait_ge(q_loaded[0], 48 * (hg * (NCH // 2 + 1) + 1))
                    elif par == 0:
                        pe.wait_ge(q_loaded[1], b * 24 + 48 * (hg * (NCH // 2) + 1))
                    else:
                        pe.wait_ge(q_loaded[0], b * 24 + (24 + 48 * (hg * (NCH // 2 + 1) + 1)))
                if first:
                    for kind, c, u in todo:
                        use_x(hg, b, par, kind, c, u)
                    return
                g = b + hg * NCH
                done = [0]

                def use_up_to(n):
                    n = min(n, len(todo) - 2) if has_next and n < len(todo) else min(n, len(todo))
                    while done[0] < n:
                        use_x(hg, b, par, *todo[done[0]])
                        done[0] += 1

                for k in range(NT):
                    goal = [len(todo) * (SPREAD * k + j + 1) // (SPREAD * (NT - 2)) for j in range(SPREAD)]
                    scores(hg, b, par, k, lambda: use_up_to(goal[0]))
                    use_up_to(goal[1])
                    if k:
                        values(hg, b, par, k - 1)
                    use_up_to(goal[2])
                values(hg, b, par, NT - 1)
                pe.wait_ge(dve_added, g * len(DVE_TILES) + (len(DVE_TILES) + RING))
                sums(par, dve_sum[:, par], P, False)
                pe.wait_ge(pool_added, g * len(POOL_TILES) + (len(POOL_TILES) + RING))
                sums(par, pool_sum[:, par], P, True).then_inc(summed, 1)
                if not has_next:
                    for n in range(QT):
                        use_x(hg, b + 1, par, "out", n, (hg + 1) * PER_HG - QT + n)

            blocks(pe, one)

        @block.scalar
        def _(act):
            act.sem_inc(exped, 2)

            def one(hg, b, par, has_next):
                if isinstance(b, int) and b < 0:
                    if hg:
                        act.wait_ge(used, hg * NCH * NT + RING)
                        act.wait_ge(pool_added, hg * NCH * len(POOL_TILES) + RING)
                        act.wait_ge(dve_added, hg * NCH * len(DVE_TILES) + RING)
                    return
                g = b + hg * NCH
                for k in range(NT):
                    act.wait_ge(scored, g * NT + (k + 1 + 2 * NT))
                    act.wait_ge(used, g * NT + (k + 1))
                    act.wait_ge(pool_added, g * len(POOL_TILES) + (up_to(POOL_TILES, k - RING) + RING))
                    act.wait_ge(dve_added, g * len(DVE_TILES) + (up_to(DVE_TILES, k - RING) + RING))
                    act.activation(probs[:, slot(par, k)], ps_s[:, k % 2], ACT.Exp, scale=scale).then_inc(exped, 1)

            blocks(act, one)

        @block.vector
        def _(dve):
            dve.sem_inc(x_free, 2)
            dve.sem_inc(dve_added, RING)

            def divide(hg, b, par):
                g = b + hg * NCH
                dve.wait_ge(summed, g + 3)
                dve.reciprocal(rden[:], ps_oz[:, par, 1, :]).then_inc(context, 1)
                dve.wait_ge(context, g * 2 + 1)
                dve.tensor_tensor(cx[:], ps_oz[:, par, 0, :], rden[:], ALU.mult).then_inc(context, 1)

            def read_x(hg, b, par, kind, c, u):
                dve.wait_ge(x_made, u + 1)
                if kind == "max":
                    kc = c % KC
                    dve.tensor_reduce(part_max[:, c // KC, kc:kc + 1], ps_x[:, c % 2, 0:min(KEYS, TOKENS - kc * KEYS)],
                                      AX.X, ALU.max).then_inc(x_free, 1)
                    if c == N_MAX - 1:
                        dve.wait_ge(x_free, u + 3)
                        dve.tensor_reduce(maxima[:], part_max[:], AX.X, ALU.max).then_inc(max_made, 1)
                elif kind == "row":
                    dve.tensor_scalar(qst[STACK:STACK + 1, 1 - par, c * 2:c * 2 + 2, :].rearrange("p h n -> p (h n)"),
                                      ps_x[STACK:STACK + 1, c, :], -1.0, None, ALU.mult).then_inc(x_free, 1)
                    if c == 1:
                        dve.wait_ge(x_free, u + 3)
                        dve.sem_inc(rows_made, 1)
                else:
                    xs = m.x[:, ds(b * QT + (c - QT), 1), :].rearrange("p a d -> p (a d)")
                    dve.tensor_tensor(xs, ps_x[:, c, 0:D], xs, ALU.add).then_inc(x_free, 1)

            def one(hg, b, par, has_next):
                first = isinstance(b, int) and b < 0
                todo = [(kind, c, uses_before(hg, b) + n) for n, (kind, c) in enumerate(uses(b, has_next))]
                if not first and not (isinstance(b, int) and b == 0):
                    divide(hg, b - 1, 1 - par)
                at = {}
                for n, k in enumerate(DVE_TILES):
                    at.setdefault(min(len(todo), len(todo) * (k + 2) // (NT - 2)), []).append(k)
                for n in range(len(todo) + 1):
                    if not first:
                        for k in at.get(n, []):
                            sum_tiles(dve, hg, b, par, k, DVE_TILES, dve_sum, dve_added)
                    if n < len(todo):
                        read_x(hg, b, par, *todo[n])
                if not has_next:
                    divide(hg, b, par)
                    for n in range(QT):
                        read_x(hg, b + 1, par, "out", n, (hg + 1) * PER_HG - QT + n)

            blocks(dve, one)
            dve.wait_ge(x_free, HG * PER_HG + 2)


def attention(nc, m, t, s):
    keep_x(nc, m, s)
    normalise(nc, m, s, m.x, m.x)
    normalise(nc, m, s, m.x, m.xhat)
    project(nc, m, t, s)
    add_rows(nc, m, s, 5)
    attend(nc, m, t, s)


def second_mixture(nc, m, t, s):
    normalise(nc, m, s, m.x, m.xhat)
    scaled, loaded = s("ln2_scaled"), s("x_back")
    with nc.sbuf_tensor(named("x_back"), [P, NT, D], F32) as back, nc.Block() as block:

        @block.sync
        def _(sp):
            sp.dma_start(back[:].rearrange("p t d -> p (t d)"), m.x_kept).then_inc(loaded, 16)

        @block.vector
        def _(dve):
            dve.tensor_tensor(m.xhat[:], m.xhat[:], m.rows[:, 2:3, :].broadcast_to([P, NT, D]), ALU.mult).then_inc(scaled, 1)
            dve.wait_ge(scaled, 1)
            dve.tensor_tensor(m.xhat[:], m.xhat[:], m.rows[:, 3:4, :].broadcast_to([P, NT, D]), ALU.add).then_inc(scaled, 1)
            dve.wait_ge(loaded, 16)
            dve.tensor_tensor(m.x[:], m.x[:], back[:], ALU.add).then_inc(scaled, 1)
            dve.wait_ge(scaled, 3)

    mixture(nc, m, t, s, 1, m.xhat, m.router, m.bias8[:, 1, :], CAPACITY, MOE1_CHUNKS, m.slots1, m.results1, m.x)


class Memory:

    def __init__(self, nc, ctx):
        def sb(name, shape, dt=F32):
            return ctx.enter_context(nc.sbuf_tensor("k_" + name, shape, dt))

        def dram(name, shape):
            return nc.dram_tensor(name, shape, F32).ap()

        self.x, self.xhat = sb("x", [P, NT, D]), sb("xhat", [P, NT, D])
        self.ident, self.ident_b = sb("ident", [P, P]), sb("ident_b", [P, P], BF16)
        self.ones, self.before = sb("ones", [P, P]), sb("before", [P, P])
        self.real, self.token, self.token_f = sb("real", [P, NT]), sb("token", [P, NT], I32), sb("token_f", [P, NT])
        self.iota, self.falling = sb("iota", [P, 64]), sb("falling", [P, EXPERTS])
        self.multiples = sb("multiples", [P, NCH])
        self.deg, self.dis0, self.dis1 = sb("deg", [P, NT]), sb("dis0", [P, NT]), sb("dis1", [P, NT])
        self.wg0, self.wg1 = sb("wg0", [P, KT, D]), sb("wg1", [P, KT, D])
        self.gate, self.router = sb("gate", [P, KT, EXPERTS]), sb("router", [P, KT, EXPERTS])
        self.rows, self.cols = sb("rows", [P, N_ROWS, D]), sb("cols", [P, N_COLS])
        self.bias8, self.logits = sb("bias8", [P, 2, EXPERTS]), sb("logits", [P, NT, EXPERTS])
        self.owner = sb("owner", [P, 64], I32)
        self.slots0 = dram("slots0", [MOE0_CHUNKS * CHUNK + TOP_K * NP, D])
        self.slots1 = dram("slots1", [MOE1_CHUNKS * CHUNK + NP, D])
        self.results0, self.results1 = dram("results0", [MOE0_CHUNKS * CHUNK, D]), dram("results1", [MOE1_CHUNKS * CHUNK, D])
        self.x_kept, self.qk = dram("x_kept", [P, NT * D]), dram("qk_parts", [2, 2 * HG, P, NP])


def program(nc, t, out, phases="gnn0 moe0 gnn1 att moe1"):
    NAMES.clear()
    with ExitStack() as ctx:
        used = [0]

        def stage():
            stack = ExitStack()

            def sem(name):
                used[0] += 1
                return stack.enter_context(nc.semaphore(f"{name}_{used[0]}"))

            return stack, sem

        m = Memory(nc, ctx)
        stack, s = stage()
        with stack:
            constants(nc, m, t, s)
        stack, s = stage()
        with stack:
            inverse_roots(nc, m, s)
        if "gnn0" in phases:
            stack, s = stage()
            with stack:
                normalise(nc, m, s, m.x, m.xhat)
                graph_layer(nc, m, t, s, m.wg0, m.dis0, m.rows[:, 0, :], False)
        if "moe0" in phases:
            stack, s = stage()
            with stack:
                normalise(nc, m, s, m.x, m.xhat)
                mixture(nc, m, t, s, 0, m.xhat, m.gate, m.bias8[:, 0, :], None, MOE0_CHUNKS, m.slots0, m.results0, m.x)
        if "gnn1" in phases:
            stack, s = stage()
            with stack:
                normalise(nc, m, s, m.x, m.xhat)
                graph_layer(nc, m, t, s, m.wg1, m.dis1, m.rows[:, 1, :], True)
        if "att" in phases:
            stack, s = stage()
            with stack:
                attention(nc, m, t, s)
        if "moe1" in phases:
            stack, s = stage()
            with stack:
                second_mixture(nc, m, t, s)
        stack, s = stage()
        with stack:
            put = s("out_stored")
            with nc.Block() as block:

                @block.sync
                def _(sp):
                    sp.dma_start(out, m.x[:]).then_inc(put, 16)
                    sp.wait_ge(put, 16)




def host_layout(inputs):
    g = {k: np.asarray(v) for k, v in inputs.items()}
    x = np.zeros((NP, D), np.float32)
    x[:TOKENS] = g["x"]
    adj = np.zeros((NP, NP), np.float32)
    adj[:TOKENS, :TOKENS] = g["adj"]
    a = {"x": x.reshape(NT, P, D).transpose(1, 0, 2), "adj": adj,
         "adjT": adj.reshape(NCH, CHUNK, 2, HALF, P).transpose(0, 2, 4, 3, 1).reshape(NCH, 2, P, HALF * CHUNK)}

    def by_feature(w):
        return w.reshape(KT, P, -1).transpose(1, 0, 2)

    a["W0"], a["W1"] = by_feature(g["L0_gnn_W"].T), by_feature(g["L1_gnn_W"])
    a["gate"], a["router"] = by_feature(g["L0_ffn_gate_w"]), by_feature(g["L1_ffn_router_w"])
    for n in "qkvo":
        a["w" + n] = by_feature(g[f"L1_ffn_w{n}"])
    rows = ("L0_gnn_b", "L1_gnn_b", "L1_ffn_ln2_g", "L1_ffn_ln2_b", "L1_ffn_bv", "L1_ffn_bo")
    a["rows"] = np.broadcast_to(np.stack([g[n] for n in rows]), (P, N_ROWS, D))
    a["cols"] = np.concatenate([g[n].reshape(KT, P).T for n in ("L1_ffn_ln1_g", "L1_ffn_ln1_b", "L1_ffn_bq", "L1_ffn_bk")], 1)
    a["bias8"] = np.broadcast_to(np.stack([g["L0_ffn_gate_b"], g["L1_ffn_router_b"]]), (P, 2, EXPERTS))
    for n in (0, 1):
        f = f"L{n}_ffn_"
        a[f"w1_{n}"] = g[f + "w1"].reshape(EXPERTS, KT, P, HID).transpose(0, 2, 1, 3).reshape(EXPERTS, P, KT * HID)
        a[f"w2_{n}"] = g[f + "w2"].reshape(EXPERTS, HT, P, D).transpose(0, 2, 1, 3).reshape(EXPERTS, P, HT * D)
        a[f"b1_{n}"] = g[f + "b1"].reshape(EXPERTS, HT, P).transpose(0, 2, 1)
        a[f"b2_{n}"] = np.broadcast_to(g[f + "b2"][:, None], (EXPERTS, P, D))
    return {k: np.ascontiguousarray(v) for k, v in a.items()}


def kernel(**inputs):
    import concourse.bacc as bacc
    from concourse.bass_utils import run_bass_kernel_spmd

    nc = bacc.Bacc("TRN2", target_bir_lowering=False, num_devices=1)
    arrays = host_layout(inputs)
    t = {n: nc.dram_tensor(n, a.shape, F32, kind="ExternalInput").ap() for n, a in arrays.items()}
    out = nc.dram_tensor("out", (P, NT, D), F32, kind="ExternalOutput").ap()
    program(nc, t, out)
    r = run_bass_kernel_spmd(nc, [arrays], core_ids=[0])
    return r.results[0]["out"].transpose(1, 0, 2).reshape(NP, D)[:TOKENS]
```

```python
import numpy as np
from contextlib import ExitStack
import concourse.bass as bass
from concourse import mybir

F32 = mybir.dt.float32
F32R = mybir.dt.float32r
BF16 = mybir.dt.bfloat16
I32 = mybir.dt.int32
ALU = mybir.AluOpType
ACT = mybir.ActivationFunctionType
AX = mybir.AxisListType
ds = bass.ds

TOKENS, D, HID, EXPERTS, HEADS = 3327, 256, 1024, 8, 8
P = 128
DK = D // HEADS
NT = -(-TOKENS // P)
NP = NT * P
KT = D // P
HT = HID // P
LAST = TOKENS - (NT - 1) * P
CHUNK = 256
NCH = NP // CHUNK
HALF = NT // 2
TOP_K = 2
CAPACITY = int(np.ceil(TOKENS * 1.6 / EXPERTS))
HG = HEADS // 4
ZERO_COLS = 1024
LN_EPS, GNN_EPS = 1e-5, 1e-8
N_ROWS, N_COLS = 6, 8


def slot_chunks(assigned):
    most = (assigned + EXPERTS * (CHUNK - 1)) // CHUNK
    return most + most % 2


MOE0_CHUNKS = slot_chunks(TOP_K * TOKENS)
MOE1_CHUNKS = slot_chunks(TOKENS)


NAMES = []


def named(name):
    NAMES.append(name)
    return f"{name}_{len(NAMES)}"


class Count:

    def __init__(self, sem):
        self.sem, self.value = sem, 0

    def inc(self, ins):
        ins.then_inc(self.sem, 1)
        self.value += 1

    def settle(self, eng):
        eng.wait_ge(self.sem, self.value)


def constants(nc, m, t, s):
    made, loaded = s("made"), s("params_loaded")
    x_loaded = s("x_loaded")
    rows_loaded = [s("rows_loaded0"), s("rows_loaded1")]
    rows_summed = s("rows_summed")
    with nc.sbuf_tensor(named("adj_rows"), [P, 2, NP], F32) as adj_rows, \
            nc.sbuf_tensor(named("iota_i"), [P, 64], I32) as iota_i, \
            nc.Block() as block:

        @block.gpsimd
        def _(pool):
            c = Count(made)
            c.inc(pool.memset(m.ident[:], 0.0))
            c.inc(pool.memset(m.ident_b[:], 0.0))
            c.inc(pool.memset(m.ones[:], 1.0))
            c.settle(pool)
            c.inc(pool.affine_select(out=m.ident[:], in_=m.ident[:], compare_op=ALU.not_equal, fill=1.0, base=0,
                                     pattern=[[-1, P]], channel_multiplier=1))
            c.inc(pool.affine_select(out=m.ident_b[:], in_=m.ident_b[:], compare_op=ALU.not_equal, fill=1.0,
                                     base=0, pattern=[[-1, P]], channel_multiplier=1))
            c.inc(pool.affine_select(out=m.before[:], in_=m.ones[:], compare_op=ALU.is_gt, fill=0.0, base=0,
                                     pattern=[[1, P]], channel_multiplier=-1))
            c.inc(pool.affine_select(out=m.real[:], in_=m.ones[:, 0:NT], compare_op=ALU.is_gt, fill=0.0,
                                     base=TOKENS, pattern=[[-P, NT]], channel_multiplier=-1))
            c.inc(pool.iota(iota_i[:], [[1, 64]], base=0, channel_multiplier=0))
            c.inc(pool.iota(m.token[:], [[P, NT]], base=0, channel_multiplier=1))
            c.settle(pool)
            c.inc(pool.tensor_copy(m.iota[:], iota_i[:]))
            c.inc(pool.tensor_copy(m.token_f[:], m.token[:]))
            c.settle(pool)
            c.inc(pool.tensor_scalar(m.multiples[:], m.iota[:, 0:NCH], float(CHUNK), None, ALU.mult))
            c.settle(pool)

        @block.scalar
        def _(act):
            for dst, src in ((m.wg0, t["W0"]), (m.wg1, t["W1"]), (m.gate, t["gate"]), (m.router, t["router"]),
                             (m.rows, t["rows"]), (m.cols, t["cols"]), (m.bias8, t["bias8"])):
                act.dma_start(dst[:], src).then_inc(loaded, 16)
            act.wait_ge(loaded, 16 * 7)

        @block.sync
        def _(sp):
            sp.dma_start(m.x[:], t["x"]).then_inc(x_loaded, 16)
            with sp.Fori(0, NT // 2) as i:
                for k in range(2):
                    sp.wait_ge(rows_summed, i * 2 + k + 1)
                    sp.dma_start(adj_rows[:, k, :], t["adj"][ds(i * 2 * P + k * P, P), :]).then_inc(rows_loaded[k], 16)
            sp.wait_ge(x_loaded, 16)

        @block.vector
        def _(dve):
            dve.sem_inc(rows_summed, 2)
            with dve.Fori(0, NT // 2) as i:
                for k in range(2):
                    dve.wait_ge(rows_loaded[k], i * 16 + 16)
                    dve.tensor_reduce(m.deg[:, ds(i * 2 + k, 1)], adj_rows[:, k, :], AX.X, ALU.add)\
                       .then_inc(rows_summed, 1)
            dve.wait_ge(rows_summed, NT + 2)


def inverse_root(dve, c, rooted, n, r, w, tmp):
    dve.wait_ge(rooted, n)
    for ins in (lambda: dve.reciprocal(r, r),
                lambda: dve.tensor_tensor(tmp, r, r, ALU.mult),
                lambda: dve.tensor_tensor(tmp, tmp, w, ALU.mult),
                lambda: dve.tensor_scalar(tmp, tmp, -0.5, 1.5, ALU.mult, ALU.add),
                lambda: dve.tensor_tensor(r, r, tmp, ALU.mult)):
        c.inc(ins())
        c.settle(dve)


def inverse_roots(nc, m, s):
    guard, rooted = s("guarded"), s("rooted")
    with nc.sbuf_tensor(named("deg_tmp"), [P, 4, NT], F32) as tmp, nc.Block() as block:

        @block.vector
        def _(dve):
            c = Count(guard)
            c.inc(dve.tensor_scalar(tmp[:, 0, :], m.deg[:], GNN_EPS, None, ALU.add))
            c.inc(dve.tensor_scalar(tmp[:, 1, :], m.deg[:], 1e-34, None, ALU.max))
            c.inc(dve.tensor_scalar(tmp[:, 2, :], m.deg[:], 0.0, None, ALU.is_gt))
            inverse_root(dve, c, rooted, 1, m.dis0[:], tmp[:, 0, :], tmp[:, 3, :])
            inverse_root(dve, c, rooted, 2, m.dis1[:], tmp[:, 1, :], tmp[:, 3, :])
            c.inc(dve.tensor_tensor(m.dis1[:], m.dis1[:], tmp[:, 2, :], ALU.mult))
            c.settle(dve)

        @block.scalar
        def _(act):
            act.wait_ge(guard, 2)
            act.activation(m.dis0[:], tmp[:, 0, :], ACT.Sqrt).then_inc(rooted, 1)
            act.activation(m.dis1[:], tmp[:, 1, :], ACT.Sqrt).then_inc(rooted, 1)


def normalise(nc, m, s, src, dst, keep=None):
    stats, rooted, applied, kept = s("stats"), s("var_rooted"), s("applied"), s("src_kept")
    DVE_SHARE = NT * 3 // 5
    with nc.sbuf_tensor(named("bn_st"), [P, NT, 6], F32) as st, nc.sbuf_tensor(named("bn_mv"), [P, NT, 2], F32) as mv, \
            nc.sbuf_tensor(named("bn_rs"), [P, NT], F32) as rs, nc.sbuf_tensor(named("bn_nb"), [P, NT], F32) as nb, \
            nc.sbuf_tensor(named("bn_vr"), [P, NT], F32) as vr, \
            nc.Block() as block:

        @block.vector
        def _(dve):
            c = Count(stats)
            for k in range(NT):
                c.inc(dve.bn_stats(st[:, k, :], src[:, k, :]))
            c.settle(dve)
            for k in range(NT):
                c.inc(dve.bn_aggr(mv[:, k, :], st[:, k, :]))
            c.settle(dve)
            c.inc(dve.tensor_scalar(vr[:], mv[:, :, 1], LN_EPS, None, ALU.add))
            inverse_root(dve, c, rooted, 1, rs[:], vr[:], nb[:])
            dve.scalar_tensor_tensor(nb[:], mv[:, :, 0], -1.0, rs[:], ALU.mult, ALU.mult).then_inc(applied, 1)
            if keep is not None:
                dve.wait_ge(kept, 16)
            for k in range(DVE_SHARE):
                dve.tensor_scalar(dst[:, k, :], src[:, k, :], mv[:, k, 0:1], rs[:, k:k + 1], ALU.subtract, ALU.mult)
            dve.drain()

        @block.scalar
        def _(act):
            act.wait_ge(stats, 2 * NT + 1)
            act.activation(rs[:], vr[:], ACT.Sqrt).then_inc(rooted, 1)
            act.wait_ge(applied, 1)
            if keep is not None:
                act.wait_ge(kept, 16)
            for k in range(DVE_SHARE, NT):
                act.activation(dst[:, k, :], src[:, k, :], ACT.Identity, bias=nb[:, k:k + 1], scale=rs[:, k:k + 1])
            act.drain()

        if keep is not None:
            @block.sync
            def _(sp):
                sp.dma_start(keep, src[:].rearrange("p t d -> p (t d)")).then_inc(kept, 16)
                sp.wait_ge(kept, 16)


def transposed_products(nc, m, s, src, products, take_act, take_dve, n_psum, affine=None, tail_sp=None, on_pool=None):
    turned, copied, multiplied = s("turned"), s("copied"), s("multiplied")
    act_took, dve_took = s("act_took"), s("dve_took")
    with nc.sbuf_tensor(named("xt"), [P, 2, KT, P], F32) as xt, nc.psum_tensor(named("ps_turn"), [P, 2, 512], F32) as ps_turn, \
            nc.psum_tensor(named("ps_prod"), [P, 2, n_psum, 512], F32) as ps, nc.Block() as block:

        @block.tensor
        def _(pe):
            def turn(k):
                if k >= 2:
                    pe.wait_ge(copied, k - 1)
                for j in range(KT):
                    last = pe.transpose(ps_turn[:, k % 2, j * P:(j + 1) * P], src[:, k, j * P:(j + 1) * P], m.ident[:])
                last.then_inc(turned, 1)

            def multiply(k):
                pe.wait_ge(copied, k + 1)
                if k >= 2:
                    pe.wait_ge(act_took, k - 1)
                    pe.wait_ge(dve_took, k - 1)
                products(pe, xt[:, k % 2], ps[:, k % 2]).then_inc(multiplied, 1)

            turn(0)
            for k in range(NT):
                if k + 1 < NT:
                    turn(k + 1)
                multiply(k)

        @block.scalar
        def _(act):
            def copy(k):
                act.wait_ge(turned, k + 1)
                if k >= 2:
                    act.wait_ge(multiplied, k - 1)
                for j in range(KT):
                    if affine:
                        last = act.activation(xt[:, k % 2, j, :], ps_turn[:, k % 2, j * P:(j + 1) * P], ACT.Identity,
                                              bias=affine[1][:, j:j + 1], scale=affine[0][:, j:j + 1])
                if not affine:
                    last = act.activation(xt[:, k % 2].rearrange("p j n -> p (j n)"), ps_turn[:, k % 2, 0:D], ACT.Copy)
                last.then_inc(copied, 1)

            copy(0)
            for k in range(NT):
                if k + 1 < NT:
                    copy(k + 1)
                act.wait_ge(multiplied, k + 1)
                take_act(act, k, ps[:, k % 2], act_took)
            act.wait_ge(act_took, NT)

        @block.vector
        def _(dve):
            for k in range(NT):
                dve.wait_ge(multiplied, k + 1)
                take_dve(dve, k, ps[:, k % 2], act_took, dve_took)
            dve.wait_ge(dve_took, NT)

        if tail_sp:
            @block.sync
            def _(sp):
                tail_sp(sp, act_took, dve_took)

        if on_pool:
            @block.gpsimd
            def _(pool):
                on_pool(pool)


def graph_layer(nc, m, t, s, w, dis, bias, relu, slots, chunks):
    with nc.sbuf_tensor(named("y_hi"), [P, NT, D], F32R) as y_hi, nc.sbuf_tensor(named("y_lo"), [P, NT, D], F32R) as y_lo:

        def products(pe, xt, ps):
            for j in range(KT):
                last = pe.matmul(ps[:, 0, 0:D], xt[:, j, :], w[:, j, :], start=j == 0, stop=j == KT - 1)
            return last

        def take_act(act, k, ps, took):
            act.activation(y_hi[:, k, :], ps[:, 0, 0:D], ACT.Copy, scale=dis[:, k:k + 1]).then_inc(took, 1)

        def take_dve(dve, k, ps, act_took, took):
            dve.wait_ge(act_took, k + 1)
            dve.scalar_tensor_tensor(y_lo[:, k, :], ps[:, 0, 0:D], dis[:, k:k + 1], y_hi[:, k, :].bitcast(F32),
                                     ALU.mult, ALU.subtract).then_inc(took, 1)

        transposed_products(nc, m, s, m.xhat, products, take_act, take_dve, 1)

        loaded = [s("adj_loaded0"), s("adj_loaded1")]
        hi_made, lo_made, used = s("hi_made"), s("lo_made"), s("halves_used")
        summed, taken, chain = s("chunk_summed"), s("chunk_taken"), s("taking")
        zero_made, cleared = s("zero_made"), s("slots_cleared")
        with nc.sbuf_tensor(named("adj_raw"), [P, 2, HALF * CHUNK], F32) as raw, \
                nc.sbuf_tensor(named("adj_hi"), [P, 2, HALF, CHUNK], F32R) as hi, \
                nc.sbuf_tensor(named("adj_lo"), [P, 2, HALF, CHUNK], F32R) as lo, \
                nc.sbuf_tensor(named("gnn_tmp"), [P, 2, D], F32) as tmp, \
                nc.sbuf_tensor(named("zeros"), [P, ZERO_COLS], F32) as zeros, \
                nc.psum_tensor(named("ps_gnn"), [P, 2, 512], F32) as ps, nc.Block() as block:

            @block.gpsimd
            def _(pool):
                pool.memset(zeros[:], 0.0).then_inc(zero_made, 1)
                pool.wait_ge(zero_made, 1)
                cols = chunks * CHUNK // P * D
                view = slots[0:chunks * CHUNK, :].rearrange("(p n) d -> p (n d)", p=P)
                starts = range(0, cols, ZERO_COLS)
                for n in starts:
                    w = min(ZERO_COLS, cols - n)
                    pool.dma_start(view[:, n:n + w], zeros[:, 0:w]).then_inc(cleared, 16)
                pool.wait_ge(cleared, 16 * len(starts))

            @block.sync
            def _(sp):
                with sp.Fori(0, NCH) as c:
                    for k in range(2):
                        sp.wait_ge(lo_made, c * 2 + k + 1)
                        sp.dma_start(raw[:, k, :], t["adjT"][ds(c, 1), k].rearrange("a p n -> p (a n)")).then_inc(loaded[k], 16)

            @block.scalar
            def _(act):
                def split_hi(c, k):
                    act.wait_ge(loaded[k], c * 16 + 16)
                    if k == 0:
                        act.wait_ge(used, c + 1)
                    else:
                        act.wait_ge(summed, c * 2 + 2)
                    act.activation(hi[:, k].rearrange("p j n -> p (j n)"), raw[:, k, :], ACT.Copy).then_inc(hi_made, 1)

                with act.Fori(0, NCH) as c:
                    for k in range(2):
                        split_hi(c, k)
                act.wait_ge(hi_made, 2 * NCH)

            @block.tensor
            def _(pe):
                pe.sem_inc(used, 1)
                pe.sem_inc(summed, 2)
                with pe.Fori(0, NCH) as c:
                    for k in range(2):
                        pe.wait_ge(hi_made, c * 2 + k + 1)
                        pe.wait_ge(lo_made, c * 2 + k + 3)
                        for i in range(2):
                            if k == 0:
                                pe.wait_ge(taken, c * 2 + i + 1)
                            for j in range(HALF):
                                rows = slice(i * P, (i + 1) * P)
                                n = k * HALF + j
                                out = ps[:, i, 0:D]
                                pe.matmul(out, hi[:, k, j, rows], y_hi[:, n, :], start=n == 0, stop=False)
                                pe.matmul(out, hi[:, k, j, rows], y_lo[:, n, :], start=False, stop=False)
                                last = pe.matmul(out, lo[:, k, j, rows], y_hi[:, n, :], start=False, stop=n == NT - 1)
                            if k == 1:
                                last.then_inc(summed, 1)
                        if k == 0:
                            last.then_inc(used, 1)

            @block.vector
            def _(dve):
                dve.sem_inc(lo_made, 2)
                dve.sem_inc(taken, 2)

                def split_lo(c, k):
                    dve.wait_ge(hi_made, c * 2 + k + 1)
                    dve.tensor_tensor(lo[:, k].rearrange("p j n -> p (j n)"), raw[:, k, :],
                                      hi[:, k].rearrange("p j n -> p (j n)").bitcast(F32), ALU.subtract).then_inc(lo_made, 1)

                def take(c):
                    for i in range(2):
                        xs = m.x[:, ds(c * 2 + i, 1), :].rearrange("p a d -> p (a d)")
                        dve.wait_ge(summed, c * 2 + i + 3)
                        dve.scalar_tensor_tensor(tmp[:, i, :], ps[:, i, 0:D], dis[:, ds(c * 2 + i, 1)], bias,
                                                 ALU.mult, ALU.add).then_inc(taken, 1)
                        dve.wait_ge(taken, c * 2 + i + 3)
                        if relu:
                            dve.scalar_tensor_tensor(xs, tmp[:, i, :], 0.0, xs, ALU.max, ALU.add).then_inc(chain, 1)
                        else:
                            dve.tensor_tensor(xs, tmp[:, i, :], xs, ALU.add).then_inc(chain, 1)
                        dve.wait_ge(chain, c * 2 + i + 1)

                split_lo(0, 0)
                split_lo(0, 1)
                with dve.Fori(0, NCH - 1) as c:
                    split_lo(c + 1, 0)
                    take(c)
                    split_lo(c + 1, 1)
                take(NCH - 1)


def mixture_routes(nc, m, s, bias, top, capacity, chunks, slot_sets, weights):
    c_act, c_dve, c_pe = s("route_exp"), s("route_dve"), s("route_sums")
    with ExitStack() as ctx:
        def sb(name, shape, dt=F32):
            return ctx.enter_context(nc.sbuf_tensor(named("rt_" + name), shape, dt))

        hots = [sb(f"choice{k}", [P, NT, EXPERTS]) for k in range(top)]
        prob, key, mask = sb("prob", [P, NT, EXPERTS]), sb("key", [P, NT, EXPERTS]), sb("mask", [P, NT, EXPERTS])
        rank, best, total = sb("rank", [P, NT, EXPERTS]), sb("best", [P, NT]), sb("total", [P, NT])
        carry = sb("carry", [P, NT + 1, EXPERTS])
        steps, full = sb("steps", [P, EXPERTS, NCH]), sb("full", [P, EXPERTS])
        ends, base = sb("ends", [P, EXPERTS + 1]), sb("base", [P, EXPERTS])
        fine = sb("fine", [P, NT])
        mask_at = []
        owner, owner_f = sb("owner", [P, chunks, EXPERTS]), sb("owner_f", [P, chunks])
        ps = ctx.enter_context(nc.psum_tensor(named("ps_rank"), [P, 2, 512], F32))
        block = ctx.enter_context(nc.Block())
        W = NT * EXPERTS
        rounds = 1 if capacity is None else 2

        def over_experts(a):
            return a.rearrange("p (t a) -> p t a", a=1).broadcast_to([P, NT, EXPERTS])

        def by_expert(a):
            return a.rearrange("p (a e) -> p a e", a=1).broadcast_to([P, NT, EXPERTS])

        @block.vector
        def _(dve):
            c = Count(c_dve)

            def do(ins):
                c.inc(ins)
                c.settle(dve)

            up = m.iota[:, 1:EXPERTS + 1]

            do(dve.tensor_tensor(mask[:], m.logits[:], by_expert(bias), ALU.add))
            do(dve.tensor_reduce(best[:], mask[:], AX.X, ALU.max))
            do(dve.tensor_tensor(key[:], mask[:], over_experts(best[:]), ALU.subtract))
            dve.wait_ge(c_act, 1)
            do(dve.tensor_reduce(total[:], prob[:], AX.X, ALU.add))
            do(dve.reciprocal(total[:], total[:]))
            do(dve.tensor_tensor(prob[:], prob[:], over_experts(total[:]), ALU.mult))

            def first_of(values, hot):
                do(dve.tensor_reduce(best[:], values[:], AX.X, ALU.max))
                do(dve.tensor_tensor(key[:], values[:], over_experts(best[:]), ALU.is_equal))
                do(dve.tensor_tensor(key[:], key[:], by_expert(m.falling[:]), ALU.mult))
                do(dve.tensor_reduce(total[:], key[:], AX.X, ALU.max))
                do(dve.tensor_tensor(hot[:], key[:], over_experts(total[:]), ALU.is_equal))

            do(dve.tensor_scalar(m.falling[:], m.iota[:, 0:EXPERTS], -1.0, float(EXPERTS), ALU.mult, ALU.add))
            for k in range(top):
                first_of(prob, hots[k])
                if capacity is None:
                    do(dve.tensor_copy(weights[k][:], best[:]))
                if k + 1 < top:
                    do(dve.scalar_tensor_tensor(prob[:], hots[k][:], -4.0, prob[:], ALU.mult, ALU.add))

            def ranks():
                mask_at.append(c.value)
                dve.wait_ge(c_pe, len(mask_at))
                do(dve.memset(carry[:, 0, :], 0.0))
                for k in range(NT):
                    do(dve.tensor_tensor(carry[:, k + 1, :], carry[:, k, :],
                                         ps[:, 1, k * EXPERTS:(k + 1) * EXPERTS], ALU.add))
                do(dve.tensor_tensor(rank[:], carry[:, 0:NT, :],
                                     ps[:, 0, 0:W].rearrange("p (t e) -> p t e", e=EXPERTS), ALU.add))

            do(dve.tensor_tensor(mask[:], hots[0][:], hots[1][:], ALU.add))
            do(dve.tensor_tensor(mask[:], mask[:], over_experts(m.real[:]), ALU.mult))
            ranks()
            if capacity is not None:
                do(dve.scalar_tensor_tensor(key[:], rank[:], float(capacity), mask[:], ALU.is_lt, ALU.mult))
                do(dve.tensor_tensor(key[:], key[:], by_expert(up), ALU.mult))
                do(dve.tensor_reduce(best[:], key[:], AX.X, ALU.max))
                do(dve.tensor_scalar(weights[0][:], best[:], 0.0, None, ALU.is_gt))
                do(dve.tensor_tensor(mask[:], key[:], over_experts(best[:]), ALU.is_equal))
                do(dve.tensor_tensor(mask[:], mask[:], over_experts(weights[0][:]), ALU.mult))
                ranks()
                rows_of, ok = [mask], weights[0]
            else:
                rows_of, ok = hots, m.real
            do(dve.tensor_tensor(steps[:], carry[:, NT, :].rearrange("p (e a) -> p e a", a=1).broadcast_to([P, EXPERTS, NCH]),
                                 m.multiples[:].rearrange("p (a n) -> p a n", a=1).broadcast_to([P, EXPERTS, NCH]), ALU.is_gt))
            do(dve.tensor_reduce(full[:], steps[:], AX.X, ALU.add))
            do(dve.memset(ends[:, 0:1], 0.0))
            for e in range(EXPERTS):
                do(dve.tensor_tensor(ends[:, e + 1:e + 2], ends[:, e:e + 1], full[:, e:e + 1], ALU.add))
            do(dve.tensor_tensor(owner[:], ends[:, 1:].rearrange("p (a e) -> p a e", a=1).broadcast_to([P, chunks, EXPERTS]),
                                 m.iota[:, 0:chunks].rearrange("p (n a) -> p n a", a=1).broadcast_to([P, chunks, EXPERTS]), ALU.is_le))
            do(dve.tensor_reduce(owner_f[:], owner[:], AX.X, ALU.add))
            do(dve.tensor_scalar(m.owner[:, 0:chunks], owner_f[:], float(EXPERTS - 1), None, ALU.min))
            do(dve.tensor_scalar(base[:], ends[:, 0:EXPERTS], float(CHUNK), None, ALU.mult))
            do(dve.tensor_tensor(rank[:], rank[:], by_expert(base[:]), ALU.add))
            do(dve.tensor_scalar(fine[:], ok[:], -1.0, 1.0, ALU.mult, ALU.add))
            for n, (hot, (put, get)) in enumerate(zip(rows_of, slot_sets)):
                do(dve.tensor_tensor(key[:], hot[:], rank[:], ALU.mult))
                do(dve.tensor_reduce(best[:], key[:], AX.X, ALU.add))
                do(dve.scalar_tensor_tensor(total[:], m.token_f[:], float(chunks * CHUNK + n * NP), best[:],
                                            ALU.add, ALU.subtract))
                do(dve.tensor_tensor(total[:], total[:], fine[:], ALU.mult))
                do(dve.tensor_tensor(put[:], total[:], best[:], ALU.add))
                do(dve.tensor_scalar(get[:], best[:], float(chunks * CHUNK - 1), None, ALU.min))

        @block.scalar
        def _(act):
            act.wait_ge(c_dve, 3)
            act.activation(prob[:], key[:], ACT.Exp).then_inc(c_act, 1)

        @block.tensor
        def _(pe):
            for r in range(rounds):
                pe.wait_ge(c_dve, mask_at[r])
                flat = mask[:].rearrange("p t e -> p (t e)")
                pe.matmul(ps[:, 0, 0:W], m.before[:], flat, start=True, stop=True)
                pe.matmul(ps[:, 1, 0:W], m.ones[:], flat, start=True, stop=True).then_inc(c_pe, 1)



def mixture_scatter(nc, m, s, rows, slots, puts):
    sent = s("rows_sent")
    with nc.Block() as block:

        @block.gpsimd
        def _(pool):
            for put in puts:
                for k in range(NT):
                    pool.indirect_dma_start(out=slots, out_offset=bass.IndirectOffsetOnAxis(put[:, k:k + 1], 0),
                                            in_=rows[:, k, :], in_offset=None).then_inc(sent, 16)
            pool.wait_ge(sent, 16 * NT * len(puts))


def expert_layers(nc, m, t, s, layer, chunks, slots, results):
    loaded = [s("expert_loaded0"), s("expert_loaded1")]
    bias_loaded = [s("bias_loaded0"), s("bias_loaded1")]
    turned, rows_hi, rows_lo = s("ex_turned"), s("ex_rows_hi"), s("ex_rows_lo")
    weights_hi, weights_lo = s("ex_weights_hi"), s("ex_weights_lo")
    hidden_ps, gelu_made, hidden_hi, hidden_lo = s("ex_hidden_ps"), s("ex_gelu"), s("ex_hidden_hi"), s("ex_hidden_lo")
    out_ps, out_made = s("ex_out_ps"), s("ex_out_made")
    stored, res_free = [s("ex_stored0"), s("ex_stored1")], s("ex_res_free")
    w1_d, w2_d, b1_d, b2_d = (t[f"{n}_{layer}"] for n in ("w1", "w2", "b1", "b2"))
    TT = CHUNK // P
    W = KT * HID
    PAIRS = HT // 2
    with ExitStack() as ctx:
        def sb(name, shape, dt=F32):
            return ctx.enter_context(nc.sbuf_tensor(named("ex_" + name), shape, dt))

        w, w_hi, w_lo = sb("w", [P, 2, 2, W]), sb("w_hi", [P, 2, 2, W], F32R), sb("w_lo", [P, 2, 2, W], F32R)
        b1, b2 = sb("b1", [P, 2, HT]), sb("b2", [P, 2, D])
        rows = sb("rows", [P, 2, TT, D])
        rt_hi, rt_lo = sb("rt_hi", [P, KT, CHUNK], F32R), sb("rt_lo", [P, KT, CHUNK], F32R)
        hid, hid_hi, hid_lo = sb("hid", [P, HT, CHUNK]), sb("hid_hi", [P, HT, CHUNK], F32R), sb("hid_lo", [P, HT, CHUNK], F32R)
        res = sb("res", [P, 2, TT, D])
        ps_t = ctx.enter_context(nc.psum_tensor(named("ps_ex_t"), [P, KT, 512], F32))
        ps_h = ctx.enter_context(nc.psum_tensor(named("ps_ex_h"), [P, 4, 512], F32))
        ps_o = ctx.enter_context(nc.psum_tensor(named("ps_ex_o"), [P, TT, 512], F32))
        block = ctx.enter_context(nc.Block())

        def each_chunk(eng, one):
            with eng.Fori(0, chunks // 2 - 1) as i:
                one(i * 2, 0, True)
                one(i * 2 + 1, 1, True)
            one(chunks - 2, 0, True)
            one(chunks - 1, 1, False)

        @block.sync
        def _(sp):
            with sp.Fori(0, chunks // 2) as i:
                for k in range(2):
                    n = i * 2 + k
                    sp.wait_ge(weights_lo, n * 2 + 2)
                    e = sp.value_load(m.owner[0:1, ds(n, 1)], min_val=0, max_val=EXPERTS - 1)
                    sp.dma_start(rows[:, k], slots[ds(i * 2 * CHUNK + k * CHUNK, CHUNK), :].rearrange("(a p) d -> p a d", p=P)).then_inc(loaded[k], 16)
                    for dst, src in ((w[:, k, 0, :], w1_d), (w[:, k, 1, :], w2_d)):
                        sp.dma_start(dst, src[ds(e, 1)].rearrange("a p n -> (a p) n")).then_inc(loaded[k], 16)
                    sp.wait_ge(out_made, n + 1)
                    for dst, src in ((b1[:, k, :], b1_d), (b2[:, k, :], b2_d)):
                        sp.dma_start(dst, src[ds(e, 1)].rearrange("a p n -> (a p) n")).then_inc(bias_loaded[k], 16)

        def arrived(eng, n, k):
            eng.wait_ge(loaded[k], n * 24 + (48 - 24 * k))

        @block.tensor
        def _(pe):
            def turn(n, k):
                arrived(pe, n, k)
                for a in range(TT):
                    for j in range(KT):
                        last = pe.transpose(ps_t[:, j, a * P:(a + 1) * P], rows[:, k, a, j * P:(j + 1) * P], m.ident[:])
                last.then_inc(turned, 1)

            def three(out, hi, lo, by_hi, by_lo, start, stop):
                pe.matmul(out, hi, by_hi, start=start, stop=False)
                pe.matmul(out, hi, by_lo, start=False, stop=False)
                return pe.matmul(out, lo, by_hi, start=False, stop=stop)

            turn(0, 0)

            def one(n, k, has_next):
                pe.wait_ge(rows_lo, n + 1)
                pe.wait_ge(weights_lo, n * 2 + 5)
                for h in range(HT):
                    pe.wait_ge(gelu_made, n * HT + (h + 1))
                    for j in range(KT):
                        at = slice(j * HID + h * P, j * HID + (h + 1) * P)
                        last = three(ps_h[:, h % 4, 0:CHUNK], w_hi[:, k, 0, at], w_lo[:, k, 0, at],
                                     rt_hi[:, j, :], rt_lo[:, j, :], j == 0, j == KT - 1)
                    last.then_inc(hidden_ps, 1)
                if has_next:
                    turn(n + 1, 1 - k)
                pe.wait_ge(out_made, n + 2)
                pe.wait_ge(hidden_lo, n * PAIRS + 2 * PAIRS)
                pe.wait_ge(weights_lo, n * 2 + 6)
                for a in range(TT):
                    for h in range(HT):
                        at, rows_at = slice(h * D, (h + 1) * D), slice(a * P, (a + 1) * P)
                        last = three(ps_o[:, a, 0:D], hid_hi[:, h, rows_at], hid_lo[:, h, rows_at],
                                     w_hi[:, k, 1, at], w_lo[:, k, 1, at], h == 0, h == HT - 1)
                last.then_inc(out_ps, 1)

            each_chunk(pe, one)

        @block.scalar
        def _(act):
            act.sem_inc(gelu_made, 4)

            def prepare(n, k):
                act.wait_ge(turned, n + 1)
                act.activation(rt_hi[:], ps_t[:, :, 0:CHUNK], ACT.Copy).then_inc(rows_hi, 1)
                arrived(act, n, k)
                for layer in range(2):
                    act.activation(w_hi[:, k, layer, :], w[:, k, layer, :], ACT.Copy).then_inc(weights_hi, 1)

            prepare(0, 0)

            def one(n, k, has_next):
                act.wait_ge(bias_loaded[k], n * 16 + (32 - 16 * k))
                for h in range(HT):
                    act.wait_ge(hidden_ps, n * HT + (h + 1))
                    if h % 2 == 0:
                        act.wait_ge(hidden_lo, n * PAIRS + (h // 2 + 1))
                    act.activation(hid[:, h, :], ps_h[:, h % 4, 0:CHUNK], ACT.Gelu, bias=b1[:, k, h:h + 1]).then_inc(gelu_made, 1)
                if has_next:
                    prepare(n + 1, 1 - k)

            each_chunk(act, one)

        @block.vector
        def _(dve):
            dve.sem_inc(out_ps, 1)
            dve.sem_inc(out_made, 2)
            dve.sem_inc(hidden_lo, PAIRS)
            dve.sem_inc(weights_lo, 4)

            def prepare(n, k):
                dve.wait_ge(rows_hi, n + 1)
                dve.tensor_tensor(rt_lo[:], ps_t[:, :, 0:CHUNK], rt_hi[:].bitcast(F32), ALU.subtract).then_inc(rows_lo, 1)
                for layer in range(2):
                    dve.wait_ge(weights_hi, n * 2 + (layer + 1))
                    dve.tensor_tensor(w_lo[:, k, layer, :], w[:, k, layer, :], w_hi[:, k, layer, :].bitcast(F32),
                                      ALU.subtract).then_inc(weights_lo, 1)

            prepare(0, 0)

            def one(n, k, has_next):
                dve.wait_ge(out_ps, n + 1)
                for q in range(PAIRS):
                    two = slice(2 * q, 2 * q + 2)
                    dve.wait_ge(gelu_made, n * HT + (2 * q + 6))
                    dve.tensor_copy(hid_hi[:, two, :], hid[:, two, :]).then_inc(hidden_hi, 1)
                    dve.wait_ge(hidden_hi, n * PAIRS + (q + 1))
                    dve.tensor_tensor(hid_lo[:, two, :], hid[:, two, :], hid_hi[:, two, :].bitcast(F32), ALU.subtract).then_inc(hidden_lo, 1)
                if has_next:
                    prepare(n + 1, 1 - k)
                dve.wait_ge(bias_loaded[k], n * 16 + (32 - 16 * k))
                dve.wait_ge(out_ps, n + 2)
                dve.wait_ge(res_free, n + 1)
                dve.tensor_tensor(res[:, k], ps_o[:, :, 0:D], b2[:, k, :].rearrange("p (a d) -> p a d", a=1).broadcast_to([P, TT, D]),
                                  ALU.add).then_inc(out_made, 1)

            each_chunk(dve, one)
            dve.wait_ge(out_made, chunks + 2)

        @block.gpsimd
        def _(pool):
            pool.sem_inc(res_free, 2)
            with pool.Fori(0, chunks // 2) as i:
                for k in range(2):
                    n = i * 2 + k
                    pool.wait_ge(out_made, n + 3)
                    pool.dma_start(results[ds(i * 2 * CHUNK + k * CHUNK, CHUNK), :].rearrange("(a p) d -> p a d", p=P),
                                   res[:, k]).then_inc(stored[k], 16)
                    pool.wait_ge(stored[k], i * 16 + 16)
                    pool.sem_inc(res_free, 1)


def mixture_gather(nc, m, s, results, gets, weights, x):
    RING = 4
    come = [s(f"row_come{k}") for k in range(RING)]
    added = s("row_added")
    with nc.sbuf_tensor(named("got"), [P, RING, D], F32) as got, nc.Block() as block:
        jobs = [(k, c) for k in range(NT) for c in range(len(gets))]

        @block.gpsimd
        def _(pool):
            for n, (k, c) in enumerate(jobs):
                if n >= RING:
                    pool.wait_ge(added, n - RING + 1)
                pool.indirect_dma_start(out=got[:, n % RING, :], out_offset=None, in_=results,
                                        in_offset=bass.IndirectOffsetOnAxis(gets[c][:, k:k + 1], 0)).then_inc(come[n % RING], 16)

        @block.vector
        def _(dve):
            for n, (k, c) in enumerate(jobs):
                dve.wait_ge(come[n % RING], 16 * (n // RING) + 16)
                if n:
                    dve.wait_ge(added, n)
                dve.scalar_tensor_tensor(x[:, k, :], got[:, n % RING, :], weights[c][:, k:k + 1], x[:, k, :],
                                         ALU.mult, ALU.add).then_inc(added, 1)
            dve.wait_ge(added, len(jobs))


def gate_logits(nc, m, s, src, w):
    def products(pe, xt, ps):
        for j in range(KT):
            last = pe.matmul(ps[:, 0, 0:EXPERTS], xt[:, j, :], w[:, j, :], start=j == 0, stop=j == KT - 1)
        return last

    def take_act(act, k, ps, took):
        act.activation(m.logits[:, k, :], ps[:, 0, 0:EXPERTS], ACT.Copy).then_inc(took, 1)

    def take_dve(dve, k, ps, act_took, took):
        dve.sem_inc(took, 1)

    transposed_products(nc, m, s, src, products, take_act, take_dve, 1)


def mixture(nc, m, t, s, layer, src, gate, bias, capacity, chunks, slots, results, x):
    n_rows = TOP_K if capacity is None else 1
    with ExitStack() as ctx:
        def sb(name, shape, dt=F32):
            return ctx.enter_context(nc.sbuf_tensor(f"mx{layer}_" + name, shape, dt))

        slot_sets = [(sb(f"put{c}", [P, NT], I32), sb(f"get{c}", [P, NT], I32)) for c in range(n_rows)]
        weights = [sb(f"weight{c}", [P, NT]) for c in range(n_rows)]
        gate_logits(nc, m, s, src, gate)
        mixture_routes(nc, m, s, bias, TOP_K, capacity, chunks, slot_sets, weights)
        mixture_scatter(nc, m, s, src, slots, [put for put, _ in slot_sets])
        expert_layers(nc, m, t, s, layer, chunks, slots, results)
        mixture_gather(nc, m, s, results, [get for _, get in slot_sets], weights, x)


def project(nc, m, t, s):
    loaded, kept, bias_added = s("qkv_loaded"), [s("qk_kept0"), s("qk_kept1")], s("bias_added")
    G = 2 * HG
    with nc.sbuf_tensor(named("wqk"), [P, 2, KT, D], F32) as wqk, nc.sbuf_tensor(named("wv"), [P, KT, D], F32) as wv, \
            nc.sbuf_tensor(named("qk_hi"), [P, 2, G, P], F32R) as hi, nc.sbuf_tensor(named("qk_lo"), [P, 2, G, P], F32R) as lo:
        with nc.Block() as block:

            @block.sync
            def _(sp):
                sp.dma_start(wqk[:, 0], t["wq"]).then_inc(loaded, 16)
                sp.dma_start(wqk[:, 1], t["wk"]).then_inc(loaded, 16)
                sp.dma_start(wv[:], t["wv"]).then_inc(loaded, 16)
                sp.wait_ge(loaded, 48)

        def products(pe, xt, ps):
            for g in range(G):
                for j in range(KT):
                    pe.matmul(ps[:, 0, g * P:(g + 1) * P], wqk[:, g // HG, j, g % HG * P:(g % HG + 1) * P], xt[:, j, :],
                              start=j == 0, stop=j == KT - 1)
            for j in range(KT):
                last = pe.matmul(ps[:, 1, 0:D], xt[:, j, :], wv[:, j, :], start=j == 0, stop=j == KT - 1)
            return last

        def take_act(act, k, ps, took):
            if k >= 2:
                act.wait_ge(kept[k % 2], k // 2 * 32)
            for g in range(G):
                last = act.activation(hi[:, k % 2, g, :], ps[:, 0, g * P:(g + 1) * P], ACT.Identity,
                                      bias=m.cols[:, 4 + g:5 + g])
            last.then_inc(took, 1)

        def take_dve(dve, k, ps, act_took, took):
            dve.tensor_tensor(m.xhat[:, k, :], ps[:, 1, 0:D], m.rows[:, 4, :], ALU.add)
            dve.wait_ge(act_took, k + 1)
            for g in range(G):
                last = dve.scalar_tensor_tensor(lo[:, k % 2, g, :], ps[:, 0, g * P:(g + 1) * P], m.cols[:, 4 + g:5 + g],
                                                hi[:, k % 2, g, :].bitcast(F32), ALU.add, ALU.subtract)
            last.then_inc(took, 1)

        def store(sp, act_took, dve_took):
            for k in range(NT):
                sp.wait_ge(act_took, k + 1)
                sp.wait_ge(dve_took, k + 1)
                for n, part in enumerate((hi, lo)):
                    sp.dma_start(m.qk[n, :, :, k * P:(k + 1) * P].rearrange("g p n -> p g n"),
                                 part[:, k % 2].bitcast(F32)).then_inc(kept[k % 2], 16)
            for k in range(2):
                sp.wait_ge(kept[k], 16 * NT)

        def add_output_bias(pool):
            pool.tensor_tensor(m.x[:], m.x[:], m.rows[:, 5:6, :].broadcast_to([P, NT, D]), ALU.add).then_inc(bias_added, 1)
            pool.wait_ge(bias_added, 1)

        transposed_products(nc, m, s, m.xhat, products, take_act, take_dve, 2,
                            affine=(m.cols[:, 0:2], m.cols[:, 2:4]), tail_sp=store, on_pool=add_output_bias)


KEYS = 512
STACK = 3 * DK
FOUR = 4
RING = 4
POOL_TILES = [k for k in range(NT - 4) if k % 4 != 2]


def up_to(tiles, k):
    return sum(x <= k for x in tiles) if k >= 0 else -sum(x > NT + k for x in tiles)


def attend(nc, m, t, s):
    KC = -(-NP // KEYS)
    QT = CHUNK // P
    N_MAX = QT * FOUR * KC
    SPREAD = 3
    MAX_TILES, ROW_TILE = NT - 3, NT - 2
    DIVIDE_AT, WO_AT = 8, 16
    ahead = [("max", c) for c in range(N_MAX)] + [("row", half) for half in range(2)]
    finish = [("out", a) for a in range(QT)]

    X_BANKS, S_BANKS = 3, 3
    NH = 2 * NT
    skipped = [("skip", a) for a in range(QT)]

    def uses(hg, b, has_next):
        last = skipped if isinstance(b, int) and b <= 0 else finish
        order = ahead[:WO_AT] + last + ahead[WO_AT:] if has_next else finish + finish + skipped
        base = (b + 1) * N_USES + hg * PER_HG
        return [(kind, c, base + n, n % X_BANKS) for n, (kind, c) in enumerate(order)]

    N_USES = len(ahead) + len(finish)
    PER_HG = N_USES * NCH + 3 * QT
    assert N_USES % X_BANKS == 0 and 3 * QT % X_BANKS == 0
    scale = float(DK) ** -0.5
    k_loaded = [s(f"k_loaded{h}") for h in range(FOUR)]
    q_loaded, wo_loaded = [s("q_loaded0"), s("q_loaded1")], s("wo_loaded")
    ones_row = s("ones_row")
    scored, exped, used = s("scored"), s("exped"), s("probs_used")
    x_made, x_free, max_made, rows_made, context = s("x_made"), s("x_free"), s("max_made"), s("rows_made"), s("context")
    pool_added, summed = s("pool_added"), s("summed")
    with ExitStack() as ctx:
        def sb(name, shape, dt=F32):
            return ctx.enter_context(nc.sbuf_tensor(named("at_" + name), shape, dt))

        def pb(name, shape):
            return ctx.enter_context(nc.psum_tensor("ps_" + name, shape, F32))

        kst, qst = sb("kst", [STACK + 1, FOUR, NP], F32R), sb("qst", [STACK + 1, 2, FOUR, CHUNK], F32R)
        probs, wo = sb("probs", [P, RING, FOUR, CHUNK]), sb("wo", [P, HG, D])
        pool_sum = sb("pool_sum", [P, 2, FOUR, CHUNK])
        part_max, maxima = sb("part_max", [P, QT * FOUR, KC]), sb("maxima", [P, QT * FOUR], BF16)
        rden, cx = sb("rden", [P, CHUNK]), sb("cx", [P, CHUNK])
        ps_s, ps_oz = pb("s", [P, S_BANKS, 2, CHUNK]), pb("oz", [P, 2, 2, CHUNK])
        ps_x = pb("x", [P, X_BANKS, 512])
        block = ctx.enter_context(nc.Block())

        def blocks(eng, one):
            for hg in range(HG):
                one(hg, -1, 1, True)
                one(hg, 0, 0, True)
                with eng.Fori(0, (NCH - 3) // 2) as i:
                    one(hg, i * 2 + 1, 1, True)
                    one(hg, i * 2 + 2, 0, True)
                one(hg, NCH - 2, 1, True)
                one(hg, NCH - 1, 0, False)

        def bank(par, j):
            return (j + par) % S_BANKS

        def slot(par, k):
            return (par * NT + k) % RING

        @block.sync
        def _(sp):
            sp.dma_start(wo[:], t["wo"]).then_inc(wo_loaded, 16)

            def load_queries(hg, b, par):
                sp.wait_ge(scored, hg * NCH * NH + 2 * NH if isinstance(b, int) else b * NH + (hg * NCH + 1) * NH)
                for r, part in enumerate((0, 1, 0)):
                    sp.dma_start(qst[r * DK:(r + 1) * DK, par, :, :].bitcast(F32),
                                 m.qk[part, hg, :, ds(b * CHUNK, CHUNK)].rearrange("(h p) n -> p h n", p=DK)).then_inc(q_loaded[par], 16)

            for hg in range(HG):
                load_queries(hg, 0, 0)
                for h in range(FOUR):
                    for r, part in enumerate((0, 0, 1)):
                        sp.dma_start(kst[r * DK:(r + 1) * DK, h, :].bitcast(F32),
                                     m.qk[part, HG + hg, h * DK:(h + 1) * DK, :]).then_inc(k_loaded[h], 16)
                with sp.Fori(0, NCH // 2) as i:
                    load_queries(hg, i * 2 + 1, 1)
                    load_queries(hg, i * 2 + 2, 0)

        @block.gpsimd
        def _(pool):
            pool.memset(kst[STACK:STACK + 1].bitcast(F32), 1.0).then_inc(ones_row, 1)
            pool.sem_inc(pool_added, RING)

            def one(hg, b, par, has_next):
                if isinstance(b, int) and b < 0:
                    return
                g = b + hg * NCH
                for n, k in enumerate(POOL_TILES[1:], 1):
                    pool.wait_ge(exped, g * NH + (2 * k + 2 + S_BANKS))
                    if n == 1:
                        pool.wait_ge(summed, g + 1)
                        pool.tensor_tensor(pool_sum[:, par], probs[:, slot(par, POOL_TILES[0])], probs[:, slot(par, k)], ALU.add)\
                            .then_inc(pool_added, 2)
                    else:
                        pool.wait_ge(pool_added, g * len(POOL_TILES) + (n + RING))
                        pool.tensor_tensor(pool_sum[:, par], pool_sum[:, par], probs[:, slot(par, k)], ALU.add).then_inc(pool_added, 1)

            blocks(pool, one)

        @block.tensor
        def _(pe):
            pe.sem_inc(scored, 2 * NH)
            pe.sem_inc(used, RING)
            pe.sem_inc(summed, 2)

            def use_x(hg, b, par, kind, c, u, turn):
                if kind == "skip":
                    pe.wait_ge(x_free, u + X_BANKS)
                    pe.sem_inc(x_made, 1)
                elif kind == "max":
                    h, qt, kc = c // (QT * KC), c // KC % QT, c % KC
                    n = min(KEYS, NP - kc * KEYS)
                    if isinstance(b, int) and b < 0 and qt == 0 and kc == 0:
                        pe.wait_ge(k_loaded[h], (hg + 1) * 48)
                    pe.wait_ge(x_free, u + 1)
                    pe.matmul(ps_x[:, turn, 0:n], qst[0:STACK, 1 - par, h, qt * P:(qt + 1) * P],
                              kst[0:STACK, h, kc * KEYS:kc * KEYS + n], start=True, stop=True).then_inc(x_made, 1)
                elif kind == "row":
                    if c == 0:
                        pe.wait_ge(max_made, b + (hg * NCH + 2))
                    pe.wait_ge(x_free, u + 1)
                    for hh in range(2):
                        for qt in range(QT):
                            col = (c * 2 + hh) * QT + qt
                            last = pe.matmul(ps_x[STACK:STACK + 1, turn, hh * CHUNK + qt * P:hh * CHUNK + (qt + 1) * P],
                                             maxima[:, col:col + 1], m.ident_b[:], start=True, stop=True)
                    last.then_inc(x_made, 1)
                else:
                    if c == 0:
                        pe.wait_ge(context, (b + hg * NCH) * 2)
                    pe.wait_ge(x_free, u + 1)
                    pe.matmul(ps_x[:, turn, 0:D], cx[:, c * P:(c + 1) * P], wo[:, hg, :], start=True, stop=True).then_inc(x_made, 1)

            def scores(hg, b, par, k, between):
                g = b + hg * NCH
                if k == 0:
                    pe.wait_ge(rows_made, g + 1)
                for j in (2 * k, 2 * k + 1):
                    sooner = 0 if par or k else (2 if j == 0 and isinstance(b, int) else 1)
                    pe.wait_ge(exped, g * NH + (j + 1 + sooner))
                    for hh in range(2):
                        h = j % 2 * 2 + hh
                        last = pe.matmul(ps_s[:, bank(par, j), hh, :], kst[:, h, k * P:(k + 1) * P], qst[:, par, h, :],
                                         start=True, stop=True)
                    last.then_inc(scored, 1)
                    if j % 2 == 0:
                        between()

            def sums(par, source, rows, stop):
                for h in range(FOUR):
                    last = pe.matmul(ps_oz[h * DK:(h + 1) * DK, par, 1, :], m.ones[0:rows, 0:DK],
                                     source[0:rows, h, :], start=False, stop=stop, skip_group_check=True)
                return last

            direct = [k for k in range(NT) if k not in POOL_TILES]

            def values(hg, b, par, k):
                g = b + hg * NCH
                pe.wait_ge(exped, g * NH + (2 * k + 2 + S_BANKS))
                rows = LAST if k == NT - 1 else P
                for h in range(FOUR):
                    lanes = slice(h * DK, (h + 1) * DK)
                    last = pe.matmul(ps_oz[lanes, par, 0, :], m.xhat[0:rows, k, (hg * FOUR + h) * DK:(hg * FOUR + h + 1) * DK],
                                     probs[0:rows, slot(par, k), h, :], start=k == 0, stop=k == NT - 1,
                                     skip_group_check=True)
                if k in direct:
                    last = sums(par, probs[:, slot(par, k)], rows, False)
                last.then_inc(used, 1)

            def one(hg, b, par, has_next):
                first = isinstance(b, int) and b < 0
                todo = uses(hg, b, has_next)
                if first and hg == 0:
                    pe.wait_ge(ones_row, 1)
                    pe.wait_ge(wo_loaded, 16)
                if has_next:
                    if first:
                        pe.wait_ge(q_loaded[0], 48 * (hg * (NCH // 2 + 1) + 1))
                    elif par == 0:
                        pe.wait_ge(q_loaded[1], b * 24 + 48 * (hg * (NCH // 2) + 1))
                    else:
                        pe.wait_ge(q_loaded[0], b * 24 + (24 + 48 * (hg * (NCH // 2 + 1) + 1)))
                if first:
                    for use in todo:
                        use_x(hg, b, par, *use)
                    return
                g = b + hg * NCH
                todo, after = (todo, []) if has_next else (todo[:QT], todo[QT:])
                tail = ahead[N_MAX:] if has_next else []
                done = [0]

                def use_up_to(n):
                    while done[0] < n:
                        use_x(hg, b, par, *todo[done[0]])
                        done[0] += 1

                for k in range(NT):
                    goal = [min(len(todo) - len(tail), (len(todo) - len(tail)) * (SPREAD * k + j + 1) // (SPREAD * MAX_TILES))
                            for j in range(SPREAD)]
                    if k >= ROW_TILE:
                        goal = [len(todo)] * SPREAD
                    scores(hg, b, par, k, lambda: use_up_to(goal[0]))
                    use_up_to(goal[1])
                    if k:
                        values(hg, b, par, k - 1)
                    use_up_to(goal[2])
                values(hg, b, par, NT - 1)
                pe.wait_ge(pool_added, g * len(POOL_TILES) + (len(POOL_TILES) + RING))
                sums(par, pool_sum[:, par], P, True).then_inc(summed, 1)
                for use in after:
                    use_x(hg, b + 1, par, *use)

            blocks(pe, one)

        @block.scalar
        def _(act):
            act.sem_inc(exped, S_BANKS)

            def one(hg, b, par, has_next):
                if isinstance(b, int) and b < 0:
                    if hg:
                        act.wait_ge(used, hg * NCH * NT + RING)
                        act.wait_ge(pool_added, hg * NCH * len(POOL_TILES) + RING)
                    return
                g = b + hg * NCH
                for j in range(NH):
                    k = j // 2
                    act.wait_ge(scored, g * NH + (j + 1 + 2 * NH))
                    if j % 2 == 0:
                        act.wait_ge(used, g * NT + (k + 1))
                        act.wait_ge(pool_added, g * len(POOL_TILES) + (up_to(POOL_TILES, k - RING) + RING))
                    act.activation(probs[:, slot(par, k), j % 2 * 2:j % 2 * 2 + 2], ps_s[:, bank(par, j)], ACT.Exp, scale=scale).then_inc(exped, 1)

            blocks(act, one)

        @block.vector
        def _(dve):
            dve.sem_inc(x_free, X_BANKS)

            def divide(hg, b, par):
                g = b + hg * NCH
                dve.wait_ge(summed, g + 3)
                dve.reciprocal(rden[:], ps_oz[:, par, 1, :]).then_inc(context, 1)
                dve.wait_ge(context, g * 2 + 1)
                dve.tensor_tensor(cx[:], ps_oz[:, par, 0, :], rden[:], ALU.mult).then_inc(context, 1)

            def read_x(hg, b, par, kind, c, u, turn):
                dve.wait_ge(x_made, u + 1)
                if kind == "skip":
                    dve.sem_inc(x_free, 1)
                elif kind == "max":
                    kc = c % KC
                    dve.tensor_reduce(part_max[:, c // KC, kc:kc + 1], ps_x[:, turn, 0:min(KEYS, TOKENS - kc * KEYS)],
                                      AX.X, ALU.max).then_inc(x_free, 1)
                    if c == N_MAX - 1:
                        dve.wait_ge(x_free, u + 1 + X_BANKS)
                        dve.tensor_reduce(maxima[:], part_max[:], AX.X, ALU.max).then_inc(max_made, 1)
                elif kind == "row":
                    dve.tensor_scalar(qst[STACK:STACK + 1, 1 - par, c * 2:c * 2 + 2, :].rearrange("p h n -> p (h n)"),
                                      ps_x[STACK:STACK + 1, turn, :], -1.0, None, ALU.mult).then_inc(x_free, 1)
                    if c == 1:
                        dve.wait_ge(x_free, u + 1 + X_BANKS)
                        dve.sem_inc(rows_made, 1)
                else:
                    xs = m.x[:, ds(b * QT + (c - QT), 1), :].rearrange("p a d -> p (a d)")
                    dve.tensor_tensor(xs, ps_x[:, turn, 0:D], xs, ALU.add).then_inc(x_free, 1)

            def one(hg, b, par, has_next):
                first = isinstance(b, int) and b < 0
                todo = uses(hg, b, has_next)
                todo, after = (todo, []) if has_next else (todo[:QT], todo[QT:])
                for n, use in enumerate(todo):
                    if n == (DIVIDE_AT if has_next else 0) and not first and not (isinstance(b, int) and b == 0):
                        divide(hg, b - 1, 1 - par)
                    read_x(hg, b, par, *use)
                if not has_next:
                    divide(hg, b, par)
                    for use in after:
                        read_x(hg, b + 1, par, *use)

            blocks(dve, one)
            dve.wait_ge(x_free, HG * PER_HG + X_BANKS)


def attention(nc, m, t, s):
    normalise(nc, m, s, m.x, m.x, keep=m.x_kept)
    normalise(nc, m, s, m.x, m.xhat)
    project(nc, m, t, s)
    attend(nc, m, t, s)


def second_mixture(nc, m, t, s):
    normalise(nc, m, s, m.x, m.xhat)
    scaled, loaded, added = s("ln2_scaled"), s("x_back"), s("back_added")
    with nc.sbuf_tensor(named("x_back"), [P, NT, D], F32) as back, nc.Block() as block:

        @block.sync
        def _(sp):
            sp.dma_start(back[:].rearrange("p t d -> p (t d)"), m.x_kept).then_inc(loaded, 16)

        @block.gpsimd
        def _(pool):
            pool.wait_ge(loaded, 16)
            pool.tensor_tensor(m.x[:], m.x[:], back[:], ALU.add).then_inc(added, 1)
            pool.wait_ge(added, 1)

        @block.vector
        def _(dve):
            dve.tensor_tensor(m.xhat[:], m.xhat[:], m.rows[:, 2:3, :].broadcast_to([P, NT, D]), ALU.mult).then_inc(scaled, 1)
            dve.wait_ge(scaled, 1)
            dve.tensor_tensor(m.xhat[:], m.xhat[:], m.rows[:, 3:4, :].broadcast_to([P, NT, D]), ALU.add).then_inc(scaled, 1)
            dve.wait_ge(scaled, 2)

    mixture(nc, m, t, s, 1, m.xhat, m.router, m.bias8[:, 1, :], CAPACITY, MOE1_CHUNKS, m.slots1, m.results1, m.x)


class Memory:

    def __init__(self, nc, ctx):
        def sb(name, shape, dt=F32):
            return ctx.enter_context(nc.sbuf_tensor("k_" + name, shape, dt))

        def dram(name, shape):
            return nc.dram_tensor(name, shape, F32).ap()

        self.x, self.xhat = sb("x", [P, NT, D]), sb("xhat", [P, NT, D])
        self.ident, self.ident_b = sb("ident", [P, P]), sb("ident_b", [P, P], BF16)
        self.ones, self.before = sb("ones", [P, P]), sb("before", [P, P])
        self.real, self.token, self.token_f = sb("real", [P, NT]), sb("token", [P, NT], I32), sb("token_f", [P, NT])
        self.iota, self.falling = sb("iota", [P, 64]), sb("falling", [P, EXPERTS])
        self.multiples = sb("multiples", [P, NCH])
        self.deg, self.dis0, self.dis1 = sb("deg", [P, NT]), sb("dis0", [P, NT]), sb("dis1", [P, NT])
        self.wg0, self.wg1 = sb("wg0", [P, KT, D]), sb("wg1", [P, KT, D])
        self.gate, self.router = sb("gate", [P, KT, EXPERTS]), sb("router", [P, KT, EXPERTS])
        self.rows, self.cols = sb("rows", [P, N_ROWS, D]), sb("cols", [P, N_COLS])
        self.bias8, self.logits = sb("bias8", [P, 2, EXPERTS]), sb("logits", [P, NT, EXPERTS])
        self.owner = sb("owner", [P, 64], I32)
        self.slots0 = dram("slots0", [MOE0_CHUNKS * CHUNK + TOP_K * NP, D])
        self.slots1 = dram("slots1", [MOE1_CHUNKS * CHUNK + NP, D])
        self.results0, self.results1 = dram("results0", [MOE0_CHUNKS * CHUNK, D]), dram("results1", [MOE1_CHUNKS * CHUNK, D])
        self.x_kept, self.qk = dram("x_kept", [P, NT * D]), dram("qk_parts", [2, 2 * HG, P, NP])


def program(nc, t, out, phases="gnn0 moe0 gnn1 att moe1"):
    NAMES.clear()
    with ExitStack() as ctx:
        used = [0]

        def stage():
            stack = ExitStack()

            def sem(name):
                used[0] += 1
                return stack.enter_context(nc.semaphore(f"{name}_{used[0]}"))

            return stack, sem

        m = Memory(nc, ctx)
        stack, s = stage()
        with stack:
            constants(nc, m, t, s)
        stack, s = stage()
        with stack:
            inverse_roots(nc, m, s)
        if "gnn0" in phases:
            stack, s = stage()
            with stack:
                normalise(nc, m, s, m.x, m.xhat)
                graph_layer(nc, m, t, s, m.wg0, m.dis0, m.rows[:, 0, :], False, m.slots0, MOE0_CHUNKS)
        if "moe0" in phases:
            stack, s = stage()
            with stack:
                normalise(nc, m, s, m.x, m.xhat)
                mixture(nc, m, t, s, 0, m.xhat, m.gate, m.bias8[:, 0, :], None, MOE0_CHUNKS, m.slots0, m.results0, m.x)
        if "gnn1" in phases:
            stack, s = stage()
            with stack:
                normalise(nc, m, s, m.x, m.xhat)
                graph_layer(nc, m, t, s, m.wg1, m.dis1, m.rows[:, 1, :], True, m.slots1, MOE1_CHUNKS)
        if "att" in phases:
            stack, s = stage()
            with stack:
                attention(nc, m, t, s)
        if "moe1" in phases:
            stack, s = stage()
            with stack:
                second_mixture(nc, m, t, s)
        stack, s = stage()
        with stack:
            put = s("out_stored")
            with nc.Block() as block:

                @block.sync
                def _(sp):
                    sp.dma_start(out, m.x[:]).then_inc(put, 16)
                    sp.wait_ge(put, 16)




def host_layout(inputs):
    g = {k: np.asarray(v) for k, v in inputs.items()}
    x = np.zeros((NP, D), np.float32)
    x[:TOKENS] = g["x"]
    adj = np.zeros((NP, NP), np.float32)
    adj[:TOKENS, :TOKENS] = g["adj"]
    a = {"x": x.reshape(NT, P, D).transpose(1, 0, 2), "adj": adj,
         "adjT": adj.reshape(NCH, CHUNK, 2, HALF, P).transpose(0, 2, 4, 3, 1).reshape(NCH, 2, P, HALF * CHUNK)}

    def by_feature(w):
        return w.reshape(KT, P, -1).transpose(1, 0, 2)

    a["W0"], a["W1"] = by_feature(g["L0_gnn_W"].T), by_feature(g["L1_gnn_W"])
    a["gate"], a["router"] = by_feature(g["L0_ffn_gate_w"]), by_feature(g["L1_ffn_router_w"])
    for n in "qkvo":
        a["w" + n] = by_feature(g[f"L1_ffn_w{n}"])
    rows = ("L0_gnn_b", "L1_gnn_b", "L1_ffn_ln2_g", "L1_ffn_ln2_b", "L1_ffn_bv", "L1_ffn_bo")
    a["rows"] = np.broadcast_to(np.stack([g[n] for n in rows]), (P, N_ROWS, D))
    a["cols"] = np.concatenate([g[n].reshape(KT, P).T for n in ("L1_ffn_ln1_g", "L1_ffn_ln1_b", "L1_ffn_bq", "L1_ffn_bk")], 1)
    a["bias8"] = np.broadcast_to(np.stack([g["L0_ffn_gate_b"], g["L1_ffn_router_b"]]), (P, 2, EXPERTS))
    for n in (0, 1):
        f = f"L{n}_ffn_"
        a[f"w1_{n}"] = g[f + "w1"].reshape(EXPERTS, KT, P, HID).transpose(0, 2, 1, 3).reshape(EXPERTS, P, KT * HID)
        a[f"w2_{n}"] = g[f + "w2"].reshape(EXPERTS, HT, P, D).transpose(0, 2, 1, 3).reshape(EXPERTS, P, HT * D)
        a[f"b1_{n}"] = g[f + "b1"].reshape(EXPERTS, HT, P).transpose(0, 2, 1)
        a[f"b2_{n}"] = np.broadcast_to(g[f + "b2"][:, None], (EXPERTS, P, D))
    return {k: np.ascontiguousarray(v) for k, v in a.items()}


def kernel(**inputs):
    import concourse.bacc as bacc
    from concourse.bass_utils import run_bass_kernel_spmd

    nc = bacc.Bacc("TRN2", target_bir_lowering=False, num_devices=1)
    arrays = host_layout(inputs)
    t = {n: nc.dram_tensor(n, a.shape, F32, kind="ExternalInput").ap() for n, a in arrays.items()}
    out = nc.dram_tensor("out", (P, NT, D), F32, kind="ExternalOutput").ap()
    program(nc, t, out)
    r = run_bass_kernel_spmd(nc, [arrays], core_ids=[0])
    return r.results[0]["out"].transpose(1, 0, 2).reshape(NP, D)[:TOKENS]
```
